# Optimizing a Trainium2 kernel written in Bass

```python
import numpy as np
import jax
import jax.numpy as jnp

def _softmax(x, axis=-1):
    return jax.nn.softmax(x, axis=axis)

def _gelu(x):
    return jax.nn.gelu(x, approximate=True)

def _silu(x):
    return jax.nn.silu(x)

def _sigmoid(x):
    return jax.nn.sigmoid(x)

def _layernorm(x, axis=-1, eps=1e-05):
    m = jnp.mean(x, axis=axis, keepdims=True)
    v = jnp.var(x, axis=axis, keepdims=True)
    return (x - m) / jnp.sqrt(v + eps)

def _scatter_add(tgt, idx, src, axis=0):
    return tgt.at[idx].add(src)

def _segment_sum(src, seg, n):
    return jax.ops.segment_sum(src, seg, n)
kernel_name = 'mk_prb_d1_jaxref_r8_0ba156'

def setup_inputs(seed: int=0):
    np.random.seed(seed)
    _w = jnp.asarray

    def _L0_attn_setup():
        import jax, jax.numpy as jnp
        import numpy as np
        B, S, D = (4, 512, 256)
        IDENTITY_WEIGHT = 0.5
        ROT_DIM = D // 2

        def _layernorm(x, gamma, beta, eps=1e-05):
            mu = jnp.mean(x, axis=-1, keepdims=True)
            var = jnp.var(x, axis=-1, keepdims=True)
            return (x - mu) * jax.lax.rsqrt(var + eps) * gamma + beta

        def _rotary(t, rot_dim, theta=10000.0):
            seq = t.shape[-2]
            inv_freq = 1.0 / theta ** (jnp.arange(0, rot_dim, 2, dtype=jnp.float32) / rot_dim)
            freqs = jnp.arange(seq, dtype=jnp.float32)[:, None] * inv_freq[None, :]
            freqs = jnp.repeat(freqs, 2, axis=-1)
            cos, sin = (jnp.cos(freqs), jnp.sin(freqs))
            t_rot, t_pass = (t[..., :rot_dim], t[..., rot_dim:])
            x1, x2 = (t_rot[..., 0::2], t_rot[..., 1::2])
            rot_half = jnp.stack([-x2, x1], axis=-1).reshape(t_rot.shape)
            return jnp.concatenate([t_rot * cos + rot_half * sin, t_pass], axis=-1)

        def _cos_sim(x):
            return x / jnp.linalg.norm(x, axis=-1, keepdims=True)
        key = jax.random.key(seed)
        ks = jax.random.split(key, 3)
        scale = 0.02
        return {'X': jax.random.normal(ks[0], (B, S, D), jnp.float32), 'W_in': jax.random.normal(ks[1], (D, 3 * D), jnp.float32) * scale, 'b_in': jnp.zeros((3 * D,), jnp.float32), 'W_out': jax.random.normal(ks[2], (D, D), jnp.float32) * scale, 'b_out': jnp.zeros((D,), jnp.float32), 'gamma': jnp.ones((D,), jnp.float32), 'beta': jnp.zeros((D,), jnp.float32)}
    _L0_attn_in = _L0_attn_setup()

    def _L0_ffn_setup():
        import jax, jax.numpy as jnp
        import numpy as np
        B, S, H = (1, 256, 256)
        E, K, I = (16, 4, 176)
        IS = 352
        CAP = 128
        key = jax.random.key(seed)
        ks = jax.random.split(key, 8)
        sc = 0.02
        return {'hidden_states': jax.random.normal(ks[0], (B, S, H), jnp.float32), 'gate_w': jax.random.normal(ks[1], (E, H), jnp.float32) * sc, 'w_gate': jax.random.normal(ks[2], (E, H, I), jnp.float32) * sc, 'w_up': jax.random.normal(ks[3], (E, H, I), jnp.float32) * sc, 'w_down': jax.random.normal(ks[4], (E, I, H), jnp.float32) * sc, 'sw_gate': jax.random.normal(ks[5], (H, IS), jnp.float32) * sc, 'sw_up': jax.random.normal(ks[6], (H, IS), jnp.float32) * sc, 'sw_down': jax.random.normal(ks[7], (IS, H), jnp.float32) * sc}
    _L0_ffn_in = _L0_ffn_setup()
    _d = {'L0_attn_X': _L0_attn_in['X'], 'L0_attn_W_in': _L0_attn_in['W_in'], 'L0_attn_b_in': _L0_attn_in['b_in'], 'L0_attn_W_out': _L0_attn_in['W_out'], 'L0_attn_b_out': _L0_attn_in['b_out'], 'L0_attn_gamma': _L0_attn_in['gamma'], 'L0_attn_beta': _L0_attn_in['beta'], 'L0_ffn_gate_w': _L0_ffn_in['gate_w'], 'L0_ffn_w_gate': _L0_ffn_in['w_gate'], 'L0_ffn_w_up': _L0_ffn_in['w_up'], 'L0_ffn_w_down': _L0_ffn_in['w_down'], 'L0_ffn_sw_gate': _L0_ffn_in['sw_gate'], 'L0_ffn_sw_up': _L0_ffn_in['sw_up'], 'L0_ffn_sw_down': _L0_ffn_in['sw_down']}
    _x0 = _d['L0_attn_X']
    _d['L0_attn_X'] = jax.random.normal(jax.random.fold_in(jax.random.key(seed), 1), (2, 1024, 256), dtype=_x0.dtype)
    del _x0
    return _d

def reference(L0_attn_X, L0_attn_W_in, L0_attn_b_in, L0_attn_W_out, L0_attn_b_out, L0_attn_gamma, L0_attn_beta, L0_ffn_gate_w, L0_ffn_w_gate, L0_ffn_w_up, L0_ffn_w_down, L0_ffn_sw_gate, L0_ffn_sw_up, L0_ffn_sw_down):

    def _L0_attn_ref(X, W_in, b_in, W_out, b_out, gamma, beta):
        import jax, jax.numpy as jnp
        import numpy as np
        B, S, D = (4, 512, 256)
        IDENTITY_WEIGHT = 0.5
        ROT_DIM = D // 2

        def _layernorm(x, gamma, beta, eps=1e-05):
            mu = jnp.mean(x, axis=-1, keepdims=True)
            var = jnp.var(x, axis=-1, keepdims=True)
            return (x - mu) * jax.lax.rsqrt(var + eps) * gamma + beta

        def _rotary(t, rot_dim, theta=10000.0):
            seq = t.shape[-2]
            inv_freq = 1.0 / theta ** (jnp.arange(0, rot_dim, 2, dtype=jnp.float32) / rot_dim)
            freqs = jnp.arange(seq, dtype=jnp.float32)[:, None] * inv_freq[None, :]
            freqs = jnp.repeat(freqs, 2, axis=-1)
            cos, sin = (jnp.cos(freqs), jnp.sin(freqs))
            t_rot, t_pass = (t[..., :rot_dim], t[..., rot_dim:])
            x1, x2 = (t_rot[..., 0::2], t_rot[..., 1::2])
            rot_half = jnp.stack([-x2, x1], axis=-1).reshape(t_rot.shape)
            return jnp.concatenate([t_rot * cos + rot_half * sin, t_pass], axis=-1)

        def _cos_sim(x):
            return x / jnp.linalg.norm(x, axis=-1, keepdims=True)
        Xn = _layernorm(X, gamma, beta)
        QKV = Xn @ W_in + b_in
        Q, K, V = jnp.split(QKV, 3, axis=-1)
        K = _rotary(K, ROT_DIM)
        V = _rotary(V, ROT_DIM)
        A = jnp.sum(_cos_sim(K) * _cos_sim(V), axis=-2)
        A = (1.0 - IDENTITY_WEIGHT) * A + IDENTITY_WEIGHT
        Y = A[:, None, :] * Q
        Y = Y @ W_out + b_out
        return Y + X

    def _L0_ffn_ref(hidden_states, gate_w, w_gate, w_up, w_down, sw_gate, sw_up, sw_down):
        import jax, jax.numpy as jnp
        import numpy as np
        B, S, H = (1, 256, 256)
        E, K, I = (16, 4, 176)
        IS = 352
        CAP = 128
        b, s, h = hidden_states.shape
        x = hidden_states.reshape(-1, h)
        T = x.shape[0]
        scores = jax.nn.softmax(x @ gate_w.T, axis=-1)
        topk_w, topk_i = jax.lax.top_k(scores, K)
        topk_w = topk_w / (topk_w.sum(-1, keepdims=True) + 1e-20)
        flat_i = topk_i.reshape(-1)
        flat_w = topk_w.reshape(-1)
        order = jnp.argsort(flat_i)
        se = flat_i[order]
        counts = jax.ops.segment_sum(jnp.ones_like(flat_i), flat_i, num_segments=E)
        starts = jnp.cumsum(counts) - counts
        rank = jnp.arange(T * K) - starts[se]
        tok = order // K
        slot = jnp.where(rank < CAP, rank, CAP)
        buf = jnp.full((E, CAP + 1), T, dtype=jnp.int32).at[se, slot].set(tok)[:, :CAP]
        wbuf = jnp.zeros((E, CAP + 1), x.dtype).at[se, slot].set(flat_w[order])[:, :CAP]
        xpad = jnp.concatenate([x, jnp.zeros((1, h), x.dtype)], axis=0)
        xg = xpad[buf]
        gact = jax.nn.silu(jnp.einsum('ech,ehi->eci', xg, w_gate))
        mid = gact * jnp.einsum('ech,ehi->eci', xg, w_up)
        eout = jnp.einsum('eci,eih->ech', mid, w_down) * wbuf[..., None]
        y = jnp.zeros((T + 1, h), x.dtype).at[buf.reshape(-1)].add(eout.reshape(-1, h))[:T]
        shared = jax.nn.silu(x @ sw_gate) * (x @ sw_up) @ sw_down
        return (y + shared).reshape(b, s, h)
    x = L0_attn_X
    xn = _layernorm(x, axis=-1)
    x = x + _L0_attn_ref(xn, L0_attn_W_in, L0_attn_b_in, L0_attn_W_out, L0_attn_b_out, L0_attn_gamma, L0_attn_beta) + _L0_ffn_ref(xn, L0_ffn_gate_w, L0_ffn_w_gate, L0_ffn_w_up, L0_ffn_w_down, L0_ffn_sw_gate, L0_ffn_sw_up, L0_ffn_sw_down)
    return x

_drawn_inputs = setup_inputs


def setup_inputs(seed=0):
    import zlib

    import numpy as np

    out = dict(_drawn_inputs(seed))
    spreads = {'L0_attn_b_in': (0.0, 0.623),
     'L0_attn_b_out': (0.0, 0.518),
     'L0_attn_gamma': (1.0, 0.6),
     'L0_attn_beta': (0.0, 2.0)}
    factors = {'L0_ffn_gate_w': 8.0,
     'L0_ffn_w_gate': 8.0,
     'L0_ffn_w_up': 8.0,
     'L0_ffn_w_down': 8.0,
     'L0_ffn_sw_gate': 5.763,
     'L0_ffn_sw_up': 5.702,
     'L0_ffn_sw_down': 5.69}
    for name, (base, spread) in spreads.items():
        noise = np.random.default_rng([zlib.crc32(name.encode()), seed]).standard_normal(out[name].shape)
        drawn = base * np.exp(spread * noise) if base else spread * noise
        out[name] = jnp.asarray(drawn.astype(out[name].dtype))
    for name, factor in factors.items():
        out[name] = (out[name] * factor).astype(out[name].dtype)
    return out
```

```python
from contextlib import ExitStack

import concourse.bass as bass
from concourse import mybir

P = 128
TOKENS, D, BATCH = 2048, 256, 2
TILES = TOKENS // P
G = 4
GROUPS = TILES // G
GROUPS_B = GROUPS // BATCH
TILES_B = TILES // BATCH
DC = D // P
ROT = D // 2
HALF = ROT // 2
E, TOP, CAP = 16, 4, 128
I = 176
I2 = I - P
UP2 = 64
GU = 2 * P + UP2 + I2
IS = 352
SC = [P, P, IS - 2 * P]
ROW = D + E
SLOT_A, SLOT_B = 8, 16
EPS = 1e-5

F32 = mybir.dt.float32
F32R = mybir.dt.float32r
F16 = mybir.dt.float16
I32 = mybir.dt.int32
U32 = mybir.dt.uint32
ALU = mybir.AluOpType
ACT = mybir.ActivationFunctionType
AX = mybir.AxisListType

C_ID = 0
C_TRI = C_ID + P
C_EXP = C_TRI + P
C_ASEL = C_EXP + E
C_I16 = C_ASEL + SLOT_A
C_TOK = C_I16 + E
C_SPARE = C_TOK + TILES
C_ROW = C_SPARE + 1
C_ALL = C_ROW + 2


def layer(nc, x, w_in, b_in, wq_t, w_out, b_out, gamma, beta, gate_t, w_gu, w_dn, sw_g, sw_u, sw_d,
          trig, consts, out):
    ctx = ExitStack()
    with ctx:
        def sb(name, shape, dt=F32):
            return ctx.enter_context(nc.sbuf_tensor(name, shape, dt))

        def sem(name):
            return ctx.enter_context(nc.semaphore(name))

        def sems(name, n):
            return [sem(f"{name}{i}") for i in range(n)]

        rows = nc.dram_tensor("rows", (TOKENS + CAP, ROW), F32, kind="Internal").ap()
        ysum = nc.dram_tensor("ysum", (TOKENS + CAP, D), F32, kind="Internal").ap()

        cst = sb("cst", [P, C_ALL])
        x_all = sb("x_all", [P, TILES, D])
        wi = sb("wi", [P, DC, 3 * D])
        wqt = sb("wqt", [P, DC, D])
        wo = sb("wo", [P, DC, D])
        x_flat = x_all[:, :, :].rearrange("p t d -> p (t d)")
        swg = x_flat[:, 0:DC * IS].rearrange("p (c n) -> p c n", c=DC)
        swu = x_flat[:, DC * IS:2 * DC * IS].rearrange("p (c n) -> p c n", c=DC)
        swd = x_flat[:, 2 * DC * IS:2 * DC * IS + 3 * D].rearrange("p (c n) -> p c n", c=3)
        gt = sb("gt", [P, DC, E])
        bin_row, bout_row = sb("bin_row", [1, 3 * D]), sb("bout_row", [1, D])
        gam, bet = sb("gam", [P, DC]), sb("bet", [P, DC])
        trg = sb("trg", [P, TILES_B, D])
        ones3 = sb("ones3", [1, 4])
        bet3 = sb("bet3", [P, DC, 3])
        wkv_s = sb("wkv_s", [P, DC, 2, 2 * D], F32R)
        gt_s = sb("gt_s", [P, DC, 2, E], F32R)
        swg_s, swu_s = sb("swg_s", [P, DC, 2, IS], F32R), sb("swu_s", [P, DC, 2, IS], F32R)
        swd_s = sb("swd_s", [P, 3, 2, D], F32R)
        b3f, b3h, b3l = sb("b3f", [3, 2 * D]), sb("b3h", [3, 2 * D], F32R), sb("b3l", [3, 2 * D])
        b3 = sb("b3", [3, 2 * D], F32R)
        st6 = sb("st6", [P, 6])
        mv = sb("mv", [P, G, 2])
        rstd, s2 = sb("rstd", [P, TILES]), sb("s2", [P, TILES])
        lt = sb("lt", [P, 4, G])
        mhalf, phalf = sb("mhalf", [P, G]), sb("phalf", [P, G])
        ihi = sb("ihi", [P, G], F32R)
        i3 = sb("i3", [P, G, 3])
        xn = sb("xn", [P, G, D])
        res = sb("res", [P, G, D])
        hl = sb("hl", [P, G, 2, DC, P], F32R)
        xt_all = sb("xt_all", [P, TILES, 2, DC, P], F32R)
        ib, ib_all = sb("ib", [3, G, P], F32R), sb("ib_all", [3, TILES, P], F32R)
        kv = sb("kv", [P, 2, 2 * D])
        junk = sb("junk", [P, 2, D])
        junk2 = junk
        nrm = sb("nrm", [P, G, 2])
        wtok, wprod = sb("wtok", [P, G]), sb("wprod", [P, G])
        ph = sb("ph", [P, G, D + ROT])
        rot = sb("rot", [P, 2, ROT])
        asum = sb("asum", [1, GROUPS, D + ROT])
        ab = sb("ab", [1, BATCH, D + ROT])
        aq, af, arow = sb("aq", [1, BATCH, HALF]), sb("af", [1, BATCH, HALF]), sb("arow", [1, BATCH, D])
        acol = sb("acol", [P, BATCH * DC])
        aw = sb("aw", [P, BATCH, DC, D])
        bq3 = sb("bq3", [P, DC, 3])
        m_s = wkv_s[:, :, :, :].rearrange("p b h (c n) -> p b c h n", n=D)
        c3f, c3h, c3l, c3 = (r[:, :].rearrange("k (b n) -> k b n", b=BATCH) for r in (b3f, b3h, b3l, b3))
        lg = sb("lg", [P, TILES, E])
        sc = sb("sc", [P, G, E])
        mx, ix = sb("mx", [P, G, 8]), sb("ix", [P, G, 8], U32)
        top1, ixf = sb("top1", [P, TILES]), sb("ixf", [P, TILES, TOP])
        eq = sb("eq", [P, TILES, TOP, E], F16)
        mask, ex, em = sb("mask", [P, TILES, E]), sb("ex", [P, TILES, E]), sb("em", [P, TILES, E])
        mask16 = sb("mask16", [P, TILES, E], F16)
        tri16, one16, exp16 = sb("tri16", [P, P], F16), sb("one16", [P, P], F16), sb("exp16", [P, E], F16)
        zsum, esum, einv = sb("zsum", [P, TILES]), sb("esum", [P, TILES]), sb("einv", [P, TILES])
        wd = sb("wd", [P, TILES, E])
        rank = sb("rank", [P, TILES, E])
        rank_i = sb("rank_i", [P, TILES, E], I32)
        ra_i, rb_i = sb("ra_i", [P, TILES, E], I32), sb("rb_i", [P, TILES, E], I32)
        ra, rb = sb("ra", [P, TILES, E], F16), sb("rb", [P, TILES, E], F16)
        iota16 = sb("iota16", [P, E], F16)
        tok16 = sb("tok16", [P, TILES], F16)
        onehots = x_all[:, :, :].rearrange("p t d -> p (t d)").bitcast(F16)
        n_a, n_b = TILES * E * SLOT_A, TILES * E * SLOT_B
        oa = onehots[:, 0:n_a].rearrange("p (t e a) -> p t e a", t=TILES, e=E)
        oat = onehots[:, n_a:2 * n_a].rearrange("p (t e a) -> p t e a", t=TILES, e=E)
        ob = onehots[:, 2 * n_a:2 * n_a + n_b].rearrange("p (t e b) -> p t e b", t=TILES, e=E)
        diag, tb = sb("diag", [P, E, SLOT_B]), sb("tb", [P, SLOT_B])
        spread = sb("spread", [P, SLOT_A, SLOT_B], F16)
        slot_v, slot_e, slot_f = sb("slot_v", [P, E]), sb("slot_e", [P, E]), sb("slot_f", [P, E])
        idx = sb("idx", [P, E], I32)
        zero = sb("zero", [P, ROW])
        wgu = sb("wgu", [P, G, DC, GU])
        wdn = trg[:, :, :].rearrange("p (j c) n -> p j c n", c=2)
        idx_g, idx_s = sb("idx_g", [P, G], I32), sb("idx_s", [P, G], I32)
        xg = sb("xg", [P, G, ROW])
        ph_flat = ph[:, :, :].rearrange("p j n -> p (j n)")
        xgt = ph_flat[:, 0:2 * DC * P].rearrange("p (k c n) -> p k c n", k=2, c=DC)
        sil = ph_flat[:, 2 * DC * P:4 * DC * P].rearrange("p (k c n) -> p k c n", k=2, c=2)
        mid = junk2[:, :, :].rearrange("p k (c n) -> p k c n", c=2)
        eo = kv[:, :, :].rearrange("p k (j n) -> p (k j) n", n=D)
        xs, ibs = hl, ib
        yin = x_flat[:, 0:G * D].rearrange("p (j n) -> p j n", j=G)
        sg = x_flat[:, G * D:2 * G * D].rearrange("p (k n) -> p k n", k=2)
        smid = x_flat[:, 2 * G * D:3 * G * D].rearrange("p (k n) -> p k n", k=2)
        ot = x_flat[:, 3 * G * D:4 * G * D].rearrange("p (j n) -> p j n", j=G)
        smid_s = sb("smid_s", [P, 3, 2, G * P], F32R)

        bank = [ctx.enter_context(nc.psum_tensor(f"bank{i}", [P, 512], F32)) for i in range(8)]

        def f(ap):
            return ap.bitcast(F32)

        x_in = sems("x_in", GROUPS)
        x_ready = sem("x_ready")
        pool_passed, dve_passed = sem("pool_passed"), sem("dve_passed")
        cst_in, wi_in, gt_in, trg_in, mix_in, sw_in = (sem(n) for n in ("cst_in", "wi_in", "gt_in", "trg_in", "mix_in", "sw_in"))
        ew_in = sems("ew_in", G)
        ones_set, prep_chain, prep_done, act_prep = sem("ones_set"), sem("prep_chain"), sem("prep_done"), sem("act_prep")
        pool_prep, pool_chain, pe_prep = sem("pool_prep"), sem("pool_chain"), sem("pe_prep")
        st_chain, stats_done, ln_ready, i3_ready, norm_done = (sem(n) for n in ("st_chain", "stats_done", "ln_ready", "i3_ready", "norm_done"))
        xn_saved, res_saved, xt_saved = sems("xn_saved", G), sems("res_saved", G), sems("xt_saved", G)
        ib_saved = sem("ib_saved")
        res_done, t_done, hi_done, lo_done = sem("res_done"), sem("t_done"), sem("hi_done"), sem("lo_done")
        ibt_done, ib_done, kv_done, router_done = sem("ibt_done"), sem("ib_done"), sem("kv_done"), sem("router_done")
        v_done, sq_done, prod_done, rot_done, tab_done = sem("v_done"), sem("sq_done"), sem("prod_done"), sem("rot_done"), sem("tab_done")
        w_ready, red_done, a_read, rt_read = sem("w_ready"), sem("red_done"), sem("a_read"), sem("rt_read")
        sc_read = sem("sc_read")
        mx_done = sem("mx_done")
        a_chain, arow_done, acol_done, acol_read, aw_done = (sem(n) for n in ("a_chain", "arow_done", "acol_done", "acol_read", "aw_done"))
        m_done, m_hi, m_lo, c_done, c3_done, mix_pe = (sem(n) for n in ("m_done", "m_hi", "m_lo", "c_done", "c3_done", "mix_pe"))
        r_chain, lm_done, exp_done, wd_done, wd_saved = (sem(n) for n in ("r_chain", "lm_done", "exp_done", "wd_done", "wd_saved"))
        mask_done, rank_done, onehot_done, oa_done, table_done, spread_done, slot_done, idx_done = (
            sem(n) for n in ("mask_done", "rank_done", "onehot_done", "oa_done", "table_done", "spread_done", "slot_done", "idx_done"))
        zero_set, pads_saved = sem("zero_set"), sem("pads_saved")
        rows_ready = sem("rows_ready")
        idx_copied = sem("idx_copied")
        gath, scat_done = sems("gath", G), sem("scat_done")
        xt_e, xgt_done, gu_done, silu_done, mid_done, d_done, eo_done = (
            sem(n) for n in ("xt_e", "xgt_done", "gu_done", "silu_done", "mid_done", "d_done", "eo_done"))
        stage_in, y_in, out_sent = sem("stage_in"), sem("y_in"), sems("out_sent", G)
        sh_done, sg_done, sm_done, hi_m, lo_m, att_done, dn_done, acc_done, ot_done = (
            sem(n) for n in ("sh_done", "sg_done", "sm_done", "hi_m", "lo_m", "att_done", "dn_done", "acc_done", "ot_done"))

        x_v = x.rearrange("b (t p) d -> p (b t) d", p=P)
        out_v = out.rearrange("b (t p) d -> p (b t) d", p=P)
        rows_v = rows.rearrange("(t p) d -> p t d", p=P)
        ysum_v = ysum.rearrange("(t p) d -> p t d", p=P)

        block = ctx.enter_context(nc.Block())

        def mm3(dst, lt_hi, lt_lo, r_hi, r_lo, start, stop):
            nc.tensor.matmul(dst, lt_hi, r_hi, start=start, stop=False)
            nc.tensor.matmul(dst, lt_hi, r_lo, start=False, stop=False)
            return nc.tensor.matmul(dst, lt_lo, r_hi, start=False, stop=stop)

        @block.sync
        def _(sp):
            def load_expert(e, j):
                sp.dma_start(wgu[:, j, :, :], w_gu[e, :, :].rearrange("(c p) n -> p c n", p=P)).then_inc(ew_in[j], 16)
                sp.dma_start(wdn[:, j, 0, :], w_dn[e, 0:P, :]).then_inc(ew_in[j], 16)
                sp.dma_start(wdn[0:I2, j, 1, :], w_dn[e, P:I, :]).then_inc(ew_in[j], 16)

            for g in range(GROUPS):
                sp.dma_start(x_all[:, g * G:(g + 1) * G, :], x_v[:, g * G:(g + 1) * G, :]).then_inc(x_in[g], 16)
            sp.dma_start(trg[:, :, :], trig.rearrange("(t p) c -> p t c", p=P)).then_inc(trg_in, 16)
            for g in range(GROUPS):
                sp.wait_ge(x_in[g], 16)
                sp.sem_inc(x_ready, 1)
            sp.wait_ge(zero_set, 1)
            sp.dma_start(rows[TOKENS:TOKENS + CAP, :], zero[:, :]).then_inc(pads_saved, 16)
            sp.dma_start(ysum[TOKENS:TOKENS + CAP, :], zero[:, 0:D]).then_inc(pads_saved, 16)

            def group_stores(g):
                for j in range(G):
                    t = g * G + j
                    sp.wait_ge(norm_done, t + 1)
                    sp.dma_start(rows_v[:, bass.ds(t, 1), 0:D], xn[:, j:j + 1, :]).then_inc(xn_saved[j], 16)
                    sp.wait_ge(res_done, t + 1)
                    sp.dma_start(ysum_v[:, bass.ds(t, 1), :], res[:, j:j + 1, :]).then_inc(res_saved[j], 16)
                sp.wait_ge(ib_done, g + 1)
                sp.dma_start(f(ib_all[:, bass.ds(g * G, G), :]), f(ib[:, :, :])).then_inc(ib_saved, 16)
                for j in range(G):
                    t = g * G + j
                    sp.wait_ge(lo_done, t + 1)
                    sp.dma_start(f(xt_all[:, bass.ds(t, 1), :, :, :]).rearrange("p a h c n -> p (a h c n)"),
                                 f(hl[:, j, :, :, :]).rearrange("p h c n -> p (h c n)")).then_inc(xt_saved[j], 16)

            with sp.Fori(0, GROUPS) as g:
                group_stores(g)
            sp.wait_ge(tab_done, TILES)
            for j in range(G):
                load_expert(j, j)
            sp.wait_ge(wd_done, 1)
            sp.dma_start(rows_v[:, 0:TILES, D:ROW], wd[:, :, :]).then_inc(wd_saved, 16)
            for j in range(G):
                sp.wait_ge(xn_saved[j], 16 * GROUPS)
                sp.wait_ge(res_saved[j], 16 * GROUPS)
            sp.wait_ge(pads_saved, 32)
            sp.wait_ge(wd_saved, 16)
            sp.sem_inc(rows_ready, 1)
            sp.wait_ge(table_done, 1)
            sp.dma_start(swg[:, :, :], sw_g.rearrange("(c p) n -> p c n", p=P)).then_inc(sw_in, 16)
            sp.dma_start(swu[:, :, :], sw_u.rearrange("(c p) n -> p c n", p=P)).then_inc(sw_in, 16)
            sp.dma_start(swd[:, 0:2, :], sw_d[0:2 * P, :].rearrange("(c p) n -> p c n", p=P)).then_inc(sw_in, 16)
            sp.dma_start(swd[0:SC[2], 2, :], sw_d[2 * P:IS, :]).then_inc(sw_in, 16)
            with sp.Fori(0, E // G - 1) as h:
                for j in range(G):
                    sp.wait_ge(gu_done, h * G + j + 1)
                    sp.wait_ge(d_done, h * G + j + 1)
                    load_expert(h * G + G + j, j)

            sp.wait_ge(prep_done, 8)
            sp.wait_ge(scat_done, 16 * E)
            for j in range(G):
                sp.wait_ge(xt_saved[j], 16 * GROUPS)
            sp.wait_ge(ib_saved, 16 * GROUPS)

            def stage(g):
                sp.dma_start(f(xs[:, :, :, :, :]).rearrange("p t h c n -> p (t h c n)"),
                             f(xt_all[:, bass.ds(g * G, G), :, :, :]).rearrange("p t h c n -> p (t h c n)")).then_inc(stage_in, 16)
                sp.dma_start(f(ibs[:, :, :]), f(ib_all[:, bass.ds(g * G, G), :])).then_inc(stage_in, 16)
                sp.dma_start(yin[:, :, :], ysum_v[:, bass.ds(g * G, G), :]).then_inc(y_in, 16)

            def send(g):
                for j in range(G):
                    sp.wait_ge(ot_done, g * G + j + 1)
                    sp.dma_start(out_v[:, bass.ds(g * G + j, 1), :], ot[:, j:j + 1, :]).then_inc(out_sent[j], 16)

            stage(0)
            with sp.Fori(1, GROUPS) as g:
                sp.wait_ge(att_done, g * G)
                sp.wait_ge(acc_done, g * G)
                stage(g)
                send(g - 1)
            send(GROUPS - 1)
            for j in range(G):
                sp.wait_ge(out_sent[j], 16 * GROUPS)

        @block.gpsimd
        def _(pool):
            pool.memset(mhalf[:, :], -0.5).then_inc(pool_prep, 1)
            pool.memset(phalf[:, :], 0.5).then_inc(pool_prep, 1)
            pool.memset(zero[:, :], 0.0).then_inc(zero_set, 1)
            pool.wait_ge(pool_prep, 2)

            def await_ge(signal, count):
                pool.wait_ge(signal, count)
                if not isinstance(count, int):
                    pool.sem_inc(pool_passed, 1)

            def ln(g):
                c = g * 7
                gs = bass.ds(g * G, G)
                await_ge(stats_done, g * G + G)
                nc.gpsimd.tensor_scalar(lt[:, 0, :], mv[:, :, 1], EPS, None, ALU.add).then_inc(pool_chain, 1)
                await_ge(pool_chain, c + 1)
                nc.gpsimd.tensor_tensor(rstd[:, gs], lt[:, 0, :], mhalf[:, :], ALU.pow).then_inc(ln_ready, 1)
                await_ge(ln_ready, g + 1)
                nc.gpsimd.tensor_tensor(lt[:, 1, :], rstd[:, gs], rstd[:, gs], ALU.mult).then_inc(pool_chain, 1)
                await_ge(pool_chain, c + 2)
                nc.gpsimd.tensor_tensor(lt[:, 2, :], lt[:, 1, :], mv[:, :, 1], ALU.mult).then_inc(pool_chain, 1)
                await_ge(pool_chain, c + 3)
                nc.gpsimd.tensor_scalar(lt[:, 3, :], lt[:, 2, :], EPS, None, ALU.add).then_inc(pool_chain, 1)
                await_ge(pool_chain, c + 4)
                nc.gpsimd.tensor_tensor(s2[:, gs], lt[:, 3, :], mhalf[:, :], ALU.pow).then_inc(pool_chain, 1)
                nc.gpsimd.tensor_tensor(lt[:, 0, :], lt[:, 3, :], phalf[:, :], ALU.pow).then_inc(pool_chain, 1)
                await_ge(pool_chain, c + 6)
                nc.gpsimd.tensor_copy(ihi[:, :], lt[:, 0, :]).then_inc(pool_chain, 1)
                await_ge(pool_chain, c + 7)
                if not isinstance(g, int) or g > 0:
                    await_ge(ibt_done, g)
                nc.gpsimd.tensor_copy(i3[:, :, 0], f(ihi[:, :])).then_inc(i3_ready, 1)
                nc.gpsimd.tensor_copy(i3[:, :, 1], f(ihi[:, :])).then_inc(i3_ready, 1)
                nc.gpsimd.tensor_tensor(i3[:, :, 2], lt[:, 0, :], f(ihi[:, :]), ALU.subtract).then_inc(i3_ready, 1)

            def residual(g, j, first):
                t = g * G + j
                if not first:
                    await_ge(res_saved[j], g * 16)
                await_ge(norm_done, t + 1)
                nc.gpsimd.tensor_tensor(res[:, j, :], x_all[:, t, :], xn[:, j, :], ALU.add).then_inc(res_done, 1)

            def rotate(g, j, half):
                t = g * G + j
                if not (isinstance(g, int) and g == 0 and j == 0):
                    await_ge(tab_done, t)
                await_ge(prod_done, 2 * t + 2)
                pxy = ph[:, j, :].rearrange("p (a n) -> p a n", n=ROT)[:, 0:3:2, :]
                nc.gpsimd.tensor_tensor(rot[:, :, :], pxy, trg[:, bass.ds(half * G + j, 1), :].rearrange("p o (a n) -> p (o a) n", a=2),
                                        ALU.mult).then_inc(rot_done, 1)
                await_ge(rot_done, t + 1)
                nc.gpsimd.tensor_tensor(ph[:, j, D:D + ROT], rot[:, 0, :], rot[:, 1, :], ALU.add).then_inc(tab_done, 1)

            def weights(g, first):
                await_ge(sq_done, 2 * (g * G + G))
                nc.gpsimd.tensor_tensor(wprod[:, :], nrm[:, :, 0], nrm[:, :, 1], ALU.mult).then_inc(w_ready, 1)
                await_ge(w_ready, 2 * g + 1)
                if not first:
                    await_ge(red_done, g)
                nc.gpsimd.tensor_tensor(wtok[:, :], wprod[:, :], mhalf[:, :], ALU.pow).then_inc(w_ready, 1)

            def body(g, first=False, last=False):
                half = g % GROUPS_B if isinstance(g, int) else g & (GROUPS_B - 1)
                for j in range(G):
                    residual(g, j, first)
                rotate(g, 0, half)
                rotate(g, 1, half)
                if not last:
                    ln(g + 1)
                rotate(g, 2, half)
                rotate(g, 3, half)
                weights(g, first)

            ln(0)
            await_ge(trg_in, 16)
            body(0, first=True)
            with pool.Fori(1, GROUPS - 1) as g:
                body(g)
            body(GROUPS - 1, last=True)

            await_ge(onehot_done, 1)
            nc.gpsimd.tensor_tensor(oat[:, :, :, :].rearrange("p t e a -> p t (e a)"), oa[:, :, :, :].rearrange("p t e a -> p t (e a)"),
                                    tok16[:, :].unsqueeze(2).to_broadcast([P, TILES, E * SLOT_A]),
                                    ALU.mult).then_inc(oa_done, 1)

            def gather(e, j, first):
                k = 2 * e if first else 2 * e - G
                nc.gpsimd.tensor_copy(idx_g[:, j:j + 1], idx[:, bass.ds(e, 1)]).then_inc(idx_copied, 1)
                await_ge(idx_copied, e + 1 if first else 2 * e - G + 2)
                nc.gpsimd.indirect_dma_start(out=xg[:, j, :], out_offset=None, in_=rows,
                                             in_offset=bass.IndirectOffsetOnAxis(ap=idx_g[:, j:j + 1], axis=0)).then_inc(gath[j], 16)

            def scatter(e, j, last):
                await_ge(eo_done, e + 1)
                if not (isinstance(e, int) and e == 0):
                    await_ge(scat_done, 16 * e)
                nc.gpsimd.tensor_copy(idx_s[:, j:j + 1], idx[:, bass.ds(e, 1)]).then_inc(idx_copied, 1)
                await_ge(idx_copied, (E + 1 + e) if last else (2 * e + G + 1))
                nc.gpsimd.indirect_dma_start(out=ysum, out_offset=bass.IndirectOffsetOnAxis(ap=idx_s[:, j:j + 1], axis=0),
                                             in_=eo[:, j, :], in_offset=None, compute_op=ALU.add).then_inc(scat_done, 16)

            await_ge(idx_done, 1)
            await_ge(rows_ready, 1)
            for j in range(G):
                gather(j, j, True)

            def moe_body(h, last=False):
                for j in range(G):
                    scatter(h * G + j, j, last)
                    if not last:
                        gather(h * G + G + j, j, False)

            moe_body(0)
            with pool.Fori(1, E // G - 1) as h:
                moe_body(h)
            moe_body(E // G - 1, last=True)

        @block.scalar
        def _(act):
            act.dma_start(cst[:, :], consts).then_inc(cst_in, 16)
            act.dma_start(wi[:, :, :], w_in.rearrange("(c p) n -> p c n", p=P)).then_inc(wi_in, 16)
            act.dma_start(gam[:, :], gamma.rearrange("p c -> p c")).then_inc(wi_in, 16)
            act.dma_start(bet[:, :], beta.rearrange("p c -> p c")).then_inc(wi_in, 16)
            act.dma_start(bin_row[:, :], b_in.rearrange("(o n) -> o n", o=1)).then_inc(wi_in, 16)
            act.dma_start(gt[:, :, :], gate_t.rearrange("(c p) n -> p c n", p=P)).then_inc(gt_in, 16)
            act.dma_start(wqt[:, :, :], wq_t.rearrange("(c p) n -> p c n", p=P)).then_inc(mix_in, 16)
            act.dma_start(wo[:, :, :], w_out.rearrange("(c p) n -> p c n", p=P)).then_inc(mix_in, 16)
            act.dma_start(bout_row[:, :], b_out.rearrange("(o n) -> o n", o=1)).then_inc(mix_in, 16)
            act.wait_ge(wi_in, 64)
            for c in range(DC):
                nc.scalar.activation(wkv_s[:, c, 0, :], wi[:, c, D:3 * D], ACT.Copy, scale=gam[:, c:c + 1]).then_inc(act_prep, 1)
            act.wait_ge(gt_in, 16)
            nc.scalar.activation(gt_s[:, :, 0, :], gt[:, :, :], ACT.Copy).then_inc(act_prep, 1)
            act.wait_ge(pe_prep, 1)
            nc.scalar.activation(b3f[:, :], bank[3][0:3, :], ACT.Copy).then_inc(act_prep, 1)
            act.wait_ge(act_prep, 4)
            nc.scalar.activation(b3h[:, :], b3f[:, :], ACT.Copy).then_inc(act_prep, 1)

            def hi(g, j, first):
                t = g * G + j
                if not first:
                    act.wait_ge(kv_done, t - G + 1)
                    act.wait_ge(xt_saved[j], g * 16)
                act.wait_ge(t_done, t + 1)
                nc.scalar.activation(hl[:, j, 0, :, :], bank[4 + j % 2][:, 0:D].rearrange("p (c n) -> p c n", c=DC),
                                     ACT.Copy).then_inc(hi_done, 1)

            def ones_rows(g, first):
                if not first:
                    act.wait_ge(kv_done, g * G)
                    act.wait_ge(ib_saved, g * 16)
                act.wait_ge(ibt_done, g + 1)
                nc.scalar.activation(ib[:, :, :], bank[2][0:3, :].rearrange("p (j n) -> p j n", j=G), ACT.Copy).then_inc(ib_done, 1)

            def values(g, j, first):
                t = g * G + j
                if not (first and j < 2):
                    act.wait_ge(prod_done, 2 * (t - 2) + 2)
                act.wait_ge(kv_done, t + 1)
                nc.scalar.activation(kv[:, j % 2, :], bank[j % 2][:, :], ACT.Copy).then_inc(v_done, 1)
                act.wait_ge(v_done, t + 1)
                if j == 0 and not first:
                    act.wait_ge(w_ready, 2 * g)
                act.wait_ge(sq_done, 2 * t) if (not first or j > 0) else None
                nc.scalar.activation(junk[:, 0, :], kv[:, j % 2, 0:D], ACT.Square, accum_out=nrm[:, j, 0:1]).then_inc(sq_done, 1)
                nc.scalar.activation(junk[:, 1, :], kv[:, j % 2, D:2 * D], ACT.Square, accum_out=nrm[:, j, 1:2]).then_inc(sq_done, 1)

            def body(g, first=False):
                hi(g, 0, first)
                hi(g, 1, first)
                ones_rows(g, first)
                values(g, 0, first)
                hi(g, 2, first)
                values(g, 1, first)
                hi(g, 3, first)
                values(g, 2, first)
                values(g, 3, first)

            body(0, first=True)
            with act.Fori(1, GROUPS) as g:
                body(g)

            act.wait_ge(lm_done, 1)
            nc.scalar.activation(ex[:, :, :], lg[:, :, :], ACT.Exp).then_inc(exp_done, 1)
            for b in range(BATCH):
                for c in range(DC):
                    act.wait_ge(m_done, b * DC + c + 1)
                    nc.scalar.activation(m_s[:, b, c, 0, :], bank[b * DC + c][:, 0:D], ACT.Copy, scale=gam[:, c:c + 1]).then_inc(m_hi, 1)

            act.wait_ge(sw_in, 64)
            nc.scalar.activation(swg_s[:, :, 0, :], swg[:, :, :], ACT.Copy).then_inc(act_prep, 1)
            nc.scalar.activation(swu_s[:, :, 0, :], swu[:, :, :], ACT.Copy).then_inc(act_prep, 1)
            nc.scalar.activation(swd_s[:, 0:2, 0, :], swd[:, 0:2, :], ACT.Copy).then_inc(act_prep, 1)
            nc.scalar.activation(swd_s[0:SC[2], 2, 0, :], swd[0:SC[2], 2, :], ACT.Copy).then_inc(act_prep, 1)

            def evac(e, k):
                if not (isinstance(e, int) and e < 2):
                    act.wait_ge(gu_done, e - 1)
                act.wait_ge(xt_e, e + 1)
                nc.scalar.activation(xgt[:, k, :, :], bank[4 + k][:, 0:D].rearrange("p (c n) -> p c n", c=DC),
                                     ACT.Copy).then_inc(xgt_done, 1)

            def silu(e, k):
                if not (isinstance(e, int) and e < 2):
                    act.wait_ge(mid_done, 2 * (e - 1))
                act.wait_ge(gu_done, e + 1)
                nc.scalar.activation(sil[:, k, 0, :], bank[k][:, 0:P], ACT.Silu).then_inc(silu_done, 1)
                nc.scalar.activation(sil[0:I2, k, 1, :], bank[k][0:I2, 2 * P:3 * P], ACT.Silu).then_inc(silu_done, 1)

            def moe_body(h, last=False):
                for j in range(G):
                    e = h * G + j
                    if not (last and j == G - 1):
                        evac(e + 1, (j + 1) % 2)
                    silu(e, j % 2)

            evac(0, 0)
            moe_body(0)
            with act.Fori(1, E // G - 1) as h:
                moe_body(h)
            moe_body(E // G - 1, last=True)

            def shared(g, first=False):
                for c in range(3):
                    n = SC[c]
                    q = g * 3 + c
                    if not (first and c < 2):
                        act.wait_ge(sm_done, q - 1)
                    act.wait_ge(sh_done, q + 1)
                    k = c % 2
                    if not first and c == 0:
                        act.wait_ge(sm_done, q)
                    nc.scalar.activation(sg[0:n, k, :], bank[2 * k][0:n, :], ACT.Silu).then_inc(sg_done, 1)
                    act.wait_ge(sm_done, q + 1)
                    if not first:
                        act.wait_ge(dn_done, g * G)
                    nc.scalar.activation(smid_s[0:n, c, 0, :], smid[0:n, k, :], ACT.Copy).then_inc(hi_m, 1)

            shared(0, first=True)
            with act.Fori(1, GROUPS) as g:
                shared(g)

        @block.vector
        def _(dve):
            def stats(g, j):
                t = g * G + j
                if j == 0 and not (isinstance(g, int) and g == 0):
                    dve.wait_ge(i3_ready, 3 * g)
                dve.wait_ge(x_ready, g + 1)
                if not (isinstance(g, int) and g == 0 and j == 0):
                    dve.wait_ge(stats_done, t)
                nc.vector.bn_stats(st6[:, :], x_all[:, t, :]).then_inc(st_chain, 1)
                dve.wait_ge(st_chain, t + 1)
                dve.sem_inc(dve_passed, 1)
                nc.vector.bn_aggr(mv[:, j, :], st6[:, :]).then_inc(stats_done, 1)

            def norm(g, j, first):
                t = g * G + j
                dve.wait_ge(ln_ready, g + 1)
                if not first:
                    dve.wait_ge(t_done, t - G + 1)
                    dve.wait_ge(xn_saved[j], g * 16)
                    dve.wait_ge(res_done, t - G + 1)
                nc.vector.tensor_scalar(xn[:, j, :], x_all[:, t, :], mv[:, j, 0:1], rstd[:, bass.ds(t, 1)],
                                        ALU.subtract, ALU.mult).then_inc(norm_done, 1)

            def lo(g, j, first):
                t = g * G + j
                if not first:
                    dve.wait_ge(kv_done, t - G + 1)
                    dve.wait_ge(xt_saved[j], g * 16)
                dve.wait_ge(hi_done, t + 1)
                nc.vector.tensor_tensor(hl[:, j, 1, :, :], bank[4 + j % 2][:, 0:D].rearrange("p (c n) -> p c n", c=DC),
                                        f(hl[:, j, 0, :, :]), ALU.subtract).then_inc(lo_done, 1)

            def products(g, j, first):
                t = g * G + j
                if j == 0 and not first:
                    dve.wait_ge(red_done, g)
                dve.wait_ge(v_done, t + 1)
                k_, v_ = kv[:, j % 2, 0:D], kv[:, j % 2, D:2 * D]
                nc.vector.tensor_tensor(ph[:, j, 0:D], k_, v_, ALU.mult).then_inc(prod_done, 1)
                v2 = v_[:, 0:ROT].rearrange("p (a n) -> p a n", a=2)[:, ::-1, :]
                nc.vector.tensor_tensor(ph[:, j, D:D + ROT].rearrange("p (a n) -> p a n", a=2),
                                        k_[:, 0:ROT].rearrange("p (a n) -> p a n", a=2), v2, ALU.mult).then_inc(prod_done, 1)

            def scores_read(g, first):
                if not first:
                    dve.wait_ge(rt_read, g * 11)
                dve.wait_ge(router_done, g + 1)
                nc.vector.tensor_copy(sc[:, :, :], bank[6][:, 0:G * E].rearrange("p (j e) -> p j e", j=G)).then_inc(sc_read, 1)

            def scores(g):
                s = sc[:, :, :]
                dve.wait_ge(sc_read, g + 1)
                nc.vector.tensor_scalar(lg[:, bass.ds(g * G, G), :], s, 0.0, None, ALU.add).then_inc(rt_read, 1)
                for j in range(G):
                    nc.vector.max(mx[:, j, :], s[:, j, :]).then_inc(rt_read, 1)
                dve.wait_ge(rt_read, g * 11 + 5)
                nc.vector.tensor_scalar(top1[:, bass.ds(g * G, G)], mx[:, :, 0], 0.0, None, ALU.add).then_inc(rt_read, 1)
                for j in range(G):
                    nc.vector.max_index(ix[:, j, :], mx[:, j, :], s[:, j, :]).then_inc(rt_read, 1)
                dve.wait_ge(rt_read, g * 11 + 10)
                nc.vector.tensor_scalar(ixf[:, bass.ds(g * G, G), :], ix[:, :, 0:TOP], 0.0, None, ALU.add).then_inc(rt_read, 1)

            def body(g, first=False, last=False):
                lo(g, 0, first)
                if not last:
                    stats(g + 1, 0)
                    stats(g + 1, 1)
                lo(g, 1, first)
                if not last:
                    stats(g + 1, 2)
                    stats(g + 1, 3)
                products(g, 0, first)
                lo(g, 2, first)
                products(g, 1, first)
                lo(g, 3, first)
                if not first:
                    asum_read(g - 1)
                products(g, 2, first)
                scores_read(g, first)
                if not last:
                    for j in range(G):
                        norm(g + 1, j, False)
                products(g, 3, first)
                scores(g)

            def asum_read(g):
                dve.wait_ge(red_done, g + 1)
                nc.vector.tensor_scalar(asum[0:1, bass.ds(g, 1), :], bank[7][0:1, 0:D + ROT].unsqueeze(1), 0.0, None, ALU.add).then_inc(a_read, 1)

            for j in range(G):
                stats(0, j)
            nc.vector.memset(ones3[:, :], 1.0).then_inc(ones_set, 1)
            nc.vector.memset(one16[:, :], 1.0).then_inc(ones_set, 1)
            dve.wait_ge(wi_in, 64)
            nc.vector.tensor_copy(bet3[:, :, :], bet[:, :].unsqueeze(2).to_broadcast([P, DC, 3])).then_inc(ones_set, 1)
            for j in range(G):
                norm(0, j, True)
            for c in range(DC):
                dve.wait_ge(act_prep, c + 1)
                nc.vector.scalar_tensor_tensor(wkv_s[:, c, 1, :], wi[:, c, D:3 * D], gam[:, c:c + 1], f(wkv_s[:, c, 0, :]),
                                               ALU.mult, ALU.subtract).then_inc(prep_done, 1)
            dve.wait_ge(act_prep, 3)
            nc.vector.tensor_tensor(gt_s[:, :, 1, :], gt[:, :, :], f(gt_s[:, :, 0, :]), ALU.subtract).then_inc(prep_done, 1)
            dve.wait_ge(cst_in, 16)
            dve.wait_ge(act_prep, 5)
            nc.vector.tensor_tensor(b3l[:, :], b3f[:, :], f(b3h[:, :]), ALU.subtract).then_inc(prep_chain, 1)
            dve.wait_ge(prep_chain, 1)
            nc.vector.tensor_scalar(b3l[:, :], b3l[:, :], cst[0:3, C_ROW + 1:C_ROW + 2], None, ALU.mult).then_inc(prep_chain, 1)
            dve.wait_ge(prep_chain, 2)
            nc.vector.scalar_tensor_tensor(b3[:, :], f(b3h[:, :]), cst[0:3, C_ROW:C_ROW + 1], b3l[:, :],
                                           ALU.mult, ALU.add).then_inc(prep_done, 1)

            body(0, first=True)
            with dve.Fori(1, GROUPS - 1) as g:
                body(g)
            body(GROUPS - 1, last=True)

            chain = [0]

            def link(ins):
                chain[0] += 1
                ins.then_inc(r_chain, 1)
                dve.wait_ge(r_chain, chain[0])

            asum_read(GROUPS - 1)
            dve.wait_ge(a_read, GROUPS)

            dve.wait_ge(rt_read, 11 * GROUPS)
            link(nc.vector.tensor_copy(iota16[:, :], cst[:, C_I16:C_I16 + E]))
            link(nc.vector.tensor_tensor(ex[:, :, :], lg[:, :, :], top1[:, :].unsqueeze(2).to_broadcast([P, TILES, E]), ALU.subtract))
            nc.vector.tensor_copy(lg[:, :, :], ex[:, :, :]).then_inc(lm_done, 1)
            link(nc.vector.tensor_tensor(eq[:, :, :, :], ixf[:, :, :].unsqueeze(3).to_broadcast([P, TILES, TOP, E]),
                                         cst[:, C_I16:C_I16 + E].unsqueeze(1).unsqueeze(1).to_broadcast([P, TILES, TOP, E]), ALU.is_equal))
            link(nc.vector.tensor_reduce(mask[:, :, :], eq[:, :, :, :].rearrange("p t k e -> p t e k"), axis=AX.X, op=ALU.add))
            nc.vector.tensor_copy(mask16[:, :, :], mask[:, :, :]).then_inc(mask_done, 1)
            nc.vector.tensor_copy(tri16[:, :], cst[:, C_TRI:C_TRI + P]).then_inc(mask_done, 1)
            nc.vector.tensor_copy(exp16[:, :], cst[:, C_EXP:C_EXP + E]).then_inc(mask_done, 1)
            link(nc.vector.tensor_copy(tok16[:, :], cst[:, C_TOK:C_TOK + TILES]))
            dve.wait_ge(rank_done, 1)
            link(nc.vector.scalar_tensor_tensor(rank[:, :, :], mask[:, :, :], -1024.0, bank[7][:, 0:TILES * E].rearrange("p (t e) -> p t e", t=TILES),
                                                ALU.mult, ALU.add))
            link(nc.vector.tensor_scalar(rank_i[:, :, :], rank[:, :, :], 1024.0, None, ALU.add))
            link(nc.vector.tensor_scalar(ra_i[:, :, :], rank_i[:, :, :], 4, None, ALU.logical_shift_right))
            link(nc.vector.tensor_copy(ra[:, :, :], ra_i[:, :, :]))
            dve.wait_ge(res_done, TILES)
            nc.vector.tensor_tensor(oa[:, :, :, :], ra[:, :, :].unsqueeze(3).to_broadcast([P, TILES, E, SLOT_A]),
                                    iota16[:, 0:SLOT_A].unsqueeze(1).unsqueeze(1).to_broadcast([P, TILES, E, SLOT_A]),
                                    ALU.is_equal).then_inc(onehot_done, 1)
            link(nc.vector.tensor_scalar(rb_i[:, :, :], rank_i[:, :, :], SLOT_B - 1, None, ALU.bitwise_and))
            link(nc.vector.tensor_copy(rb[:, :, :], rb_i[:, :, :]))
            nc.vector.tensor_tensor(ob[:, :, :, :], rb[:, :, :].unsqueeze(3).to_broadcast([P, TILES, E, SLOT_B]),
                                    iota16[:, :].unsqueeze(1).unsqueeze(1).to_broadcast([P, TILES, E, SLOT_B]),
                                    ALU.is_equal).then_inc(onehot_done, 1)
            dve.wait_ge(exp_done, 1)
            link(nc.vector.tensor_reduce(zsum[:, :], ex[:, :, :], axis=AX.X, op=ALU.add))
            link(nc.vector.tensor_tensor(em[:, :, :], ex[:, :, :], mask[:, :, :], ALU.mult))
            link(nc.vector.tensor_reduce(esum[:, :], em[:, :, :], axis=AX.X, op=ALU.add))
            link(nc.vector.scalar_tensor_tensor(esum[:, :], zsum[:, :], 1e-20, esum[:, :], ALU.mult, ALU.add))
            link(nc.vector.reciprocal(einv[:, :], esum[:, :]))
            nc.vector.tensor_tensor(wd[:, :, :], em[:, :, :], einv[:, :].unsqueeze(2).to_broadcast([P, TILES, E]), ALU.mult).then_inc(wd_done, 1)
            dve.wait_ge(table_done, 1)
            link(nc.vector.tensor_tensor(diag[:, :, :], bank[6][:, 0:E * SLOT_B].rearrange("p (e b) -> p e b", e=E),
                                         cst[:, C_EXP:C_EXP + E].unsqueeze(2).to_broadcast([P, E, SLOT_B]), ALU.mult))
            link(nc.vector.tensor_reduce(tb[:, :], diag[:, :, :].rearrange("p e b -> p b e"), axis=AX.X, op=ALU.add))
            nc.vector.tensor_tensor(spread[:, :, :], tb[:, :].unsqueeze(1).to_broadcast([P, SLOT_A, SLOT_B]),
                                    cst[:, C_ASEL:C_ASEL + SLOT_A].unsqueeze(2).to_broadcast([P, SLOT_A, SLOT_B]), ALU.mult).then_inc(spread_done, 1)
            dve.wait_ge(slot_done, 1)
            link(nc.vector.tensor_copy(slot_v[:, :], bank[6][:, 256:256 + E]))
            link(nc.vector.tensor_scalar(slot_e[:, :], slot_v[:, :], 0.0, cst[:, C_SPARE:C_SPARE + 1], ALU.is_equal, ALU.mult))
            link(nc.vector.tensor_tensor(slot_f[:, :], slot_v[:, :], slot_e[:, :], ALU.add))
            nc.vector.tensor_scalar(idx[:, :], slot_f[:, :], -1.0, None, ALU.add).then_inc(idx_done, 1)

            av = asum[:, :, :].rearrange("o (b g) n -> o b g n", b=BATCH)
            link(nc.vector.tensor_tensor(ab[:, :, :], av[:, :, 0, :], av[:, :, 1, :], ALU.add))
            link(nc.vector.tensor_tensor(aq[:, :, :], ab[:, :, 0:HALF], ab[:, :, HALF:ROT], ALU.add))
            link(nc.vector.tensor_scalar(aq[:, :, :], aq[:, :, :], 0.25, 0.5, ALU.mult, ALU.add))
            link(nc.vector.tensor_tensor(af[:, :, :], ab[:, :, D:D + HALF], ab[:, :, D + HALF:D + ROT], ALU.add))
            link(nc.vector.tensor_tensor(arow[:, :, 0:HALF], aq[:, :, :], af[:, :, :], ALU.add))
            link(nc.vector.tensor_tensor(arow[:, :, HALF:ROT], aq[:, :, :], af[:, :, :], ALU.subtract))
            nc.vector.tensor_scalar(arow[:, :, ROT:D], ab[:, :, ROT:D], 0.5, 0.5, ALU.mult, ALU.add).then_inc(arow_done, 1)
            dve.wait_ge(acol_done, 1)
            link(nc.vector.tensor_copy(acol[:, :], bank[4][:, 0:BATCH * DC]))
            nc.vector.tensor_copy(bq3[:, :, :], bank[4][:, 8:8 + DC * 3].rearrange("p (c k) -> p c k", c=DC)).then_inc(aw_done, 1)
            dve.wait_ge(mix_in, 48)
            for b in range(BATCH):
                for c in range(DC):
                    nc.vector.tensor_scalar(aw[:, b, c, :], wo[:, c, :], acol[:, b * DC + c:b * DC + c + 1], None, ALU.mult).then_inc(aw_done, 1)
            for b in range(BATCH):
                for c in range(DC):
                    dve.wait_ge(m_hi, b * DC + c + 1)
                    nc.vector.scalar_tensor_tensor(m_s[:, b, c, 1, :], bank[b * DC + c][:, 0:D], gam[:, c:c + 1], f(m_s[:, b, c, 0, :]),
                                                   ALU.mult, ALU.subtract).then_inc(m_lo, 1)
            dve.wait_ge(c_done, 1)
            link(nc.vector.tensor_copy(c3f[:, :, :], bank[7][0:3, :].rearrange("p (b n) -> p b n", b=BATCH)))
            link(nc.vector.tensor_copy(c3h[:, :, :], c3f[:, :, :]))
            link(nc.vector.tensor_tensor(c3l[:, :, :], c3f[:, :, :], f(c3h[:, :, :]), ALU.subtract))
            link(nc.vector.tensor_scalar(c3l[:, :, :], c3l[:, :, :], cst[0:3, C_ROW + 1:C_ROW + 2], None, ALU.mult))
            nc.vector.scalar_tensor_tensor(c3[:, :, :], f(c3h[:, :, :]), cst[0:3, C_ROW:C_ROW + 1], c3l[:, :, :],
                                           ALU.mult, ALU.add).then_inc(c3_done, 1)
            dve.wait_ge(act_prep, 9)
            nc.vector.tensor_tensor(swg_s[:, :, 1, :], swg[:, :, :], f(swg_s[:, :, 0, :]), ALU.subtract).then_inc(prep_done, 1)
            nc.vector.tensor_tensor(swu_s[:, :, 1, :], swu[:, :, :], f(swu_s[:, :, 0, :]), ALU.subtract).then_inc(prep_done, 1)
            nc.vector.tensor_tensor(swd_s[:, 0:2, 1, :], swd[:, 0:2, :], f(swd_s[:, 0:2, 0, :]), ALU.subtract).then_inc(prep_done, 1)
            nc.vector.tensor_tensor(swd_s[0:SC[2], 2, 1, :], swd[0:SC[2], 2, :], f(swd_s[0:SC[2], 2, 0, :]), ALU.subtract).then_inc(prep_done, 1)

            def gated(e, k):
                if not (isinstance(e, int) and e < 2):
                    dve.wait_ge(d_done, e - 1)
                dve.wait_ge(silu_done, 2 * e + 2)
                nc.vector.tensor_tensor(mid[:, k, 0, :], sil[:, k, 0, :], bank[k][:, P:2 * P], ALU.mult).then_inc(mid_done, 1)
                nc.vector.tensor_tensor(mid[0:I2, k, 1, :], sil[0:I2, k, 1, :], bank[k][UP2:UP2 + I2, 2 * P:3 * P], ALU.mult).then_inc(mid_done, 1)

            def weigh(e, j, first):
                if not first:
                    dve.wait_ge(scat_done, 16 * (e - G + 1))
                dve.wait_ge(d_done, e + 1)
                nc.vector.tensor_scalar(eo[:, j, :], bank[2 + j % 2][:, 0:D], xg[:, j, bass.ds(D + e, 1)], None, ALU.mult).then_inc(eo_done, 1)

            def moe_body(h, first=False):
                for j in range(G):
                    e = h * G + j
                    gated(e, j % 2)
                    if not (first and j == 0):
                        weigh(e - 1, (j - 1) % G, first)

            moe_body(0, first=True)
            gated(G, 0)
            weigh(G - 1, G - 1, True)
            for j in range(1, G):
                gated(G + j, j % 2)
                weigh(G + j - 1, j - 1, False)
            with dve.Fori(2, E // G) as h:
                moe_body(h)
            weigh(E - 1, G - 1, False)

            def shared(g, first=False):
                for c in range(3):
                    n, k, q = SC[c], c % 2, g * 3 + c
                    dve.wait_ge(sg_done, q + 1)
                    if not (first and c < 2):
                        dve.wait_ge(lo_m, q - 1)
                        if c == 0:
                            dve.wait_ge(lo_m, q)
                    nc.vector.tensor_tensor(smid[0:n, k, :], sg[0:n, k, :], bank[2 * k + 1][0:n, :], ALU.mult).then_inc(sm_done, 1)
                    dve.wait_ge(hi_m, q + 1)
                    nc.vector.tensor_tensor(smid_s[0:n, c, 1, :], smid[0:n, k, :], f(smid_s[0:n, c, 0, :]), ALU.subtract).then_inc(lo_m, 1)
                dve.wait_ge(y_in, g * 16 + 16)
                for j in range(G):
                    t = g * G + j
                    if not first:
                        dve.wait_ge(out_sent[j], g * 16)
                    dve.wait_ge(att_done, t + 1)
                    nc.vector.scalar_tensor_tensor(ot[:, j, :], bank[4 + j][:, 0:D], s2[:, bass.ds(t, 1)], yin[:, j, :],
                                                   ALU.mult, ALU.add).then_inc(acc_done, 1)
                for j in range(G):
                    t = g * G + j
                    dve.wait_ge(acc_done, t + 1)
                    dve.wait_ge(dn_done, t + 1)
                    nc.vector.tensor_tensor(ot[:, j, :], ot[:, j, :], bank[4 + j][:, D:2 * D], ALU.add).then_inc(ot_done, 1)

            shared(0, first=True)
            with dve.Fori(1, GROUPS) as g:
                shared(g)

        @block.tensor
        def _(pe):
            ident = cst[:, C_ID:C_ID + P]
            pe.wait_ge(ones_set, 3)
            pe.wait_ge(wi_in, 64)
            for c in range(DC):
                nc.tensor.matmul(bank[3][0:3, :], bet3[:, c, :], wi[:, c, D:3 * D], start=c == 0, stop=False)
            nc.tensor.matmul(bank[3][0:3, :], ones3[:, 0:3], bin_row[:, D:3 * D], start=False, stop=True).then_inc(pe_prep, 1)
            pe.wait_ge(cst_in, 16)

            def turn(g, j, first):
                t = g * G + j
                pe.wait_ge(norm_done, t + 1)
                if not (first and j < 2):
                    pe.wait_ge(lo_done, t - 1)
                for c in range(DC):
                    last = nc.tensor.transpose(bank[4 + j % 2][:, c * P:(c + 1) * P], xn[:, j, c * P:(c + 1) * P], ident)
                last.then_inc(t_done, 1)

            def turn_rows(g, first):
                pe.wait_ge(i3_ready, 3 * g + 3)
                if not first:
                    pe.wait_ge(ib_done, g)
                for j in range(G):
                    last = nc.tensor.transpose(bank[2][0:3, j * P:(j + 1) * P], i3[:, j, :], ident)
                last.then_inc(ibt_done, 1)

            def route(g, j, first):
                t = g * G + j
                pe.wait_ge(lo_done, t + 1)
                if first and j == 0:
                    pe.wait_ge(prep_done, 4)
                if not first and j == 0:
                    pe.wait_ge(sc_read, g)
                for c in range(DC):
                    last = mm3(bank[6][:, j * E:(j + 1) * E], hl[:, j, 0, c, :], hl[:, j, 1, c, :],
                               gt_s[:, c, 0, :], gt_s[:, c, 1, :], c == 0, c == DC - 1)
                if j == G - 1:
                    last.then_inc(router_done, 1)

            def keys(g, j, first):
                t = g * G + j
                if j == 0:
                    pe.wait_ge(ib_done, g + 1)
                if not (first and j < 2):
                    pe.wait_ge(v_done, t - 1)
                for c in range(DC):
                    mm3(bank[j % 2][:, :], hl[:, j, 0, c, :], hl[:, j, 1, c, :], wkv_s[:, c, 0, :], wkv_s[:, c, 1, :], c == 0, False)
                nc.tensor.matmul(bank[j % 2][:, :], ib[:, j, :], b3[:, :], start=False, stop=True).then_inc(kv_done, 1)

            def reduce(g, first):
                pe.wait_ge(w_ready, 2 * g + 2)
                pe.wait_ge(tab_done, g * G + G)
                if not first:
                    pe.wait_ge(a_read, g)
                for j in range(G):
                    last = nc.tensor.matmul(bank[7][0:1, 0:D + ROT], wtok[:, j:j + 1], ph[:, j, :], start=j == 0, stop=j == G - 1)
                last.then_inc(red_done, 1)

            def body(g, first=False, second=False):
                turn(g, 0, first)
                turn(g, 1, first)
                turn_rows(g, first)
                if not first:
                    reduce(g - 1, second)
                route(g, 0, first)
                keys(g, 0, first)
                turn(g, 2, first)
                route(g, 1, first)
                keys(g, 1, first)
                turn(g, 3, first)
                for j in (2, 3):
                    route(g, j, first)
                    keys(g, j, first)

            body(0, first=True)
            body(1, second=True)
            with pe.Fori(2, GROUPS) as g:
                body(g)
            reduce(GROUPS - 1, False)

            pe.wait_ge(mask_done, 3)
            pe.wait_ge(a_read, GROUPS)
            nc.tensor.matmul(bank[7][:, 0:TILES * E], tri16[:, :], mask16[:, :, :].rearrange("p t e -> p (t e)"), start=True, stop=False)
            for t in range(TILES - 1):
                n = TILES - 1 - t
                last = nc.tensor.matmul(bank[7][:, (t + 1) * E:TILES * E].rearrange("p (t e) -> p t e", e=E), one16[:, :],
                                        mask16[:, t:t + 1, :].to_broadcast([P, n, E]), start=False, stop=t == TILES - 2)
            last.then_inc(rank_done, 1)
            pe.wait_ge(rt_read, 11 * GROUPS)
            pe.wait_ge(onehot_done, 2)
            pe.wait_ge(oa_done, 1)
            for t in range(TILES):
                last = nc.tensor.matmul(bank[6][:, 0:E * SLOT_B], oat[:, t, :, :].rearrange("p e a -> p (e a)"),
                                        ob[:, t, :, :].rearrange("p e b -> p (e b)"), start=t == 0, stop=t == TILES - 1)
            last.then_inc(table_done, 1)
            pe.wait_ge(spread_done, 1)
            nc.tensor.matmul(bank[6][:, 256:256 + E], spread[:, :, :].rearrange("p a b -> p (a b)"), exp16[:, :],
                             start=True, stop=True).then_inc(slot_done, 1)

            pe.wait_ge(lo_done, TILES)
            pe.wait_ge(arow_done, 1)
            for b in range(BATCH):
                for c in range(DC):
                    nc.tensor.matmul(bank[4][:, b * DC + c:b * DC + c + 1], arow[0:1, b, c * P:(c + 1) * P], ones3[0:1, 0:1], start=True, stop=True)
            for c in range(DC):
                for k in range(DC):
                    nc.tensor.matmul(bank[4][:, 8 + c * 3:11 + c * 3], wi[:, k, c * P:(c + 1) * P], bet3[:, k, :], start=k == 0, stop=False)
                last = nc.tensor.matmul(bank[4][:, 8 + c * 3:11 + c * 3], bin_row[:, c * P:(c + 1) * P], ones3[:, 0:3], start=False, stop=True)
            last.then_inc(acol_done, 1)
            pe.wait_ge(aw_done, 1 + BATCH * DC)
            pe.wait_ge(mix_in, 48)
            for b in range(BATCH):
                for c in range(DC):
                    for k in range(DC):
                        last = nc.tensor.matmul(bank[b * DC + c][:, 0:D], wqt[:, k, c * P:(c + 1) * P], aw[:, b, k, :], start=k == 0, stop=k == DC - 1)
                    last.then_inc(m_done, 1)
            for b in range(BATCH):
                for k in range(DC):
                    nc.tensor.matmul(bank[7][0:3, b * D:(b + 1) * D], bq3[:, k, :], aw[:, b, k, :], start=k == 0, stop=False)
                last = nc.tensor.matmul(bank[7][0:3, b * D:(b + 1) * D], ones3[:, 0:3], bout_row[:, :], start=False, stop=True)
            last.then_inc(c_done, 1)

            def turn_rows_e(e, j, h):
                pe.wait_ge(gath[j], 16 * (h + 1))
                if not (isinstance(e, int) and e < 2):
                    pe.wait_ge(xgt_done, e - 1)
                for c in range(DC):
                    last = nc.tensor.transpose(bank[4 + j % 2][:, c * P:(c + 1) * P], xg[:, j, c * P:(c + 1) * P], ident)
                last.then_inc(xt_e, 1)

            def gate_up(e, j, h):
                k = j % 2
                pe.wait_ge(ew_in[j], 48 * (h + 1))
                if not (isinstance(e, int) and e < 2):
                    pe.wait_ge(mid_done, 2 * (e - 1))
                pe.wait_ge(xgt_done, e + 1)
                for q, (lo_, n) in enumerate(((0, P), (P, P), (2 * P, UP2 + I2))):
                    for c in range(DC):
                        last = nc.tensor.matmul(bank[k][0:n, q * P:(q + 1) * P], wgu[:, j, c, lo_:lo_ + n], xgt[:, k, c, :],
                                                start=c == 0, stop=c == DC - 1)
                last.then_inc(gu_done, 1)

            def down(e, j, first):
                k = j % 2
                pe.wait_ge(mid_done, 2 * e + 2)
                if not first:
                    pe.wait_ge(eo_done, e - 1)
                nc.tensor.matmul(bank[2 + k][:, 0:D], mid[:, k, 0, :], wdn[:, j, 0, :], start=True, stop=False)
                nc.tensor.matmul(bank[2 + k][:, 0:D], mid[0:I2, k, 1, :], wdn[0:I2, j, 1, :], start=False, stop=True).then_inc(d_done, 1)

            def moe_body(h, first=False, last=False):
                for j in range(G):
                    e = h * G + j
                    if not (last and j == G - 1):
                        turn_rows_e(e + 1, (j + 1) % G, h + (j + 1) // G)
                    gate_up(e, j, h)
                    if not (first and j == 0):
                        down(e - 1, (j - 1) % G, first and j <= 2)

            pe.wait_ge(acol_done, 1)
            pe.wait_ge(aw_done, 1 + BATCH * DC)
            pe.wait_ge(m_lo, BATCH * DC)
            turn_rows_e(0, 0, 0)
            moe_body(0, first=True)
            with pe.Fori(1, E // G - 1) as h:
                moe_body(h)
            moe_body(E // G - 1, last=True)
            down(E - 1, G - 1, False)

            pe.wait_ge(prep_done, 8)
            pe.wait_ge(c3_done, 1)
            pe.wait_ge(eo_done, E)

            def shared(g, first=False):
                b = g // GROUPS_B if isinstance(g, int) else (g >> (GROUPS_B // 2)) & (BATCH - 1)
                for c in range(3):
                    n, k, q = SC[c], c % 2, g * 3 + c
                    if not (first and c < 2):
                        pe.wait_ge(sm_done, q - 1)
                        if c == 0:
                            pe.wait_ge(sm_done, q)
                    for w_s, dst in ((swg_s, bank[2 * k]), (swu_s, bank[2 * k + 1])):
                        for d in range(DC):
                            xr = xt_all[:, bass.ds(g * G, G), :, d, :]
                            last = mm3(dst[0:n, :].rearrange("p (t n) -> p t n", n=P), w_s[:, d, 0, c * P:c * P + n], w_s[:, d, 1, c * P:c * P + n],
                                       xr[:, :, 0, :], xr[:, :, 1, :], d == 0, d == DC - 1)
                    last.then_inc(sh_done, 1)
                pe.wait_ge(stage_in, g * 32 + 32)
                for j in range(G):
                    t = g * G + j
                    if not first:
                        pe.wait_ge(ot_done, t - G + 1)
                    for d in range(DC):
                        mm3(bank[4 + j][:, 0:D], xs[:, j, 0, d, :], xs[:, j, 1, d, :], m_s[:, bass.ds(b, 1), d, 0, :], m_s[:, bass.ds(b, 1), d, 1, :], d == 0, False)
                    nc.tensor.matmul(bank[4 + j][:, 0:D], ibs[:, j, :], c3[:, bass.ds(b, 1), :], start=False, stop=True).then_inc(att_done, 1)
                pe.wait_ge(lo_m, g * 3 + 3)
                for j in range(G):
                    pe.wait_ge(acc_done, g * G + j + 1)
                    for c in range(3):
                        n = SC[c]
                        last = mm3(bank[4 + j][:, D:2 * D], smid_s[0:n, c, 0, j * P:(j + 1) * P], smid_s[0:n, c, 1, j * P:(j + 1) * P],
                                   swd_s[0:n, c, 0, :], swd_s[0:n, c, 1, :], c == 0, c == 2)
                    last.then_inc(dn_done, 1)

            shared(0, first=True)
            with pe.Fori(1, GROUPS) as g:
                shared(g)


def kernel(L0_attn_X, L0_attn_W_in, L0_attn_b_in, L0_attn_W_out, L0_attn_b_out, L0_attn_gamma, L0_attn_beta,
           L0_ffn_gate_w, L0_ffn_w_gate, L0_ffn_w_up, L0_ffn_w_down, L0_ffn_sw_gate, L0_ffn_sw_up, L0_ffn_sw_down):
    import numpy as np
    import concourse.bacc as bacc
    from concourse.bass_utils import run_bass_kernel_spmd as run

    order = np.concatenate([np.arange(0, ROT, 2), np.arange(1, ROT, 2), np.arange(ROT, D)])
    w_in, b_in = np.asarray(L0_attn_W_in), np.asarray(L0_attn_b_in)
    cols = np.concatenate([order + k * D for k in range(3)])
    w_gate, w_up = np.asarray(L0_ffn_w_gate), np.asarray(L0_ffn_w_up)
    gap = np.zeros((E, D, UP2 - I2), np.float32)
    w_gu = np.concatenate([w_gate[:, :, :P], w_up[:, :, :P], w_gate[:, :, P:], gap, w_up[:, :, P:]], axis=2)

    seq = TOKENS // BATCH
    inv = (1.0 / np.float32(10000.0) ** (np.arange(0, ROT, 2, dtype=np.float32) / np.float32(ROT))).astype(np.float32)
    angle = (np.arange(seq, dtype=np.float32)[:, None] * inv[None, :]).astype(np.float64)
    cos, sin = np.cos(2 * angle) / 4, np.sin(2 * angle) / 4
    trig = np.concatenate([cos, -cos, -sin, -sin], axis=1).astype(np.float32)

    p = np.arange(P)
    consts = np.zeros((P, C_ALL), np.float32)
    consts[:, C_ID:C_ID + P] = np.eye(P)
    consts[:, C_TRI:C_TRI + P] = p[:, None] < p[None, :]
    consts[:, C_EXP:C_EXP + E] = (p[:, None] // SLOT_A) == np.arange(E)[None, :]
    consts[:, C_ASEL:C_ASEL + SLOT_A] = (p[:, None] % SLOT_A) == np.arange(SLOT_A)[None, :]
    consts[:, C_I16:C_I16 + E] = np.arange(E)[None, :]
    consts[:, C_TOK:C_TOK + TILES] = P * np.arange(TILES)[None, :] + p[:, None] + 1
    consts[:, C_SPARE] = TOKENS + 1 + p
    consts[0:3, C_ROW] = (1, 0, 1)
    consts[0:3, C_ROW + 1] = (0, 1, 0)

    ins = {
        "x": L0_attn_X, "w_in": w_in[:, cols], "b_in": b_in[cols], "wq_t": w_in[:, order].T,
        "w_out": np.asarray(L0_attn_W_out)[order, :], "b_out": L0_attn_b_out,
        "gamma": np.asarray(L0_attn_gamma).reshape(DC, P).T, "beta": np.asarray(L0_attn_beta).reshape(DC, P).T,
        "gate_t": np.asarray(L0_ffn_gate_w).T, "w_gu": w_gu, "w_dn": L0_ffn_w_down,
        "sw_g": L0_ffn_sw_gate, "sw_u": L0_ffn_sw_up, "sw_d": L0_ffn_sw_down, "trig": trig, "consts": consts,
    }
    nc = bacc.Bacc("TRN2", target_bir_lowering=False, num_devices=1)
    arrays, args = {}, []
    for name, a in ins.items():
        a = np.ascontiguousarray(a)
        arrays[f"in_{name}"] = a
        args.append(nc.dram_tensor(f"in_{name}", a.shape, mybir.dt.from_np(a.dtype), kind="ExternalInput").ap())
    args.append(nc.dram_tensor("out", (BATCH, TOKENS // BATCH, D), F32, kind="ExternalOutput").ap())
    layer(nc, *args)
    r = run(nc, [arrays], core_ids=[0])
    return r.results[0]["out"]
```

```python
from contextlib import ExitStack

import concourse.bass as bass
from concourse import mybir

P = 128
TOKENS, D, BATCH = 2048, 256, 2
TILES = TOKENS // P
G = 4
GROUPS = TILES // G
GROUPS_B = GROUPS // BATCH
TILES_B = TILES // BATCH
DC = D // P
ROT = D // 2
HALF = ROT // 2
E, TOP, CAP = 16, 4, 128
I = 176
I2 = I - P
UP2 = 64
GU = 2 * P + UP2 + I2
IS = 352
SC = [P, P, IS - 2 * P]
ROW = D + E
SLOT_A, SLOT_B = 8, 16
EPS = 1e-5
GAP_PAIR = (0, 4, 0)
UNIT_BANK = (4, 5, 6, 7, 0, 1, 2, 3)

F32 = mybir.dt.float32
F32R = mybir.dt.float32r
F16 = mybir.dt.float16
I32 = mybir.dt.int32
U32 = mybir.dt.uint32
ALU = mybir.AluOpType
ACT = mybir.ActivationFunctionType
AX = mybir.AxisListType

C_ID = 0
C_TRI = C_ID + P
C_EXP = C_TRI + P
C_ASEL = C_EXP + E
C_I16 = C_ASEL + SLOT_A
C_TOK = C_I16 + E
C_SPARE = C_TOK + TILES
C_ROW = C_SPARE + 1
C_ALL = C_ROW + 2


def layer(nc, x, w_in, bias, wq_t, w_out, gb, w_gu, w_dn, sw_g, sw_u, sw_d,
          trig, consts, out):
    ctx = ExitStack()
    with ctx:
        def sb(name, shape, dt=F32):
            return ctx.enter_context(nc.sbuf_tensor(name, shape, dt))

        def sem(name):
            return ctx.enter_context(nc.semaphore(name))

        def sems(name, n):
            return [sem(f"{name}{i}") for i in range(n)]

        rows = nc.dram_tensor("rows", (TOKENS + CAP, ROW), F32, kind="Internal").ap()
        ysum = nc.dram_tensor("ysum", (TOKENS + CAP, D), F32, kind="Internal").ap()

        cst = sb("cst", [P, C_ALL])
        x_all = sb("x_all", [P, TILES, D])
        wi = sb("wi", [P, DC, 3 * D + E])
        wqt = sb("wqt", [P, DC, D])
        wo = sb("wo", [P, DC, D])
        sh = x_all
        gt = wi[:, :, 3 * D:3 * D + E]
        bias_row = sb("bias_row", [1, 4 * D])
        bin_row, bout_row = bias_row[:, 0:3 * D], bias_row[:, 3 * D:4 * D]
        gb_cols = sb("gb_cols", [P, 2 * DC])
        gam, bet = gb_cols[:, 0:DC], gb_cols[:, DC:2 * DC]
        trg = sb("trg", [P, TILES_B, D])
        ones3 = sb("ones3", [1, 4])
        bet3 = sb("bet3", [P, DC, 3])
        wkv_s = sb("wkv_s", [P, DC, 2, 2 * D], F32R)
        gt_s = sb("gt_s", [P, DC, 2, E], F32R)
        swg_s, swu_s = sb("swg_s", [P, DC, 2, IS], F32R), sb("swu_s", [P, DC, 2, IS], F32R)
        swd_s = sb("swd_s", [P, 3, 2, D], F32R)
        b3f, b3h, b3l = sb("b3f", [3, 2 * D]), sb("b3h", [3, 2 * D], F32R), sb("b3l", [3, 2 * D])
        b3 = sb("b3", [3, 2 * D], F32R)
        st6 = sb("st6", [P, G, 6])
        mv = sb("mv", [P, TILES, 2])
        rstd, s2 = sb("rstd", [P, TILES]), sb("s2", [P, TILES])
        lt = sb("lt", [P, 4, TILES])
        mhalf = sb("mhalf", [P, TILES])
        ihi = sb("ihi", [P, TILES], F32R)
        i3 = sb("i3", [P, TILES, 3])
        xn = sb("xn", [P, G, D])
        hl = sb("hl", [P, G, 2, DC, P], F32R)
        xt_all = sb("xt_all", [P, TILES, 2, DC, P], F32R)
        ib, ib_all = sb("ib", [3, G, P], F32R), sb("ib_all", [3, TILES, P], F32R)
        kv = sb("kv", [P, 2, 2 * D])
        junk = sb("junk", [P, 2, D])
        junk2 = junk
        nrm = sb("nrm", [P, G, 2])
        wtok, wprod = sb("wtok", [P, G]), sb("wprod", [P, G])
        ph = sb("ph", [P, G, D + ROT])
        rot = sb("rot", [P, 2, ROT])
        acc = sb("acc", [P, BATCH, D + ROT])
        one_col = sb("one_col", [P, 1])
        ab = sb("ab", [1, BATCH, D + ROT])
        aq, af, arow = sb("aq", [1, BATCH, HALF]), sb("af", [1, BATCH, HALF]), sb("arow", [1, BATCH, D])
        acol = sb("acol", [P, BATCH * DC])
        aw = sb("aw", [P, BATCH, DC, D])
        bq3 = sb("bq3", [P, DC, 3])
        m_s = wkv_s[:, :, :, :].rearrange("p b h (c n) -> p b c h n", n=D)
        c3f, c3h, c3l, c3 = (r[:, :].rearrange("k (b n) -> k b n", b=BATCH) for r in (b3f, b3h, b3l, b3))
        lg = sb("lg", [P, TILES, E])
        sc = sb("sc", [P, G, E])
        mx, ix = sb("mx", [P, G, 8]), sb("ix", [P, G, 8], U32)
        top1, ixf = sb("top1", [P, TILES]), sb("ixf", [P, TILES, TOP], F16)
        eq = sb("eq", [P, TILES, E, TOP], F16)
        ex, em = sb("ex", [P, TILES, E]), sb("em", [P, TILES, E])
        mask16 = sb("mask16", [P, TILES, E], F16)
        tri16, one16, exp16 = sb("tri16", [P, P], F16), sb("one16", [P, P], F16), sb("exp16", [P, E], F16)
        zsum, esum, einv = sb("zsum", [P, TILES]), sb("esum", [P, TILES]), sb("einv", [P, TILES])
        wd = sb("wd", [P, TILES, E])
        rank = sb("rank", [P, TILES, E])
        rank_i = sb("rank_i", [P, TILES, E], I32)
        ra_i, rb_i = sb("ra_i", [P, TILES, E], I32), sb("rb_i", [P, TILES, E], I32)
        ra, rb = sb("ra", [P, TILES, E], F16), sb("rb", [P, TILES, E], F16)
        iota_b, iota_k = sb("iota_b", [P, SLOT_B, E], F16), sb("iota_k", [P, E, TOP], F16)
        tok16 = sb("tok16", [P, TILES], F16)
        onehots = x_all[:, :, :].rearrange("p t d -> p (t d)").bitcast(F16)
        n_a, n_b = TILES * E * SLOT_A, TILES * E * SLOT_B
        oa = onehots[:, 0:n_a].rearrange("p (t a e) -> p t a e", t=TILES, e=E)
        oat = onehots[:, n_a:2 * n_a].rearrange("p (t a e) -> p t a e", t=TILES, e=E)
        ob = onehots[:, 2 * n_a:2 * n_a + n_b].rearrange("p (t b e) -> p t b e", t=TILES, e=E)
        diag, tb = sb("diag", [P, SLOT_B, E]), sb("tb", [P, SLOT_B])
        spread = sb("spread", [P, SLOT_A, SLOT_B], F16)
        slot_v, slot_e, slot_f = sb("slot_v", [P, E]), sb("slot_e", [P, E]), sb("slot_f", [P, E])
        idx = sb("idx", [P, E], I32)
        zero = sb("zero", [P, ROW])
        wgu = sb("wgu", [P, G, DC, GU])
        wdn = trg[:, :, :].rearrange("p (j c) n -> p j c n", c=2)
        idx_g, idx_s = sb("idx_g", [P, G], I32), sb("idx_s", [P, G], I32)
        xg = sb("xg", [P, G, ROW])
        sw_flat = wgu[:, :, :, :].rearrange("p j c n -> p (j c n)")
        swg = sw_flat[:, 0:DC * IS].rearrange("p (c n) -> p c n", c=DC)
        swu = sw_flat[:, DC * IS:2 * DC * IS].rearrange("p (c n) -> p c n", c=DC)
        swd = sw_flat[:, 2 * DC * IS:2 * DC * IS + 3 * D].rearrange("p (c n) -> p c n", c=3)
        ph_flat = ph[:, :, :].rearrange("p j n -> p (j n)")
        xgt = ph_flat[:, 0:2 * DC * P].rearrange("p (k c n) -> p k c n", k=2, c=DC)
        sil = ph_flat[:, 2 * DC * P:4 * DC * P].rearrange("p (k c n) -> p k c n", k=2, c=2)
        mid = junk2[:, :, :].rearrange("p k (c n) -> p k c n", c=2)
        eo = kv[:, :, :].rearrange("p k (j n) -> p (k j) n", n=D)
        sg, smid = sb("sg", [P, 2, G * P]), sb("smid", [P, 2, G * P])
        yin = [b[:, :, :].rearrange("p k (j n) -> p (k j) n", n=D) for b in (sg, smid)]
        smid_s = sb("smid_s", [P, 3, 2, G * P], F32R)

        bank = [ctx.enter_context(nc.psum_tensor(f"bank{i}", [P, 512], F32)) for i in range(8)]

        def f(ap):
            return ap.bitcast(F32)

        x_in = sems("x_in", GROUPS)
        ib_in = sems("ib_in", 2)
        pool_passed, dve_passed, sp_passed = sem("pool_passed"), sem("dve_passed"), sem("sp_passed")
        cst_in, wi_in, trg_in, mix_in, sw_in = (sem(n) for n in ("cst_in", "wi_in", "trg_in", "mix_in", "sw_in"))
        ew_in = sems("ew_in", G)
        ones_set, prep_chain, prep_done, act_prep = sem("ones_set"), sem("prep_chain"), sem("prep_done"), sem("act_prep")
        pool_prep, a_pool, pe_prep = sem("pool_prep"), sem("a_pool"), sem("pe_prep")
        v2_chain, v2_ready, s2_ready, i3_chain = sem("v2_chain"), sem("v2_ready"), sem("s2_ready"), sem("i3_chain")
        st_chain, stats_done, ln_ready, i3_ready, norm_done = (sem(n) for n in ("st_chain", "stats_done", "ln_ready", "i3_ready", "norm_done"))
        xn_saved, xt_saved = sems("xn_saved", 2), sems("xt_saved", 2)
        x_saved = sem("x_saved")
        t_done, hi_done, lo_done = sem("t_done"), sem("hi_done"), sem("lo_done")
        ibt_done, ib_done, kv_done, router_done = sem("ibt_done"), sem("ib_done"), sem("kv_done"), sem("router_done")
        v_done, sq_done, prod_done, rot_done, tab_done = sem("v_done"), sem("sq_done"), sem("prod_done"), sem("rot_done"), sem("tab_done")
        w_ready, w_chain, acc_zero, acc_done_t, red_done = sem("w_ready"), sem("w_chain"), sem("acc_zero"), sem("acc_done_t"), sem("red_done")
        rt_read = sem("rt_read")
        sc_read = sem("sc_read")
        ab_done, arow_done, acol_done, acol_read, aw_done = (sem(n) for n in ("ab_done", "arow_done", "acol_done", "acol_read", "aw_done"))
        m_done, m_hi, m_lo, c_done, c3_done, mix_pe = (sem(n) for n in ("m_done", "m_hi", "m_lo", "c_done", "c3_done", "mix_pe"))
        r_chain, lm_done, exp_done, wd_done, wd_saved = (sem(n) for n in ("r_chain", "lm_done", "exp_done", "wd_done", "wd_saved"))
        mask_done, rank_done, onehot_done, oa_done, table_done, spread_done, slot_done, idx_done = (
            sem(n) for n in ("mask_done", "rank_done", "onehot_done", "oa_done", "table_done", "spread_done", "slot_done", "idx_done"))
        zero_set, pads_saved = sem("zero_set"), sem("pads_saved")
        rows_ready = sem("rows_ready")
        idx_copied = sem("idx_copied")
        gath, scat_done = sems("gath", G), sem("scat_done")
        xt_e, xgt_done, gu_done, silu_done, mid_done, d_done, eo_done = (
            sem(n) for n in ("xt_e", "xgt_done", "gu_done", "silu_done", "mid_done", "d_done", "eo_done"))
        c3_chain = sem("c3_chain")
        sw_hi, sw_lo, const_done = sem("sw_hi"), sem("sw_lo"), sem("const_done")
        xn_in, y_in, out_sent = sem("xn_in"), sems("y_in", 2), sems("out_sent", 2)
        sh_done, sg_done, sm_done, hi_m, lo_m, dn_done, kept = (
            sem(n) for n in ("sh_done", "sg_done", "sm_done", "hi_m", "lo_m", "dn_done", "kept"))
        att_done, half_done, ot_pool, ot_dve = sem("att_done"), sem("half_done"), sem("ot_pool"), sem("ot_dve")

        x_v = x.rearrange("b (t p) d -> p (b t) d", p=P)
        out_v = out.rearrange("b (t p) d -> p (b t) d", p=P)
        rows_v = rows.rearrange("(t p) d -> p t d", p=P)
        ysum_v = ysum.rearrange("(t p) d -> p t d", p=P)

        block = ctx.enter_context(nc.Block())

        def mm3(dst, lt_hi, lt_lo, r_hi, r_lo, start, stop):
            nc.tensor.matmul(dst, lt_hi, r_hi, start=start, stop=False)
            nc.tensor.matmul(dst, lt_hi, r_lo, start=False, stop=False)
            return nc.tensor.matmul(dst, lt_lo, r_hi, start=False, stop=stop)

        @block.sync
        def _(sp):
            def load_expert(e, j):
                sp.dma_start(wgu[:, j, :, :], w_gu[e, :, :].rearrange("(c p) n -> p c n", p=P)).then_inc(ew_in[j], 16)
                sp.dma_start(wdn[:, j, 0, :], w_dn[e, 0:P, :]).then_inc(ew_in[j], 16)
                sp.dma_start(wdn[0:I2, j, 1, :], w_dn[e, P:I, :]).then_inc(ew_in[j], 16)

            def load_x(g):
                sp.dma_start(x_all[:, g * G:(g + 1) * G, :], x_v[:, g * G:(g + 1) * G, :]).then_inc(x_in[g], 16)

            load_x(0)
            sp.dma_start(wi[:, :, :], w_in.rearrange("(c p) n -> p c n", p=P)).then_inc(wi_in, 16)
            for g in range(1, GROUPS):
                load_x(g)
            sp.dma_start(trg[:, :, :], trig.rearrange("(t p) c -> p t c", p=P)).then_inc(trg_in, 16)
            sp.dma_start(swg[:, :, :], sw_g.rearrange("(c p) n -> p c n", p=P)).then_inc(sw_in, 16)
            sp.dma_start(swu[:, :, :], sw_u.rearrange("(c p) n -> p c n", p=P)).then_inc(sw_in, 16)
            sp.dma_start(swd[:, 0:2, :], sw_d[0:2 * P, :].rearrange("(c p) n -> p c n", p=P)).then_inc(sw_in, 16)
            sp.dma_start(swd[0:SC[2], 2, :], sw_d[2 * P:IS, :]).then_inc(sw_in, 16)

            def save_xn(t, q):
                sp.wait_ge(norm_done, t + 2)
                sp.dma_start(rows_v[:, bass.ds(t, 2), 0:D], xn[:, 2 * q:2 * q + 2, :]).then_inc(xn_saved[q], 16)

            def save_xt(t, q):
                sp.wait_ge(lo_done, t + 2)
                sp.dma_start(f(xt_all[:, bass.ds(t, 2), :, :, :]).rearrange("p a h c n -> p (a h c n)"),
                             f(hl[:, 2 * q:2 * q + 2, :, :, :]).rearrange("p a h c n -> p (a h c n)")).then_inc(xt_saved[q], 16)

            def load_ib(t, q):
                sp.dma_start(f(ib[:, 2 * q:2 * q + 2, :]), f(ib_all[:, bass.ds(t, 2), :])).then_inc(ib_in[q], 16)

            save_xn(0, 0)
            save_xn(2, 1)
            sp.wait_ge(ib_done, 1)
            load_ib(0, 0)
            load_ib(2, 1)
            save_xt(0, 0)
            with sp.Fori(0, GROUPS - 1) as h:
                for q in range(2):
                    save_xn(h * G + 2 * q + G, q)
                    save_xt(h * G + 2 * q + 2, 1 - q)
                    sp.wait_ge(kv_done, h * G + 2 * q + 2)
                    if q == 0:
                        sp.sem_inc(sp_passed, 1)
                        sp.wait_ge(ib_done, h + 2)
                    load_ib(h * G + 2 * q + G, q)
            save_xt(TILES - 2, 1)
            sp.dma_start(ysum_v[:, 0:TILES, :], x_all[:, :, :]).then_inc(x_saved, 16)
            sp.dma_start(wqt[:, :, :], wq_t.rearrange("(c p) n -> p c n", p=P)).then_inc(mix_in, 16)
            sp.dma_start(wo[:, :, :], w_out.rearrange("(c p) n -> p c n", p=P)).then_inc(mix_in, 16)
            sp.wait_ge(zero_set, 1)
            sp.dma_start(rows[TOKENS:TOKENS + CAP, :], zero[:, :]).then_inc(pads_saved, 16)
            sp.dma_start(ysum[TOKENS:TOKENS + CAP, :], zero[:, 0:D]).then_inc(pads_saved, 16)
            for q in range(2):
                sp.wait_ge(xn_saved[q], 16 * TILES // 4)

            def load_xn(g):
                sp.dma_start(xn[:, :, :], rows_v[:, bass.ds(g * G, G), 0:D]).then_inc(xn_in, 16)

            load_xn(0)
            sp.wait_ge(tab_done, TILES)
            sp.wait_ge(sw_lo, 4)
            for j in range(G):
                load_expert(j, j)
            sp.wait_ge(wd_done, 1)
            sp.dma_start(rows_v[:, 0:TILES, D:ROW], wd[:, :, :]).then_inc(wd_saved, 16)
            sp.wait_ge(x_saved, 16)
            sp.wait_ge(pads_saved, 32)
            sp.wait_ge(wd_saved, 16)
            sp.sem_inc(rows_ready, 1)
            with sp.Fori(0, E // G - 1) as h:
                for j in range(G):
                    if j == 3:
                        sp.wait_ge(kept, 2 * h + 2)
                        load_xn(h + 1)
                    sp.wait_ge(gu_done, h * G + j + 1)
                    sp.wait_ge(d_done, h * G + j + 1)
                    load_expert(h * G + G + j, j)

            def load_y(g, k):
                sp.dma_start(yin[k][:, :, :], ysum_v[:, bass.ds(g * G, G), :]).then_inc(y_in[k], 16)

            def send(g, k):
                sp.wait_ge(ot_pool, 2 * g + 2)
                sp.wait_ge(ot_dve, 2 * g + 2)
                sp.dma_start(out_v[:, bass.ds(g * G, G), :], sh[:, bass.ds(g * G, G), :]).then_inc(out_sent[k], 16)

            sp.wait_ge(lo_m, 3 * GROUPS)
            sp.wait_ge(scat_done, 16 * E)
            load_y(0, 0)
            load_y(1, 1)
            send(0, 0)
            load_y(2, 0)
            send(1, 1)
            load_y(3, 1)
            for g in (2, 3):
                sp.wait_ge(out_sent[g % 2], 16)
                send(g, g % 2)
            for k in range(2):
                sp.wait_ge(out_sent[k], 32)
            for q in range(2):
                sp.wait_ge(xt_saved[q], 16 * TILES // 4)

        @block.gpsimd
        def _(pool):
            pool.memset(mhalf[:, :], -0.5).then_inc(pool_prep, 1)
            pool.memset(zero[:, :], 0.0).then_inc(zero_set, 1)
            pool.wait_ge(pool_prep, 1)

            def await_ge(signal, count):
                pool.wait_ge(signal, count)
                if not isinstance(count, int):
                    pool.sem_inc(pool_passed, 1)

            def rstd_of(k, a, b):
                pool.wait_ge(stats_done, b // G)
                nc.gpsimd.tensor_tensor(rstd[:, a:b], lt[:, 0, a:b], mhalf[:, 0:b - a], ALU.pow).then_inc(ln_ready, 1)

            def s2_of(k, a, b):
                pool.wait_ge(v2_ready, k)
                nc.gpsimd.tensor_tensor(s2[:, a:b], lt[:, 3, a:b], mhalf[:, 0:b - a], ALU.pow).then_inc(s2_ready, 1)

            def rotate(g, j, half, first):
                t = g * G + j
                if not (first and j == 0):
                    await_ge(tab_done, t)
                await_ge(prod_done, 2 * t + 2)
                pxy = ph[:, j, :].rearrange("p (a n) -> p a n", n=ROT)[:, 0:3:2, :]
                nc.gpsimd.tensor_tensor(rot[:, :, :], pxy, trg[:, bass.ds(half * G + j, 1), :].rearrange("p o (a n) -> p (o a) n", a=2),
                                        ALU.mult).then_inc(rot_done, 1)
                await_ge(sq_done, 2 * t + 2)
                nc.gpsimd.tensor_tensor(wprod[:, j:j + 1], nrm[:, j, 0:1], nrm[:, j, 1:2], ALU.mult).then_inc(w_chain, 1)
                await_ge(rot_done, t + 1)
                nc.gpsimd.tensor_tensor(ph[:, j, D:D + ROT], rot[:, 0, :], rot[:, 1, :], ALU.add).then_inc(tab_done, 1)
                await_ge(w_chain, t + 1)
                if not first:
                    await_ge(acc_done_t, t - G + 1)
                nc.gpsimd.tensor_tensor(wtok[:, j:j + 1], wprod[:, j:j + 1], mhalf[:, 0:1], ALU.pow).then_inc(w_ready, 1)

            rstd_of(1, 0, G)
            s2_of(1, 0, G)
            rstd_of(2, G, 2 * G)
            s2_of(2, G, 2 * G)
            pool.wait_ge(trg_in, 16)
            rotate(0, 0, 0, True)
            rstd_of(3, 2 * G, TILES)
            rotate(0, 1, 0, True)
            s2_of(3, 2 * G, TILES)
            rotate(0, 2, 0, True)
            rotate(0, 3, 0, True)
            with pool.Fori(1, GROUPS) as g:
                for j in range(G):
                    rotate(g, j, g & (GROUPS_B - 1), False)

            pool.wait_ge(sw_hi, 4)
            nc.gpsimd.tensor_tensor(swg_s[:, :, 1, :], swg[:, :, :], f(swg_s[:, :, 0, :]), ALU.subtract).then_inc(sw_lo, 1)
            nc.gpsimd.tensor_tensor(swu_s[:, :, 1, :], swu[:, :, :], f(swu_s[:, :, 0, :]), ALU.subtract).then_inc(sw_lo, 1)
            def a_link(ins, n):
                ins.then_inc(a_pool, 1)
                pool.wait_ge(a_pool, n)

            pool.wait_ge(ab_done, BATCH)
            a_link(nc.gpsimd.tensor_tensor(aq[:, :, :], ab[:, :, 0:HALF], ab[:, :, HALF:ROT], ALU.add), 1)
            a_link(nc.gpsimd.tensor_tensor(af[:, :, :], ab[:, :, D:D + HALF], ab[:, :, D + HALF:D + ROT], ALU.add), 2)
            a_link(nc.gpsimd.tensor_scalar(aq[:, :, :], aq[:, :, :], 0.25, 0.5, ALU.mult, ALU.add), 3)
            nc.gpsimd.tensor_scalar(arow[:, :, ROT:D], ab[:, :, ROT:D], 0.5, 0.5, ALU.mult, ALU.add).then_inc(arow_done, 1)
            nc.gpsimd.tensor_tensor(arow[:, :, 0:HALF], aq[:, :, :], af[:, :, :], ALU.add).then_inc(arow_done, 1)
            nc.gpsimd.tensor_tensor(arow[:, :, HALF:ROT], aq[:, :, :], af[:, :, :], ALU.subtract).then_inc(arow_done, 1)
            nc.gpsimd.tensor_tensor(swd_s[:, 0:2, 1, :], swd[:, 0:2, :], f(swd_s[:, 0:2, 0, :]), ALU.subtract).then_inc(sw_lo, 1)
            nc.gpsimd.tensor_tensor(swd_s[0:SC[2], 2, 1, :], swd[0:SC[2], 2, :], f(swd_s[0:SC[2], 2, 0, :]), ALU.subtract).then_inc(sw_lo, 1)

            await_ge(onehot_done, 1)
            nc.gpsimd.tensor_tensor(oat[:, :, :, :].rearrange("p t a e -> p t (a e)"), oa[:, :, :, :].rearrange("p t a e -> p t (a e)"),
                                    tok16[:, :].unsqueeze(2).to_broadcast([P, TILES, E * SLOT_A]),
                                    ALU.mult).then_inc(oa_done, 1)

            def gather(e, j, first):
                nc.gpsimd.tensor_copy(idx_g[:, j:j + 1], idx[:, bass.ds(e, 1)]).then_inc(idx_copied, 1)
                await_ge(idx_copied, e + 1 if first else 2 * e - 3)
                nc.gpsimd.indirect_dma_start(out=xg[:, j, :], out_offset=None, in_=rows,
                                             in_offset=bass.IndirectOffsetOnAxis(ap=idx_g[:, j:j + 1], axis=0)).then_inc(gath[j], 16)

            def scatter(e, j, last):
                if not (isinstance(e, int) and e == 0):
                    await_ge(scat_done, 16 * e)
                nc.gpsimd.tensor_copy(idx_s[:, j:j + 1], idx[:, bass.ds(e, 1)]).then_inc(idx_copied, 1)
                await_ge(idx_copied, (E + 1 + e) if last else (2 * e + G + 2))
                nc.gpsimd.indirect_dma_start(out=ysum, out_offset=bass.IndirectOffsetOnAxis(ap=idx_s[:, j:j + 1], axis=0),
                                             in_=eo[:, j, :], in_offset=None, compute_op=ALU.add).then_inc(scat_done, 16)

            await_ge(idx_done, 1)
            await_ge(rows_ready, 1)
            for j in range(G):
                gather(j, j, True)

            def moe_body(h, last=False):
                for j in range(G):
                    e = h * G + j
                    await_ge(eo_done, e + 1)
                    if not last:
                        gather(e + G, j, False)
                    scatter(e, j, last)

            moe_body(0)
            with pool.Fori(1, E // G - 1) as h:
                moe_body(h)
            moe_body(E // G - 1, last=True)

            for g in range(GROUPS):
                pool.wait_ge(y_in[g % 2], 16 * (g // 2 + 1))
                for j in range(0, G, 2):
                    t = g * G + j
                    pool.wait_ge(half_done, t + 2)
                    nc.gpsimd.tensor_tensor(sh[:, t, :], sh[:, t, :], yin[g % 2][:, j, :], ALU.add).then_inc(ot_pool, 1)

        @block.scalar
        def _(act):
            act.dma_start(cst[:, :], consts).then_inc(cst_in, 16)
            act.dma_start(gb_cols[:, :], gb).then_inc(wi_in, 16)
            act.dma_start(bias_row[:, :], bias).then_inc(wi_in, 16)
            act.wait_ge(wi_in, 48)
            for c in range(DC):
                nc.scalar.activation(wkv_s[:, c, 0, :], wi[:, c, D:3 * D], ACT.Copy, scale=gam[:, c:c + 1]).then_inc(act_prep, 1)
            nc.scalar.activation(gt_s[:, :, 0, :], gt[:, :, :], ACT.Copy).then_inc(act_prep, 1)

            def hi(g, j, first):
                t = g * G + j
                if not first:
                    act.wait_ge(kv_done, t - G + 1)
                    act.wait_ge(router_done, 2 * g + (j // 2) - 1)
                    act.wait_ge(xt_saved[j // 2], g * 16)
                act.wait_ge(t_done, t + 1)
                nc.scalar.activation(hl[:, j, 0, :, :], bank[4 + j % 2][:, 0:D].rearrange("p (c n) -> p c n", c=DC),
                                     ACT.Copy).then_inc(hi_done, 1)

            def ones_rows(g):
                act.wait_ge(ibt_done, g + 1)
                nc.scalar.activation(ib_all[:, g * G:(g + 1) * G, :], bank[2 + g % 2][0:3, :].rearrange("p (j n) -> p j n", j=G), ACT.Copy).then_inc(ib_done, 1)

            def values(g, j, first):
                t = g * G + j
                if not (first and j < 2):
                    act.wait_ge(prod_done, 2 * (t - 2) + 2)
                act.wait_ge(kv_done, t + 1)
                nc.scalar.activation(kv[:, j % 2, :], bank[j % 2][:, :], ACT.Copy).then_inc(v_done, 1)
                if not first:
                    act.wait_ge(w_chain, t - G + 1)
                if not (first and j == 0):
                    act.wait_ge(sq_done, 2 * t)
                nc.scalar.activation(junk[:, 0, :], bank[j % 2][:, 0:D], ACT.Square, accum_out=nrm[:, j, 0:1]).then_inc(sq_done, 1)
                nc.scalar.activation(junk[:, 1, :], bank[j % 2][:, D:2 * D], ACT.Square, accum_out=nrm[:, j, 1:2]).then_inc(sq_done, 1)

            def body(g, first=False, last=False):
                for j in range(G):
                    if j < 2:
                        hi(g, j + 2, first)
                    elif not last:
                        hi(g + 1, j - 2, False)
                    if first and j == 0:
                        ones_rows(0)
                    if first and j == 3:
                        ones_rows(1)
                    values(g, j, first)
                    if first and j == 3:
                        ones_rows(2)
                        ones_rows(3)
                    if last:
                        if j == 0:
                            act.wait_ge(sw_in, 64)
                        w_s, w, n, c = ((swg_s, swg, P, slice(0, 2)), (swu_s, swu, P, slice(0, 2)), (swd_s, swd, P, slice(0, 2)),
                                        (swd_s, swd, SC[2], slice(2, 3)))[j]
                        nc.scalar.activation(w_s[0:n, c, 0, :], w[0:n, c, :], ACT.Copy).then_inc(sw_hi, 1)

            hi(0, 0, True)
            hi(0, 1, True)
            act.wait_ge(pe_prep, 1)
            nc.scalar.activation(b3f[:, :], bank[3][0:3, :], ACT.Copy).then_inc(act_prep, 1)
            act.wait_ge(act_prep, 4)
            nc.scalar.activation(b3h[:, :], b3f[:, :], ACT.Copy).then_inc(act_prep, 1)
            body(0, first=True)
            with act.Fori(1, GROUPS - 1) as g:
                body(g)
            body(GROUPS - 1, last=True)

            def shared(g, c, pair):
                n, k, q = SC[c], c % 2, g * 3 + c
                if not (isinstance(g, int) and q < 2):
                    act.wait_ge(sm_done, q - 1 if c else q)
                act.wait_ge(sh_done, q + 1)
                nc.scalar.activation(sg[0:n, k, :], bank[pair][0:n, :], ACT.Silu).then_inc(sg_done, 1)
                act.wait_ge(sm_done, q + 1)
                if not (isinstance(g, int) and g == 0):
                    act.wait_ge(dn_done, 2 * g)
                nc.scalar.activation(smid_s[0:n, c, 0, :], smid[0:n, k, :], ACT.Copy).then_inc(hi_m, 1)

            act.wait_ge(red_done, 1)
            for b in range(BATCH):
                nc.scalar.activation(ab[:, b, :], bank[2 + b][0:1, 0:D + ROT], ACT.Copy).then_inc(ab_done, 1)
            act.wait_ge(lm_done, 1)
            nc.scalar.activation(ex[:, :, :], ex[:, :, :], ACT.Exp).then_inc(exp_done, 1)
            for c in range(3):
                shared(0, c, GAP_PAIR[c])
            for b in range(BATCH):
                for c in range(DC):
                    act.wait_ge(m_done, b * DC + c + 1)
                    nc.scalar.activation(m_s[:, b, c, 0, :], bank[2 + b * DC + c][:, 0:D], ACT.Copy, scale=gam[:, c:c + 1]).then_inc(m_hi, 1)

            def evac(e, k):
                if not (isinstance(e, int) and e < 2):
                    act.wait_ge(gu_done, e - 1)
                act.wait_ge(xt_e, e + 1)
                nc.scalar.activation(xgt[:, k, :, :], bank[4 + k][:, 0:D].rearrange("p (c n) -> p c n", c=DC),
                                     ACT.Copy).then_inc(xgt_done, 1)

            def silu(e, k):
                if not (isinstance(e, int) and e < 2):
                    act.wait_ge(mid_done, 2 * (e - 1))
                act.wait_ge(gu_done, e + 1)
                nc.scalar.activation(sil[:, k, 0, :], bank[k][:, 0:P], ACT.Silu).then_inc(silu_done, 1)
                nc.scalar.activation(sil[0:I2, k, 1, :], bank[k][0:I2, 2 * P:3 * P], ACT.Silu).then_inc(silu_done, 1)

            def moe_body(h, first=False, last=False):
                for j in range(G):
                    e = h * G + j
                    if not (last and j == G - 1):
                        evac(e + 1, (j + 1) % 2)
                    silu(e, j % 2)
                    if not first and j < 3:
                        shared(h, j, 6)

            act.wait_ge(c_done, 1)
            nc.scalar.activation(c3f[:, :, :], bank[7][0:3, :].rearrange("p (b n) -> p b n", b=BATCH), ACT.Copy).then_inc(c3_chain, 1)
            act.wait_ge(c3_chain, 1)
            nc.scalar.activation(c3h[:, :, :], c3f[:, :, :], ACT.Copy).then_inc(c3_chain, 1)

            evac(0, 0)
            moe_body(0, first=True)
            with act.Fori(1, E // G - 1) as h:
                moe_body(h)
            moe_body(E // G - 1, last=True)

        @block.vector
        def _(dve):
            def stats(g):
                dve.wait_ge(x_in[g], 16)
                if g > 0:
                    dve.wait_ge(st_chain, g * 8)
                for j in range(G):
                    nc.vector.bn_stats(st6[:, j, :], x_all[:, g * G + j, :]).then_inc(st_chain, 1)
                dve.wait_ge(st_chain, g * 8 + G)
                for j in range(G):
                    nc.vector.bn_aggr(mv[:, g * G + j, :], st6[:, j, :]).then_inc(st_chain, 1)
                dve.wait_ge(st_chain, g * 8 + 8)
                nc.vector.tensor_scalar(lt[:, 0, g * G:(g + 1) * G], mv[:, g * G:(g + 1) * G, 1], EPS, None, ALU.add).then_inc(stats_done, 1)

            def second_var(k, a, b):
                dve.wait_ge(ln_ready, k)
                nc.vector.tensor_tensor(lt[:, 1, a:b], rstd[:, a:b], rstd[:, a:b], ALU.mult).then_inc(v2_chain, 1)
                dve.wait_ge(v2_chain, 2 * k - 1)
                nc.vector.tensor_tensor(lt[:, 2, a:b], lt[:, 1, a:b], mv[:, a:b, 1], ALU.mult).then_inc(v2_chain, 1)
                dve.wait_ge(v2_chain, 2 * k)
                nc.vector.tensor_scalar(lt[:, 3, a:b], lt[:, 2, a:b], EPS, None, ALU.add).then_inc(v2_ready, 1)

            def inverse(k, a, b):
                dve.wait_ge(s2_ready, k)
                nc.vector.tensor_tensor(lt[:, 0, a:b], lt[:, 3, a:b], s2[:, a:b], ALU.mult).then_inc(i3_chain, 1)
                dve.wait_ge(i3_chain, 2 * k - 1)
                nc.vector.tensor_copy(ihi[:, a:b], lt[:, 0, a:b]).then_inc(i3_chain, 1)
                dve.wait_ge(i3_chain, 2 * k)
                nc.vector.tensor_copy(i3[:, a:b, 0:2], f(ihi[:, a:b]).unsqueeze(2).to_broadcast([P, b - a, 2])).then_inc(i3_ready, 1)
                nc.vector.tensor_tensor(i3[:, a:b, 2], lt[:, 0, a:b], f(ihi[:, a:b]), ALU.subtract).then_inc(i3_ready, 1)

            def norm(g, j, first):
                t = g * G + j
                dve.wait_ge(ln_ready, 1 if first else 2 if isinstance(g, int) and g == 1 else 3)
                if not first:
                    dve.wait_ge(t_done, t - G + 1)
                    dve.wait_ge(xn_saved[j // 2], g * 16)
                nc.vector.tensor_scalar(xn[:, j, :], x_all[:, t, :], mv[:, bass.ds(t, 1), 0], rstd[:, bass.ds(t, 1)],
                                        ALU.subtract, ALU.mult).then_inc(norm_done, 1)

            def lo(g, j, first):
                t = g * G + j
                dve.wait_ge(hi_done, t + 1)
                nc.vector.tensor_tensor(hl[:, j, 1, :, :], bank[4 + j % 2][:, 0:D].rearrange("p (c n) -> p c n", c=DC),
                                        f(hl[:, j, 0, :, :]), ALU.subtract).then_inc(lo_done, 1)

            def products(g, j, first):
                t = g * G + j
                if not first:
                    dve.wait_ge(acc_done_t, t - G + 1)
                dve.wait_ge(v_done, t + 1)
                k_, v_ = kv[:, j % 2, 0:D], kv[:, j % 2, D:2 * D]
                v2 = v_[:, 0:ROT].rearrange("p (a n) -> p a n", a=2)[:, ::-1, :]
                nc.vector.tensor_tensor(ph[:, j, D:D + ROT].rearrange("p (a n) -> p a n", a=2),
                                        k_[:, 0:ROT].rearrange("p (a n) -> p a n", a=2), v2, ALU.mult).then_inc(prod_done, 1)
                nc.vector.tensor_tensor(ph[:, j, 0:D], k_, v_, ALU.mult).then_inc(prod_done, 1)

            def accumulate(g, j, b, first):
                t = g * G + j
                dve.wait_ge(acc_done_t, t) if not (first and j == 0) else dve.wait_ge(acc_zero, 1)
                dve.wait_ge(tab_done, t + 1)
                dve.wait_ge(w_ready, t + 1)
                nc.vector.scalar_tensor_tensor(acc[:, b, :], ph[:, j, :], wtok[:, j:j + 1], acc[:, b, :], ALU.mult, ALU.add).then_inc(acc_done_t, 1)

            def scores_read(g, q, first):
                if not first:
                    dve.wait_ge(rt_read, g * 11)
                dve.wait_ge(router_done, 2 * g + q + 1)
                nc.vector.tensor_copy(sc[:, 2 * q:2 * q + 2, :], bank[6 + q][:, 0:2 * E].rearrange("p (j e) -> p j e", j=2)).then_inc(sc_read, 1)

            def largest(g):
                s = sc[:, :, :]
                dve.wait_ge(sc_read, 2 * g + 2)
                nc.vector.tensor_scalar(lg[:, bass.ds(g * G, G), :], s, 0.0, None, ALU.add).then_inc(rt_read, 1)
                for j in range(G):
                    nc.vector.max(mx[:, j, :], s[:, j, :]).then_inc(rt_read, 1)

            def places(g):
                s = sc[:, :, :]
                dve.wait_ge(rt_read, g * 11 + 5)
                nc.vector.tensor_scalar(top1[:, bass.ds(g * G, G)], mx[:, :, 0], 0.0, None, ALU.add).then_inc(rt_read, 1)
                for j in range(G):
                    nc.vector.max_index(ix[:, j, :], mx[:, j, :], s[:, j, :]).then_inc(rt_read, 1)
                dve.wait_ge(rt_read, g * 11 + 10)
                nc.vector.tensor_scalar(ixf[:, bass.ds(g * G, G), :], ix[:, :, 0:TOP], 0.0, None, ALU.add).then_inc(rt_read, 1)

            def body(g, first=False, second=False, last=False):
                batch = (lambda k: k // GROUPS_B) if isinstance(g, int) else (lambda k: bass.ds((k >> 1) & 1, 1))
                for j in range(G):
                    if j < 2:
                        lo(g, j + 2, first)
                    elif not last:
                        lo(g + 1, j - 2, False)
                    products(g, j, first)
                    if not last:
                        norm(g + 1, j, False)
                    if j < 2 and not first:
                        accumulate(g - 1, j + 2, batch(g - 1), second)
                    if j >= 2:
                        accumulate(g, j - 2, batch(g), first)
                    if j == 0 and not first:
                        scores_read(g - 1, 1, second)
                        largest(g - 1)
                    if j == 1 and not first:
                        places(g - 1)
                    if j == 2:
                        scores_read(g, 0, first)
                    if first and j == 0:
                        stats(3)
                    if first and j == 1:
                        second_var(3, 2 * G, TILES)
                    if first and j == 2:
                        inverse(3, 2 * G, TILES)

            stats(0)
            nc.vector.memset(ones3[:, :], 1.0).then_inc(ones_set, 1)
            nc.vector.memset(one16[:, :], 1.0).then_inc(ones_set, 1)
            nc.vector.memset(one_col[:, :], 1.0).then_inc(ones_set, 1)
            nc.vector.memset(acc[:, :, :], 0.0).then_inc(acc_zero, 1)
            dve.wait_ge(wi_in, 48)
            nc.vector.tensor_copy(bet3[:, :, :], bet[:, :].unsqueeze(2).to_broadcast([P, DC, 3])).then_inc(ones_set, 1)
            for j in range(G):
                norm(0, j, True)
            second_var(1, 0, G)
            for c in range(DC):
                dve.wait_ge(act_prep, c + 1)
                nc.vector.scalar_tensor_tensor(wkv_s[:, c, 1, :], wi[:, c, D:3 * D], gam[:, c:c + 1], f(wkv_s[:, c, 0, :]),
                                               ALU.mult, ALU.subtract).then_inc(prep_done, 1)
            inverse(1, 0, G)
            lo(0, 0, True)
            lo(0, 1, True)
            stats(1)
            dve.wait_ge(act_prep, 3)
            nc.vector.tensor_tensor(gt_s[:, :, 1, :], gt[:, :, :], f(gt_s[:, :, 0, :]), ALU.subtract).then_inc(prep_done, 1)
            dve.wait_ge(cst_in, 16)
            nc.vector.tensor_copy(iota_b[:, :, :], cst[:, C_I16:C_I16 + E].unsqueeze(2).to_broadcast([P, SLOT_B, E])).then_inc(const_done, 1)
            nc.vector.tensor_copy(iota_k[:, :, :], cst[:, C_I16:C_I16 + E].unsqueeze(2).to_broadcast([P, E, TOP])).then_inc(const_done, 1)
            nc.vector.tensor_copy(tri16[:, :], cst[:, C_TRI:C_TRI + P]).then_inc(const_done, 1)
            nc.vector.tensor_copy(exp16[:, :], cst[:, C_EXP:C_EXP + E]).then_inc(const_done, 1)
            nc.vector.tensor_copy(tok16[:, :], cst[:, C_TOK:C_TOK + TILES]).then_inc(const_done, 1)
            dve.wait_ge(act_prep, 5)
            nc.vector.tensor_tensor(b3l[:, :], b3f[:, :], f(b3h[:, :]), ALU.subtract).then_inc(prep_chain, 1)
            dve.wait_ge(prep_chain, 1)
            nc.vector.tensor_scalar(b3l[:, :], b3l[:, :], cst[0:3, C_ROW + 1:C_ROW + 2], None, ALU.mult).then_inc(prep_chain, 1)
            dve.wait_ge(prep_chain, 2)
            nc.vector.scalar_tensor_tensor(b3[:, :], f(b3h[:, :]), cst[0:3, C_ROW:C_ROW + 1], b3l[:, :],
                                           ALU.mult, ALU.add).then_inc(prep_done, 1)
            second_var(2, G, 2 * G)
            stats(2)
            inverse(2, G, 2 * G)
            body(0, first=True)
            body(1, second=True)
            with dve.Fori(2, GROUPS - 1) as g:
                body(g)
            body(GROUPS - 1, last=True)
            for j in (2, 3):
                accumulate(GROUPS - 1, j, BATCH - 1, False)
            scores_read(GROUPS - 1, 1, False)
            largest(GROUPS - 1)
            places(GROUPS - 1)

            chain = [0]

            def link(ins):
                chain[0] += 1
                ins.then_inc(r_chain, 1)
                dve.wait_ge(r_chain, chain[0])

            def shared_mid(g, c, pair):
                n, k, q = SC[c], c % 2, g * 3 + c
                if not (isinstance(g, int) and q < 2):
                    dve.wait_ge(lo_m, q - 1 if c else q)
                dve.wait_ge(sg_done, q + 1)
                nc.vector.tensor_tensor(smid[0:n, k, :], sg[0:n, k, :], bank[pair + 1][0:n, :], ALU.mult).then_inc(sm_done, 1)

            def shared_lo(g, c):
                n, k, q = SC[c], c % 2, g * 3 + c
                dve.wait_ge(hi_m, q + 1)
                nc.vector.tensor_tensor(smid_s[0:n, c, 1, :], smid[0:n, k, :], f(smid_s[0:n, c, 0, :]), ALU.subtract).then_inc(lo_m, 1)

            def keep(g, pair):
                dve.wait_ge(xn_in, 16 * g + 16)
                for q in range(2):
                    dve.wait_ge(dn_done, 2 * g + q + 1)
                    nc.vector.tensor_tensor(sh[:, bass.ds(g * G + 2 * q, 2), :], xn[:, 2 * q:2 * q + 2, :],
                                            bank[pair + q][:, :].rearrange("p (j n) -> p j n", j=2), ALU.add).then_inc(kept, 1)

            dve.wait_ge(rt_read, 11 * GROUPS)
            dve.wait_ge(const_done, 5)
            link(nc.vector.tensor_tensor(eq[:, :, :, :], ixf[:, :, :].unsqueeze(2).to_broadcast([P, TILES, E, TOP]),
                                         iota_k[:, :, :].unsqueeze(1).to_broadcast([P, TILES, E, TOP]), ALU.is_equal))
            with nc.allow_low_precision("a sum of four zeros and ones"):
                nc.vector.tensor_reduce(mask16[:, :, :], eq[:, :, :, :], axis=AX.X, op=ALU.add).then_inc(mask_done, 1)
            nc.vector.tensor_tensor(ex[:, :, :], lg[:, :, :], top1[:, :].unsqueeze(2).to_broadcast([P, TILES, E]), ALU.subtract).then_inc(lm_done, 1)

            dve.wait_ge(mask_done, 1)
            dve.wait_ge(rank_done, 1)
            link(nc.vector.scalar_tensor_tensor(rank[:, :, :], mask16[:, :, :], -1024.0, bank[7][:, 0:TILES * E].rearrange("p (t e) -> p t e", t=TILES),
                                                ALU.mult, ALU.add))
            link(nc.vector.tensor_scalar(rank_i[:, :, :], rank[:, :, :], 1024.0, None, ALU.add))
            link(nc.vector.tensor_scalar(ra_i[:, :, :], rank_i[:, :, :], 4, None, ALU.logical_shift_right))
            link(nc.vector.tensor_copy(ra[:, :, :], ra_i[:, :, :]))
            dve.wait_ge(x_saved, 16)
            nc.vector.tensor_tensor(oa[:, :, :, :], ra[:, :, :].unsqueeze(2).to_broadcast([P, TILES, SLOT_A, E]),
                                    iota_b[:, 0:SLOT_A, :].unsqueeze(1).to_broadcast([P, TILES, SLOT_A, E]),
                                    ALU.is_equal).then_inc(onehot_done, 1)
            link(nc.vector.tensor_scalar(rb_i[:, :, :], rank_i[:, :, :], SLOT_B - 1, None, ALU.bitwise_and))
            link(nc.vector.tensor_copy(rb[:, :, :], rb_i[:, :, :]))
            nc.vector.tensor_tensor(ob[:, :, :, :], rb[:, :, :].unsqueeze(2).to_broadcast([P, TILES, SLOT_B, E]),
                                    iota_b[:, :, :].unsqueeze(1).to_broadcast([P, TILES, SLOT_B, E]),
                                    ALU.is_equal).then_inc(onehot_done, 1)
            shared_mid(0, 0, GAP_PAIR[0])
            dve.wait_ge(exp_done, 1)
            link(nc.vector.tensor_reduce(zsum[:, :], ex[:, :, :], axis=AX.X, op=ALU.add))
            link(nc.vector.tensor_tensor(em[:, :, :], ex[:, :, :], mask16[:, :, :], ALU.mult))
            link(nc.vector.tensor_reduce(esum[:, :], em[:, :, :], axis=AX.X, op=ALU.add))
            link(nc.vector.scalar_tensor_tensor(esum[:, :], zsum[:, :], 1e-20, esum[:, :], ALU.mult, ALU.add))
            link(nc.vector.reciprocal(einv[:, :], esum[:, :]))
            nc.vector.tensor_tensor(wd[:, :, :], em[:, :, :], einv[:, :].unsqueeze(2).to_broadcast([P, TILES, E]), ALU.mult).then_inc(wd_done, 1)
            dve.wait_ge(table_done, 1)
            link(nc.vector.tensor_tensor(diag[:, :, :], bank[6][:, 0:E * SLOT_B].rearrange("p (b e) -> p b e", e=E),
                                         cst[:, C_EXP:C_EXP + E].unsqueeze(1).to_broadcast([P, SLOT_B, E]), ALU.mult))
            link(nc.vector.tensor_reduce(tb[:, :], diag[:, :, :], axis=AX.X, op=ALU.add))
            nc.vector.tensor_tensor(spread[:, :, :], tb[:, :].unsqueeze(1).to_broadcast([P, SLOT_A, SLOT_B]),
                                    cst[:, C_ASEL:C_ASEL + SLOT_A].unsqueeze(2).to_broadcast([P, SLOT_A, SLOT_B]), ALU.mult).then_inc(spread_done, 1)
            shared_lo(0, 0)
            dve.wait_ge(slot_done, 1)
            link(nc.vector.tensor_copy(slot_v[:, :], bank[6][:, 256:256 + E]))
            link(nc.vector.tensor_scalar(slot_e[:, :], slot_v[:, :], 0.0, cst[:, C_SPARE:C_SPARE + 1], ALU.is_equal, ALU.mult))
            link(nc.vector.tensor_tensor(slot_f[:, :], slot_v[:, :], slot_e[:, :], ALU.add))
            nc.vector.tensor_scalar(idx[:, :], slot_f[:, :], -1.0, None, ALU.add).then_inc(idx_done, 1)
            dve.wait_ge(acol_done, 1)
            link(nc.vector.tensor_copy(acol[:, :], bank[2][:, 384:384 + BATCH * DC]))
            nc.vector.tensor_copy(bq3[:, :, :], bank[2][:, 392:392 + DC * 3].rearrange("p (c k) -> p c k", c=DC)).then_inc(aw_done, 1)
            dve.wait_ge(mix_in, 32)
            for b in range(BATCH):
                for c in range(DC):
                    nc.vector.tensor_scalar(aw[:, b, c, :], wo[:, c, :], acol[:, b * DC + c:b * DC + c + 1], None, ALU.mult).then_inc(aw_done, 1)
            for c in (1, 2):
                shared_mid(0, c, GAP_PAIR[c])
                shared_lo(0, c)
            for b in range(BATCH):
                for c in range(DC):
                    dve.wait_ge(m_hi, b * DC + c + 1)
                    nc.vector.scalar_tensor_tensor(m_s[:, b, c, 1, :], bank[2 + b * DC + c][:, 0:D], gam[:, c:c + 1], f(m_s[:, b, c, 0, :]),
                                                   ALU.mult, ALU.subtract).then_inc(m_lo, 1)
            keep(0, 0)

            def gated(e, k):
                if not (isinstance(e, int) and e < 2):
                    dve.wait_ge(d_done, e - 1)
                dve.wait_ge(silu_done, 2 * e + 2)
                nc.vector.tensor_tensor(mid[:, k, 0, :], sil[:, k, 0, :], bank[k][:, P:2 * P], ALU.mult).then_inc(mid_done, 1)
                nc.vector.tensor_tensor(mid[0:I2, k, 1, :], sil[0:I2, k, 1, :], bank[k][UP2:UP2 + I2, 2 * P:3 * P], ALU.mult).then_inc(mid_done, 1)

            def weigh(eh, j, first):
                e = eh * G + j
                if not first:
                    dve.wait_ge(scat_done, 16 * (e - G + 1))
                dve.wait_ge(d_done, e + 1)
                nc.vector.tensor_scalar(eo[:, j, :], bank[2 + j % 2][:, 0:D], xg[:, j, bass.ds(D + e, 1)], None, ALU.mult).then_inc(eo_done, 1)

            def moe_body(h, first=False, second=False):
                for j in range(G):
                    e = h * G + j
                    early = first or (second and j == 0)
                    gated(e, j % 2)
                    if not (first and j == 0):
                        weigh(h + (j - 1) // G, (j - 1) % G, early)
                    if not first:
                        if j < 3:
                            shared_mid(h, j, 6)
                            shared_lo(h, j)
                        else:
                            keep(h, 6)

            moe_body(0, first=True)
            dve.wait_ge(c3_chain, 2)
            link(nc.vector.tensor_tensor(c3l[:, :, :], c3f[:, :, :], f(c3h[:, :, :]), ALU.subtract))
            link(nc.vector.tensor_scalar(c3l[:, :, :], c3l[:, :, :], cst[0:3, C_ROW + 1:C_ROW + 2], None, ALU.mult))
            nc.vector.scalar_tensor_tensor(c3[:, :, :], f(c3h[:, :, :]), cst[0:3, C_ROW:C_ROW + 1], c3l[:, :, :],
                                           ALU.mult, ALU.add).then_inc(c3_done, 1)
            moe_body(1, second=True)
            with dve.Fori(2, E // G) as h:
                moe_body(h)
            weigh(E // G - 1, G - 1, False)

            with dve.Fori(0, BATCH) as b:
                for u in range(TILES_B):
                    t = b * TILES_B + u
                    dve.wait_ge(att_done, t + 1)
                    nc.vector.scalar_tensor_tensor(sh[:, bass.ds(t, 1), :], bank[UNIT_BANK[u]][:, 0:D].unsqueeze(1), s2[:, bass.ds(t, 1)],
                                                   sh[:, bass.ds(t, 1), :], ALU.mult, ALU.add).then_inc(half_done, 1)
            for g in range(GROUPS):
                dve.wait_ge(y_in[g % 2], 16 * (g // 2 + 1))
                for j in range(1, G, 2):
                    t = g * G + j
                    dve.wait_ge(half_done, t + 1)
                    nc.vector.tensor_tensor(sh[:, t, :], sh[:, t, :], yin[g % 2][:, j, :], ALU.add).then_inc(ot_dve, 1)

        @block.tensor
        def _(pe):
            ident = cst[:, C_ID:C_ID + P]
            pe.wait_ge(cst_in, 16)

            def turn(g, j, first):
                t = g * G + j
                pe.wait_ge(norm_done, t + 1)
                if not (first and j < 2):
                    pe.wait_ge(lo_done, t - 1)
                for c in range(DC):
                    last = nc.tensor.transpose(bank[4 + j % 2][:, c * P:(c + 1) * P], xn[:, j, c * P:(c + 1) * P], ident)
                last.then_inc(t_done, 1)

            def turn_rows(g):
                pe.wait_ge(i3_ready, min(2 * g + 2, 6))
                if g == 1:
                    pe.wait_ge(act_prep, 4)
                if g >= 2:
                    pe.wait_ge(ib_done, g - 1)
                for j in range(G):
                    last = nc.tensor.transpose(bank[2 + g % 2][0:3, j * P:(j + 1) * P], i3[:, g * G + j, :], ident)
                last.then_inc(ibt_done, 1)

            def route(g, j, first):
                q = j // 2
                if not first and j % 2 == 0:
                    pe.wait_ge(sc_read, 2 * g + q - 1)
                for c in range(DC):
                    last = mm3(bank[6 + q][:, j % 2 * E:(j % 2 + 1) * E], hl[:, j, 0, c, :], hl[:, j, 1, c, :],
                               gt_s[:, c, 0, :], gt_s[:, c, 1, :], c == 0, c == DC - 1)
                if j % 2 == 1:
                    last.then_inc(router_done, 1)

            def keys(g, j, first):
                t = g * G + j
                if not (first and j < 2):
                    pe.wait_ge(sq_done, 2 * t - 2)
                pe.wait_ge(lo_done, t + 1)
                if first and j == 0:
                    pe.wait_ge(prep_done, 2)
                for c in range(DC):
                    mm3(bank[j % 2][:, :], hl[:, j, 0, c, :], hl[:, j, 1, c, :], wkv_s[:, c, 0, :], wkv_s[:, c, 1, :], c == 0, False)
                if j % 2 == 0:
                    pe.wait_ge(ib_in[j // 2], 16 * (g + 1))
                if first and j == 0:
                    pe.wait_ge(prep_done, 4)
                nc.tensor.matmul(bank[j % 2][:, :], ib[:, j, :], b3[:, :], start=False, stop=True).then_inc(kv_done, 1)

            def body(g, first=False, last=False):
                for j in range(G):
                    if j < 2:
                        turn(g, j + 2, first)
                    elif not last:
                        turn(g + 1, j - 2, False)
                    keys(g, j, first)
                    route(g, j, first)
                    if first and j == 2:
                        turn_rows(1)
                    if first and j == 3:
                        turn_rows(2)
                        turn_rows(3)

            turn(0, 0, True)
            turn(0, 1, True)
            pe.wait_ge(ones_set, 4)
            pe.wait_ge(wi_in, 48)
            for c in range(DC):
                nc.tensor.matmul(bank[3][0:3, :], bet3[:, c, :], wi[:, c, D:3 * D], start=c == 0, stop=False)
            nc.tensor.matmul(bank[3][0:3, :], ones3[:, 0:3], bin_row[:, D:3 * D], start=False, stop=True).then_inc(pe_prep, 1)
            turn_rows(0)
            body(0, first=True)
            with pe.Fori(1, GROUPS - 1) as g:
                body(g)
            body(GROUPS - 1, last=True)
            pe.wait_ge(ib_done, GROUPS)
            for c in range(DC):
                for k in range(DC):
                    nc.tensor.matmul(bank[2][:, 392 + c * 3:395 + c * 3], wi[:, k, c * P:(c + 1) * P], bet3[:, k, :], start=k == 0, stop=False)
                nc.tensor.matmul(bank[2][:, 392 + c * 3:395 + c * 3], bin_row[:, c * P:(c + 1) * P], ones3[:, 0:3], start=False, stop=True)
            pe.wait_ge(acc_done_t, TILES)
            for b in range(BATCH):
                last = nc.tensor.matmul(bank[2 + b][0:1, 0:D + ROT], one_col[:, :], acc[:, b, :], start=True, stop=True)
            last.then_inc(red_done, 1)

            def shared(g, c, pair):
                n, q = SC[c], g * 3 + c
                if not isinstance(g, int) or g > 0:
                    pe.wait_ge(sm_done, q)
                if not (isinstance(g, int) and g == 0) and c == 0:
                    pe.wait_ge(kept, 2 * g)
                for w_s, dst in ((swg_s, bank[pair]), (swu_s, bank[pair + 1])):
                    for d in range(DC):
                        xr = xt_all[:, bass.ds(g * G, G), :, d, :]
                        last = mm3(dst[0:n, :].rearrange("p (t n) -> p t n", n=P), w_s[:, d, 0, c * P:c * P + n], w_s[:, d, 1, c * P:c * P + n],
                                   xr[:, :, 0, :], xr[:, :, 1, :], d == 0, d == DC - 1)
                last.then_inc(sh_done, 1)

            def shared_down(g, pair):
                pe.wait_ge(lo_m, g * 3 + 3)
                for j in range(G):
                    for c in range(3):
                        n = SC[c]
                        last = mm3(bank[pair + j // 2][:, j % 2 * D:(j % 2 + 1) * D], smid_s[0:n, c, 0, j * P:(j + 1) * P],
                                   smid_s[0:n, c, 1, j * P:(j + 1) * P], swd_s[0:n, c, 0, :], swd_s[0:n, c, 1, :], c == 0, c == 2)
                    if j % 2 == 1:
                        last.then_inc(dn_done, 1)

            pe.wait_ge(mask_done, 1)
            pe.wait_ge(const_done, 5)
            pe.wait_ge(sc_read, 2 * GROUPS)
            nc.tensor.matmul(bank[7][:, 0:TILES * E], tri16[:, :], mask16[:, :, :].rearrange("p t e -> p (t e)"), start=True, stop=False)
            for t in range(TILES - 1):
                n = TILES - 1 - t
                last = nc.tensor.matmul(bank[7][:, (t + 1) * E:TILES * E].rearrange("p (t e) -> p t e", e=E), one16[:, :],
                                        mask16[:, t:t + 1, :].to_broadcast([P, n, E]), start=False, stop=t == TILES - 2)
            last.then_inc(rank_done, 1)
            for q in range(2):
                pe.wait_ge(xt_saved[q], 16 * TILES // 4)
            pe.wait_ge(sw_lo, 2)
            pe.wait_ge(sq_done, 2 * TILES)
            shared(0, 0, GAP_PAIR[0])
            pe.wait_ge(arow_done, 3)
            for b in range(BATCH):
                for c in range(DC):
                    last = nc.tensor.matmul(bank[2][:, 384 + b * DC + c:385 + b * DC + c], arow[0:1, b, c * P:(c + 1) * P], ones3[0:1, 0:1],
                                            start=True, stop=True)
            last.then_inc(acol_done, 1)
            pe.wait_ge(onehot_done, 2)
            pe.wait_ge(oa_done, 1)
            for t in range(TILES):
                last = nc.tensor.matmul(bank[6][:, 0:E * SLOT_B], oat[:, t, :, :].rearrange("p a e -> p (a e)"),
                                        ob[:, t, :, :].rearrange("p b e -> p (b e)"), start=t == 0, stop=t == TILES - 1)
            last.then_inc(table_done, 1)
            pe.wait_ge(lo_done, TILES)
            shared(0, 1, GAP_PAIR[1])
            pe.wait_ge(spread_done, 1)
            nc.tensor.matmul(bank[6][:, 256:256 + E], spread[:, :, :].rearrange("p a b -> p (a b)"), exp16[:, :],
                             start=True, stop=True).then_inc(slot_done, 1)
            pe.wait_ge(sm_done, 1)
            shared(0, 2, GAP_PAIR[2])

            pe.wait_ge(aw_done, 1 + BATCH * DC)
            pe.wait_ge(mix_in, 32)
            for b in range(BATCH):
                for c in range(DC):
                    if b * DC + c == 2:
                        pe.wait_ge(sm_done, 2)
                    for k in range(DC):
                        last = nc.tensor.matmul(bank[2 + b * DC + c][:, 0:D], wqt[:, k, c * P:(c + 1) * P], aw[:, b, k, :], start=k == 0, stop=k == DC - 1)
                    last.then_inc(m_done, 1)
            pe.wait_ge(onehot_done, 1)
            for b in range(BATCH):
                for k in range(DC):
                    nc.tensor.matmul(bank[7][0:3, b * D:(b + 1) * D], bq3[:, k, :], aw[:, b, k, :], start=k == 0, stop=False)
                last = nc.tensor.matmul(bank[7][0:3, b * D:(b + 1) * D], ones3[:, 0:3], bout_row[:, :], start=False, stop=True)
            last.then_inc(c_done, 1)
            pe.wait_ge(sw_lo, 4)
            pe.wait_ge(sm_done, 3)
            shared_down(0, 0)

            def turn_rows_e(e, j, h):
                pe.wait_ge(gath[j], 16 * (h + 1))
                if not (isinstance(e, int) and e < 2):
                    pe.wait_ge(xgt_done, e - 1)
                for c in range(DC):
                    last = nc.tensor.transpose(bank[4 + j % 2][:, c * P:(c + 1) * P], xg[:, j, c * P:(c + 1) * P], ident)
                last.then_inc(xt_e, 1)

            def gate_up(e, j, h):
                k = j % 2
                pe.wait_ge(ew_in[j], 48 * (h + 1))
                if not (isinstance(e, int) and e < 2):
                    pe.wait_ge(mid_done, 2 * (e - 1))
                pe.wait_ge(xgt_done, e + 1)
                for q, (lo_, n) in enumerate(((0, P), (P, P), (2 * P, UP2 + I2))):
                    for c in range(DC):
                        last = nc.tensor.matmul(bank[k][0:n, q * P:(q + 1) * P], wgu[:, j, c, lo_:lo_ + n], xgt[:, k, c, :],
                                                start=c == 0, stop=c == DC - 1)
                last.then_inc(gu_done, 1)

            def down(e, j, first):
                k = j % 2
                pe.wait_ge(mid_done, 2 * e + 2)
                if not first:
                    pe.wait_ge(eo_done, e - 1)
                nc.tensor.matmul(bank[2 + k][:, 0:D], mid[:, k, 0, :], wdn[:, j, 0, :], start=True, stop=False)
                nc.tensor.matmul(bank[2 + k][:, 0:D], mid[0:I2, k, 1, :], wdn[0:I2, j, 1, :], start=False, stop=True).then_inc(d_done, 1)

            def moe_body(h, first=False, last=False):
                for j in range(G):
                    e = h * G + j
                    if not (last and j == G - 1):
                        turn_rows_e(e + 1, (j + 1) % G, h + (j + 1) // G)
                    gate_up(e, j, h)
                    if not (first and j == 0):
                        down(e - 1, (j - 1) % G, first and j <= 2)
                    if not first:
                        if j < 3:
                            shared(h, j, 6)
                        else:
                            shared_down(h, 6)

            pe.wait_ge(m_lo, BATCH * DC)
            turn_rows_e(0, 0, 0)
            pe.wait_ge(kept, 2)
            moe_body(0, first=True)
            pe.wait_ge(c3_chain, 1)
            pe.wait_ge(idx_done, 1)
            with pe.Fori(1, E // G - 1) as h:
                moe_body(h)
            moe_body(E // G - 1, last=True)
            down(E - 1, G - 1, False)

            pe.wait_ge(c3_done, 1)
            pe.wait_ge(kept, 2 * GROUPS)
            pe.wait_ge(mid_done, 2 * E)
            for t in range(TILES):
                b, u = t // TILES_B, t % TILES_B
                dst = bank[UNIT_BANK[u]][:, 0:D]
                if b == 0 and UNIT_BANK[u] == 2:
                    pe.wait_ge(eo_done, E)
                if b > 0:
                    pe.wait_ge(half_done, t - TILES_B + 1)
                for d in range(DC):
                    mm3(dst, xt_all[:, t, 0, d, :], xt_all[:, t, 1, d, :], m_s[:, b, d, 0, :], m_s[:, b, d, 1, :], d == 0, False)
                nc.tensor.matmul(dst, ib_all[:, t, :], c3[:, b, :], start=False, stop=True).then_inc(att_done, 1)


def kernel(L0_attn_X, L0_attn_W_in, L0_attn_b_in, L0_attn_W_out, L0_attn_b_out, L0_attn_gamma, L0_attn_beta,
           L0_ffn_gate_w, L0_ffn_w_gate, L0_ffn_w_up, L0_ffn_w_down, L0_ffn_sw_gate, L0_ffn_sw_up, L0_ffn_sw_down):
    import numpy as np
    import concourse.bacc as bacc
    from concourse.bass_utils import run_bass_kernel_spmd as run

    order = np.concatenate([np.arange(0, ROT, 2), np.arange(1, ROT, 2), np.arange(ROT, D)])
    w_in, b_in = np.asarray(L0_attn_W_in), np.asarray(L0_attn_b_in)
    cols = np.concatenate([order + k * D for k in range(3)])
    w_gate, w_up = np.asarray(L0_ffn_w_gate), np.asarray(L0_ffn_w_up)
    gap = np.zeros((E, D, UP2 - I2), np.float32)
    w_gu = np.concatenate([w_gate[:, :, :P], w_up[:, :, :P], w_gate[:, :, P:], gap, w_up[:, :, P:]], axis=2)

    seq = TOKENS // BATCH
    inv = (1.0 / np.float32(10000.0) ** (np.arange(0, ROT, 2, dtype=np.float32) / np.float32(ROT))).astype(np.float32)
    angle = (np.arange(seq, dtype=np.float32)[:, None] * inv[None, :]).astype(np.float64)
    cos, sin = np.cos(2 * angle) / 4, np.sin(2 * angle) / 4
    trig = np.concatenate([cos, -cos, -sin, -sin], axis=1).astype(np.float32)

    p = np.arange(P)
    consts = np.zeros((P, C_ALL), np.float32)
    consts[:, C_ID:C_ID + P] = np.eye(P)
    consts[:, C_TRI:C_TRI + P] = p[:, None] < p[None, :]
    consts[:, C_EXP:C_EXP + E] = (p[:, None] % E) == np.arange(E)[None, :]
    consts[:, C_ASEL:C_ASEL + SLOT_A] = (p[:, None] // E) == np.arange(SLOT_A)[None, :]
    consts[:, C_I16:C_I16 + E] = np.arange(E)[None, :]
    consts[:, C_TOK:C_TOK + TILES] = P * np.arange(TILES)[None, :] + p[:, None] + 1
    consts[:, C_SPARE] = TOKENS + 1 + p
    consts[0:3, C_ROW] = (1, 0, 1)
    consts[0:3, C_ROW + 1] = (0, 1, 0)

    ins = {
        "x": L0_attn_X, "w_in": np.concatenate([w_in[:, cols], np.asarray(L0_ffn_gate_w).T], axis=1),
        "bias": np.concatenate([b_in[cols], np.asarray(L0_attn_b_out)])[None, :], "wq_t": w_in[:, order].T,
        "w_out": np.asarray(L0_attn_W_out)[order, :],
        "gb": np.concatenate([np.asarray(a).reshape(DC, P).T for a in (L0_attn_gamma, L0_attn_beta)], axis=1),
        "w_gu": w_gu, "w_dn": L0_ffn_w_down,
        "sw_g": L0_ffn_sw_gate, "sw_u": L0_ffn_sw_up, "sw_d": L0_ffn_sw_down, "trig": trig, "consts": consts,
    }
    nc = bacc.Bacc("TRN2", target_bir_lowering=False, num_devices=1)
    arrays, args = {}, []
    for name, a in ins.items():
        a = np.ascontiguousarray(a)
        arrays[f"in_{name}"] = a
        args.append(nc.dram_tensor(f"in_{name}", a.shape, mybir.dt.from_np(a.dtype), kind="ExternalInput").ap())
    args.append(nc.dram_tensor("out", (BATCH, TOKENS // BATCH, D), F32, kind="ExternalOutput").ap())
    layer(nc, *args)
    r = run(nc, [arrays], core_ids=[0])
    return r.results[0]["out"]
```

```python
from contextlib import ExitStack

import concourse.bass as bass
from concourse import mybir

P = 128
TOKENS, D, BATCH = 2048, 256, 2
TILES = TOKENS // P
G = 4
GROUPS = TILES // G
GROUPS_B = GROUPS // BATCH
TILES_B = TILES // BATCH
DC = D // P
ROT = D // 2
HALF = ROT // 2
E, TOP, CAP = 16, 4, 128
I = 176
I2 = I - P
UP2 = 64
GU = 2 * P + UP2 + I2
KVR = 2 * D + E
IS = 352
SC = [P, P, IS - 2 * P]
ROW = D + E
SLOT_A, SLOT_B = 8, 16
EPS = 1e-5
WARM_UP = 7
GAP_PAIR = (0, 4, 0)
MIX_BANK = (6, 7, 6, 7, 6, 7, 6, 7, 4, 5, 0, 1, 2, 3, 4, 5)
MIX_FIRST = ((), (0, 1), (2,), (3,))
MIX_LAST = ((4,), (5,), (6,), (7,))
MIX_CHUNK = ((8, 9), (10, 11), (12, 13, 14, 15))

F32 = mybir.dt.float32
F32R = mybir.dt.float32r
F16 = mybir.dt.float16
I32 = mybir.dt.int32
U32 = mybir.dt.uint32
ALU = mybir.AluOpType
ACT = mybir.ActivationFunctionType
AX = mybir.AxisListType

C_ID = 0
C_TRI = C_ID + P
C_EXP = C_TRI + P
C_ASEL = C_EXP + E
C_I16 = C_ASEL + SLOT_A
C_TOK = C_I16 + E
C_SPARE = C_TOK + TILES
C_ROW = C_SPARE + 1
C_ALL = C_ROW + 2


def layer(nc, x, w_in, bias, wq_t, w_out, gb, w_gu, w_dn, sw_g, sw_u, sw_d,
          trig, consts, out):
    ctx = ExitStack()
    with ctx:
        def sb(name, shape, dt=F32):
            return ctx.enter_context(nc.sbuf_tensor(name, shape, dt))

        def sem(name):
            return ctx.enter_context(nc.semaphore(name))

        def sems(name, n):
            return [sem(f"{name}{i}") for i in range(n)]

        rows = nc.dram_tensor("rows", (TOKENS + CAP, ROW), F32, kind="Internal").ap()
        ysum = nc.dram_tensor("ysum", (TOKENS + CAP, D), F32, kind="Internal").ap()

        cst = sb("cst", [P, C_ALL])
        x_all = sb("x_all", [P, TILES, D])
        wi = sb("wi", [P, DC, 3 * D + E])
        wqt = sb("wqt", [P, DC, D])
        wo = sb("wo", [P, DC, D])
        sh = x_all
        gt = wi[:, :, 3 * D:3 * D + E]
        bias_row = sb("bias_row", [1, 4 * D])
        bin_row, bout_row = bias_row[:, 0:3 * D], bias_row[:, 3 * D:4 * D]
        gb_cols = sb("gb_cols", [P, 2 * DC])
        gam, bet = gb_cols[:, 0:DC], gb_cols[:, DC:2 * DC]
        trg = sb("trg", [P, TILES_B, D])
        ones3 = sb("ones3", [1, 4])
        bet3 = sb("bet3", [P, DC, 3])
        wkvr_s = sb("wkvr_s", [P, DC, 2, KVR], F32R)
        wkv_s, gt_s = wkvr_s[:, :, :, 0:2 * D], wkvr_s[:, :, :, 2 * D:KVR]
        swg_s, swu_s = sb("swg_s", [P, DC, 2, IS], F32R), sb("swu_s", [P, DC, 2, IS], F32R)
        swd_s = sb("swd_s", [P, 3, 2, D], F32R)
        b3h, b3u = sb("b3h", [3, 2 * D], F32R), sb("b3u", [3, 2 * D])
        b3 = sb("b3", [3, KVR], F32R)
        st6 = sb("st6", [P, G, 6])
        mv = sb("mv", [P, TILES, 2])
        rstd, s2 = sb("rstd", [P, TILES]), sb("s2", [P, TILES])
        lt = sb("lt", [P, 4, TILES])
        mhalf = sb("mhalf", [P, TILES])
        ihi = sb("ihi", [P, TILES], F32R)
        i3 = sb("i3", [P, TILES, 3])
        xn = sb("xn", [P, G, D])
        hl = sb("hl", [P, G, 2, DC, P], F32R)
        xt_all = sb("xt_all", [P, TILES, 2, DC, P], F32R)
        ib, ib_all = sb("ib", [3, G, P], F32R), sb("ib_all", [3, TILES, P], F32R)
        kv = sb("kv", [P, 2, KVR])
        junk = sb("junk", [P, 2, D])
        nrm = sb("nrm", [P, G, 2])
        wtok, wprod = sb("wtok", [P, G]), sb("wprod", [P, G])
        ph = sb("ph", [P, G, D + ROT])
        rot = sb("rot", [P, 2, ROT])
        acc = sb("acc", [P, BATCH, D + ROT])
        one_col = sb("one_col", [P, 1])
        ab = sb("ab", [1, BATCH, D + ROT])
        aq, af, arow = sb("aq", [1, BATCH, HALF]), sb("af", [1, BATCH, HALF]), sb("arow", [1, BATCH, D])
        acol = sb("acol", [P, BATCH * DC])
        aw = sb("aw", [P, BATCH, DC, D])
        bq3 = sb("bq3", [P, DC, 3])
        m_s = wkv_s.rearrange("p b h (c n) -> p b c h n", n=D)
        c3h, c3u, c3 = (r.rearrange("k (b n) -> k b n", b=BATCH) for r in (b3h[:, :], b3u[:, :], b3[:, 0:2 * D]))
        lg = sb("lg", [P, TILES, E])
        mx, ix = sb("mx", [P, G, 8]), sb("ix", [P, G, 8], U32)
        top1, ixf = sb("top1", [P, TILES]), sb("ixf", [P, TILES, TOP], F16)
        eq = sb("eq", [P, TILES, E, TOP], F16)
        ex, em = sb("ex", [P, TILES, E]), sb("em", [P, TILES, E])
        mask16 = sb("mask16", [P, TILES, E], F16)
        tri16, one16, exp16 = sb("tri16", [P, P], F16), sb("one16", [P, P], F16), sb("exp16", [P, E], F16)
        zsum, esum, einv = sb("zsum", [P, TILES]), sb("esum", [P, TILES]), sb("einv", [P, TILES])
        wd = sb("wd", [P, TILES, E])
        rank = sb("rank", [P, TILES, E])
        rank_i = sb("rank_i", [P, TILES, E], I32)
        ra_i, rb_i = sb("ra_i", [P, TILES, E], I32), sb("rb_i", [P, TILES, E], I32)
        ra, rb = sb("ra", [P, TILES, E], F16), sb("rb", [P, TILES, E], F16)
        iota_b, iota_k = sb("iota_b", [P, SLOT_B, E], F16), sb("iota_k", [P, E, TOP], F16)
        tok16 = sb("tok16", [P, TILES], F16)
        onehots = x_all[:, :, :].rearrange("p t d -> p (t d)").bitcast(F16)
        n_a, n_b = TILES * E * SLOT_A, TILES * E * SLOT_B
        oa = onehots[:, 0:n_a].rearrange("p (t a e) -> p t a e", t=TILES, e=E)
        oat = onehots[:, n_a:2 * n_a].rearrange("p (t a e) -> p t a e", t=TILES, e=E)
        ob = onehots[:, 2 * n_a:2 * n_a + n_b].rearrange("p (t b e) -> p t b e", t=TILES, e=E)
        diag, tb = sb("diag", [P, SLOT_B, E]), sb("tb", [P, SLOT_B])
        spread = sb("spread", [P, SLOT_A, SLOT_B], F16)
        slot_v, slot_e, slot_f = sb("slot_v", [P, E]), sb("slot_e", [P, E]), sb("slot_f", [P, E])
        idx = sb("idx", [P, E], I32)
        zero = sb("zero", [P, ROW])
        wgu = sb("wgu", [P, G, DC, GU])
        wdn = trg[:, :, :].rearrange("p (j c) n -> p j c n", c=2)
        idx_g, idx_s = sb("idx_g", [P, G], I32), sb("idx_s", [P, G], I32)
        xg = sb("xg", [P, G, ROW])
        sw_flat = wgu[:, :, :, :].rearrange("p j c n -> p (j c n)")
        swg = sw_flat[:, 0:DC * IS].rearrange("p (c n) -> p c n", c=DC)
        swu = sw_flat[:, DC * IS:2 * DC * IS].rearrange("p (c n) -> p c n", c=DC)
        swd = sw_flat[:, 2 * DC * IS:2 * DC * IS + 3 * D].rearrange("p (c n) -> p c n", c=3)
        ph_flat = ph[:, :, :].rearrange("p j n -> p (j n)")
        xgt = ph_flat[:, 0:2 * DC * P].rearrange("p (k c n) -> p k c n", k=2, c=DC)
        sil = ph_flat[:, 2 * DC * P:4 * DC * P].rearrange("p (k c n) -> p k c n", k=2, c=2)
        mid = junk[:, :, :].rearrange("p k (c n) -> p k c n", c=2)
        eo = kv[:, :, :].rearrange("p k n -> p (k n)")[:, 0:G * D].rearrange("p (j n) -> p j n", n=D)
        sg, smid = sb("sg", [P, 2, G * P]), sb("smid", [P, 2, G * P])
        w_flat, d_flat = sw_flat, trg[:, :, :].rearrange("p t n -> p (t n)")
        yin = [r[:, k * G * D:(k + 1) * G * D].rearrange("p (j n) -> p j n", n=D) for r in (w_flat, d_flat) for k in range(2)]
        smid_s = sb("smid_s", [P, 3, 2, G * P], F32R)

        bank = [ctx.enter_context(nc.psum_tensor(f"bank{i}", [P, 512], F32)) for i in range(8)]

        def f(ap):
            return ap.bitcast(F32)

        x_in = sems("x_in", GROUPS)
        ib_in, ib_set = sems("ib_in", 2), sem("ib_set")
        pool_passed, sp_passed = sem("pool_passed"), sem("sp_passed")
        cst_in, wi_in, trg_in, mix_in, sw_in = (sem(n) for n in ("cst_in", "wi_in", "trg_in", "mix_in", "sw_in"))
        ew_in = sems("ew_in", G)
        ones_set, prep_done, act_prep = sem("ones_set"), sem("prep_done"), sem("act_prep")
        pool_prep, a_pool, pe_prep = sem("pool_prep"), sem("a_pool"), sem("pe_prep")
        v2_chain, v2_ready, s2_ready, i3_chain = sem("v2_chain"), sem("v2_ready"), sem("s2_ready"), sem("i3_chain")
        st_chain, stats_done, ln_ready, i3_ready, norm_done = (sem(n) for n in ("st_chain", "stats_done", "ln_ready", "i3_ready", "norm_done"))
        xn_saved, xt_saved = sems("xn_saved", 2), sems("xt_saved", 2)
        x_saved = sem("x_saved")
        t_done, hi_done, lo_done = sem("t_done"), sem("hi_done"), sem("lo_done")
        ibt_done, ib_done, kv_done = sem("ibt_done"), sem("ib_done"), sem("kv_done")
        v_done, sq_done, prod_done, rot_done, tab_done = sem("v_done"), sem("sq_done"), sem("prod_done"), sem("rot_done"), sem("tab_done")
        w_ready, w_chain, acc_zero, acc_done_t, red_done = sem("w_ready"), sem("w_chain"), sem("acc_zero"), sem("acc_done_t"), sem("red_done")
        lg_kept, mx_done, ix_done, top_kept = sem("lg_kept"), sem("mx_done"), sem("ix_done"), sem("top_kept")
        ab_done, arow_done, acol_done, aw_done = (sem(n) for n in ("ab_done", "arow_done", "acol_done", "aw_done"))
        m_done, m_hi, m_lo, c_done, c3_done = (sem(n) for n in ("m_done", "m_hi", "m_lo", "c_done", "c3_done"))
        r_chain, lm_done, exp_done, wd_done, wd_saved = (sem(n) for n in ("r_chain", "lm_done", "exp_done", "wd_done", "wd_saved"))
        mask_done, rank_done, onehot_done, oa_done, table_done, spread_done, slot_done, idx_done = (
            sem(n) for n in ("mask_done", "rank_done", "onehot_done", "oa_done", "table_done", "spread_done", "slot_done", "idx_done"))
        zero_set, pads_saved = sem("zero_set"), sem("pads_saved")
        rows_ready = sem("rows_ready")
        idx_copied = sem("idx_copied")
        gath, scat_done = sems("gath", G), sem("scat_done")
        xt_e, xgt_done, gu_done, silu_done, mid_done, d_done, eo_done = (
            sem(n) for n in ("xt_e", "xgt_done", "gu_done", "silu_done", "mid_done", "d_done", "eo_done"))
        c3_chain, yx_done = sem("c3_chain"), sem("yx_done")
        sw_hi, sw_lo, const_done = sem("sw_hi"), sem("sw_lo"), sem("const_done")
        xn_in, y_in, out_sent = sem("xn_in"), sems("y_in", GROUPS), sems("out_sent", GROUPS + 1)
        sh_done, sg_done, sm_done, hi_m, lo_m, dn_done, kept = (
            sem(n) for n in ("sh_done", "sg_done", "sm_done", "hi_m", "lo_m", "dn_done", "kept"))
        att_done, half_done, ot_pool, ot_dve = sem("att_done"), sem("half_done"), sem("ot_pool"), sem("ot_dve")

        x_v = x.rearrange("b (t p) d -> p (b t) d", p=P)
        out_v = out.rearrange("b (t p) d -> p (b t) d", p=P)
        rows_v = rows.rearrange("(t p) d -> p t d", p=P)
        ysum_v = ysum.rearrange("(t p) d -> p t d", p=P)

        block = ctx.enter_context(nc.Block())

        def mm3(dst, lt_hi, lt_lo, r_hi, r_lo, start, stop):
            nc.tensor.matmul(dst, lt_hi, r_hi, start=start, stop=False)
            nc.tensor.matmul(dst, lt_hi, r_lo, start=False, stop=False)
            return nc.tensor.matmul(dst, lt_lo, r_hi, start=False, stop=stop)

        @block.sync
        def _(sp):
            def load_expert(e, j):
                sp.dma_start(wgu[:, j, :, :], w_gu[e, :, :].rearrange("(c p) n -> p c n", p=P)).then_inc(ew_in[j], 16)
                sp.dma_start(wdn[:, j, 0, :], w_dn[e, 0:P, :]).then_inc(ew_in[j], 16)
                sp.dma_start(wdn[0:I2, j, 1, :], w_dn[e, P:I, :]).then_inc(ew_in[j], 16)

            def load_x(g):
                sp.dma_start(x_all[:, g * G:(g + 1) * G, :], x_v[:, g * G:(g + 1) * G, :]).then_inc(x_in[g], 16)

            load_x(0)
            sp.dma_start(wi[:, :, :], w_in.rearrange("(c p) n -> p c n", p=P)).then_inc(wi_in, 16)
            for g in range(1, GROUPS):
                load_x(g)
            sp.dma_start(trg[:, :, :], trig.rearrange("(t p) c -> p t c", p=P)).then_inc(trg_in, 16)
            sp.dma_start(swg[:, :, :], sw_g.rearrange("(c p) n -> p c n", p=P)).then_inc(sw_in, 16)
            sp.dma_start(swu[:, :, :], sw_u.rearrange("(c p) n -> p c n", p=P)).then_inc(sw_in, 16)
            sp.dma_start(swd[:, 0:2, :], sw_d[0:2 * P, :].rearrange("(c p) n -> p c n", p=P)).then_inc(sw_in, 16)
            sp.dma_start(swd[0:SC[2], 2, :], sw_d[2 * P:IS, :]).then_inc(sw_in, 16)

            def save_xn(t, q):
                sp.wait_ge(norm_done, t + 2)
                sp.dma_start(rows_v[:, bass.ds(t, 2), 0:D], xn[:, 2 * q:2 * q + 2, :]).then_inc(xn_saved[q], 16)

            def save_xt(t, q):
                sp.wait_ge(lo_done, t + 2)
                sp.dma_start(f(xt_all[:, bass.ds(t, 2), :, :, :]).rearrange("p a h c n -> p (a h c n)"),
                             f(hl[:, 2 * q:2 * q + 2, :, :, :]).rearrange("p a h c n -> p (a h c n)")).then_inc(xt_saved[q], 16)

            def load_ib(t, q):
                sp.dma_start(f(ib[:, 2 * q:2 * q + 2, :]), f(ib_all[:, bass.ds(t, 2), :])).then_inc(ib_in[q], 16)

            save_xn(0, 0)
            save_xn(2, 1)
            save_xt(0, 0)
            with sp.Fori(0, GROUPS - 1) as h:
                for q in range(2):
                    save_xn(h * G + 2 * q + G, q)
                    save_xt(h * G + 2 * q + 2, 1 - q)
                    sp.wait_ge(kv_done, h * G + 2 * q + 2)
                    if q == 0:
                        sp.sem_inc(sp_passed, 1)
                        sp.wait_ge(ib_done, h + 2)
                    load_ib(h * G + 2 * q + G, q)
            save_xt(TILES - 2, 1)
            sp.dma_start(ysum_v[:, 0:TILES, :], x_all[:, :, :]).then_inc(x_saved, 16)
            sp.dma_start(wqt[:, :, :], wq_t.rearrange("(c p) n -> p c n", p=P)).then_inc(mix_in, 16)
            sp.dma_start(wo[:, :, :], w_out.rearrange("(c p) n -> p c n", p=P)).then_inc(mix_in, 16)
            sp.wait_ge(zero_set, 1)
            sp.dma_start(rows[TOKENS:TOKENS + CAP, :], zero[:, :]).then_inc(pads_saved, 16)
            sp.dma_start(ysum[TOKENS:TOKENS + CAP, :], zero[:, 0:D]).then_inc(pads_saved, 16)
            for q in range(2):
                sp.wait_ge(xn_saved[q], 16 * TILES // 4)

            def load_xn(g):
                sp.dma_start(xn[:, :, :], rows_v[:, bass.ds(g * G, G), 0:D]).then_inc(xn_in, 16)

            load_xn(0)
            sp.wait_ge(tab_done, TILES)
            sp.wait_ge(sw_lo, 4)
            for j in range(G):
                load_expert(j, j)
            sp.wait_ge(wd_done, 1)
            sp.dma_start(rows_v[:, 0:TILES, D:ROW], wd[:, :, :]).then_inc(wd_saved, 16)
            sp.wait_ge(x_saved, 16)
            sp.wait_ge(pads_saved, 32)
            sp.wait_ge(wd_saved, 16)
            sp.sem_inc(rows_ready, 1)
            with sp.Fori(0, E // G - 1) as h:
                for j in range(G):
                    if j == 3:
                        sp.wait_ge(kept, 2 * h + 2)
                        load_xn(h + 1)
                    sp.wait_ge(gu_done, h * G + j + 1)
                    sp.wait_ge(d_done, h * G + j + 1)
                    load_expert(h * G + G + j, j)

            sp.wait_ge(gu_done, E)
            sp.wait_ge(d_done, E)
            sp.wait_ge(scat_done, 16 * E)
            for g in range(GROUPS):
                sp.dma_start(yin[g][:, :, :], ysum_v[:, g * G:(g + 1) * G, :]).then_inc(y_in[g], 16)
            for g in range(GROUPS - 1):
                sp.wait_ge(ot_pool, 2 * g + 2)
                sp.wait_ge(ot_dve, 2 * g + 2)
                sp.dma_start(out_v[:, g * G:(g + 1) * G, :], sh[:, g * G:(g + 1) * G, :]).then_inc(out_sent[g], 16)
            for q in range(2):
                t = TILES - G + 2 * q
                sp.wait_ge(kept, 2 * (GROUPS - 1) + q + 1)
                sp.dma_start(out_v[:, t:t + 2, :], sh[:, t:t + 2, :]).then_inc(out_sent[GROUPS - 1 + q], 16)
            for sent in out_sent:
                sp.wait_ge(sent, 16)
            for q in range(2):
                sp.wait_ge(xt_saved[q], 16 * TILES // 4)

        @block.gpsimd
        def _(pool):
            pool.memset(mhalf[:, :], -0.5).then_inc(pool_prep, 1)
            pool.memset(zero[:, :], 0.0).then_inc(zero_set, 1)
            pool.wait_ge(pool_prep, 1)

            def await_ge(signal, count):
                pool.wait_ge(signal, count)
                if not isinstance(count, int):
                    pool.sem_inc(pool_passed, 1)

            def rstd_of(k, a, b):
                pool.wait_ge(stats_done, b // G)
                nc.gpsimd.tensor_tensor(rstd[:, a:b], lt[:, 0, a:b], mhalf[:, 0:b - a], ALU.pow).then_inc(ln_ready, 1)

            def s2_of(k, a, b):
                pool.wait_ge(v2_ready, k)
                nc.gpsimd.tensor_tensor(s2[:, a:b], lt[:, 3, a:b], mhalf[:, 0:b - a], ALU.pow).then_inc(s2_ready, 1)

            def rotate(g, j, half, first):
                t = g * G + j
                if not (first and j == 0):
                    await_ge(tab_done, t)
                await_ge(prod_done, 2 * t + 2)
                pxy = ph[:, j, :].rearrange("p (a n) -> p a n", n=ROT)[:, 0:3:2, :]
                nc.gpsimd.tensor_tensor(rot[:, :, :], pxy, trg[:, bass.ds(half * G + j, 1), :].rearrange("p o (a n) -> p (o a) n", a=2),
                                        ALU.mult).then_inc(rot_done, 1)
                await_ge(sq_done, 2 * t + 2)
                nc.gpsimd.tensor_tensor(wprod[:, j:j + 1], nrm[:, j, 0:1], nrm[:, j, 1:2], ALU.mult).then_inc(w_chain, 1)
                await_ge(rot_done, t + 1)
                nc.gpsimd.tensor_tensor(ph[:, j, D:D + ROT], rot[:, 0, :], rot[:, 1, :], ALU.add).then_inc(tab_done, 1)
                await_ge(w_chain, t + 1)
                if not first:
                    await_ge(acc_done_t, t - G + 1)
                nc.gpsimd.tensor_tensor(wtok[:, j:j + 1], wprod[:, j:j + 1], mhalf[:, 0:1], ALU.pow).then_inc(w_ready, 1)

            rstd_of(1, 0, G)
            s2_of(1, 0, G)
            rstd_of(2, G, 2 * G)
            s2_of(2, G, 2 * G)
            pool.wait_ge(trg_in, 16)
            pool.wait_ge(sw_hi, 1)
            nc.gpsimd.tensor_tensor(swg_s[:, :, 1, :], swg[:, :, :], f(swg_s[:, :, 0, :]), ALU.subtract).then_inc(sw_lo, 1)
            rotate(0, 0, 0, True)
            rstd_of(3, 2 * G, TILES)
            rotate(0, 1, 0, True)
            s2_of(3, 2 * G, TILES)
            rotate(0, 2, 0, True)
            pool.wait_ge(sw_hi, 2)
            nc.gpsimd.tensor_tensor(swu_s[:, :, 1, :], swu[:, :, :], f(swu_s[:, :, 0, :]), ALU.subtract).then_inc(sw_lo, 1)
            rotate(0, 3, 0, True)
            with pool.Fori(1, GROUPS) as g:
                for j in range(G):
                    rotate(g, j, g & (GROUPS_B - 1), False)

            def a_link(ins, n):
                ins.then_inc(a_pool, 1)
                pool.wait_ge(a_pool, n)

            pool.wait_ge(ab_done, BATCH)
            a_link(nc.gpsimd.tensor_tensor(aq[:, :, :], ab[:, :, 0:HALF], ab[:, :, HALF:ROT], ALU.add), 1)
            a_link(nc.gpsimd.tensor_tensor(af[:, :, :], ab[:, :, D:D + HALF], ab[:, :, D + HALF:D + ROT], ALU.add), 2)
            a_link(nc.gpsimd.tensor_scalar(aq[:, :, :], aq[:, :, :], 0.25, 0.5, ALU.mult, ALU.add), 3)
            nc.gpsimd.tensor_scalar(arow[:, :, ROT:D], ab[:, :, ROT:D], 0.5, 0.5, ALU.mult, ALU.add).then_inc(arow_done, 1)
            nc.gpsimd.tensor_tensor(arow[:, :, 0:HALF], aq[:, :, :], af[:, :, :], ALU.add).then_inc(arow_done, 1)
            nc.gpsimd.tensor_tensor(arow[:, :, HALF:ROT], aq[:, :, :], af[:, :, :], ALU.subtract).then_inc(arow_done, 1)
            pool.wait_ge(sw_hi, 4)
            nc.gpsimd.tensor_tensor(swd_s[:, 0:2, 1, :], swd[:, 0:2, :], f(swd_s[:, 0:2, 0, :]), ALU.subtract).then_inc(sw_lo, 1)
            nc.gpsimd.tensor_tensor(swd_s[0:SC[2], 2, 1, :], swd[0:SC[2], 2, :], f(swd_s[0:SC[2], 2, 0, :]), ALU.subtract).then_inc(sw_lo, 1)

            await_ge(onehot_done, 1)
            nc.gpsimd.tensor_tensor(oat[:, :, :, :].rearrange("p t a e -> p t (a e)"), oa[:, :, :, :].rearrange("p t a e -> p t (a e)"),
                                    tok16[:, :].unsqueeze(2).to_broadcast([P, TILES, E * SLOT_A]),
                                    ALU.mult).then_inc(oa_done, 1)

            def gather(e, j, first):
                nc.gpsimd.tensor_copy(idx_g[:, j:j + 1], idx[:, bass.ds(e, 1)]).then_inc(idx_copied, 1)
                await_ge(idx_copied, e + 1 if first else 2 * e - 3)
                nc.gpsimd.indirect_dma_start(out=xg[:, j, :], out_offset=None, in_=rows,
                                             in_offset=bass.IndirectOffsetOnAxis(ap=idx_g[:, j:j + 1], axis=0)).then_inc(gath[j], 16)

            def scatter(e, j, last):
                if not (isinstance(e, int) and e == 0):
                    await_ge(scat_done, 16 * e)
                nc.gpsimd.tensor_copy(idx_s[:, j:j + 1], idx[:, bass.ds(e, 1)]).then_inc(idx_copied, 1)
                await_ge(idx_copied, (E + 1 + e) if last else (2 * e + G + 2))
                nc.gpsimd.indirect_dma_start(out=ysum, out_offset=bass.IndirectOffsetOnAxis(ap=idx_s[:, j:j + 1], axis=0),
                                             in_=eo[:, j, :], in_offset=None, compute_op=ALU.add).then_inc(scat_done, 16)

            await_ge(idx_done, 1)
            await_ge(rows_ready, 1)
            for j in range(G):
                gather(j, j, True)

            def moe_body(h, last=False):
                for j in range(G):
                    e = h * G + j
                    await_ge(eo_done, e + 1)
                    if not last:
                        gather(e + G, j, False)
                    scatter(e, j, last)

            moe_body(0)
            with pool.Fori(1, E // G - 1) as h:
                moe_body(h)
            moe_body(E // G - 1, last=True)

            def add_y(g):
                pool.wait_ge(y_in[g], 16)
                for j in range(0, G, 2):
                    t = g * G + j
                    pool.wait_ge(half_done, t + 1)
                    nc.gpsimd.tensor_tensor(sh[:, t, :], sh[:, t, :], yin[g][:, j, :], ALU.add).then_inc(ot_pool, 1)

            add_y(0)
            add_y(1)
            pool.wait_ge(xn_in, 16 * GROUPS)
            pool.wait_ge(y_in[GROUPS - 1], 16)
            for q in range(2):
                pair = slice(2 * q, 2 * q + 2)
                nc.gpsimd.tensor_tensor(xn[:, pair, :], xn[:, pair, :], yin[GROUPS - 1][:, pair, :], ALU.add).then_inc(yx_done, 1)
            add_y(2)

        @block.scalar
        def _(act):
            act.dma_start(cst[:, :], consts).then_inc(cst_in, 16)
            act.dma_start(gb_cols[:, :], gb).then_inc(wi_in, 16)
            act.dma_start(bias_row[:, :], bias).then_inc(wi_in, 16)
            def hi(g, j, first):
                t = g * G + j
                if not first:
                    act.wait_ge(kv_done, t - G + 1)
                    act.wait_ge(xt_saved[j // 2], g * 16)
                act.wait_ge(t_done, t + 1)
                nc.scalar.activation(hl[:, j, 0, :, :], bank[4 + j % 2][:, 0:D].rearrange("p (c n) -> p c n", c=DC),
                                     ACT.Copy).then_inc(hi_done, 1)

            def ones_rows(g):
                act.wait_ge(ibt_done, g + 1)
                if g == 0:
                    nc.scalar.activation(ib[:, :, :], bank[2][0:3, :].rearrange("p (j n) -> p j n", j=G), ACT.Copy).then_inc(ib_set, 1)
                nc.scalar.activation(ib_all[:, g * G:(g + 1) * G, :], bank[2 + g % 2][0:3, :].rearrange("p (j n) -> p j n", j=G), ACT.Copy).then_inc(ib_done, 1)

            def values(g, j, first):
                t = g * G + j
                if not (first and j < 2):
                    act.wait_ge(ix_done, t - 1)
                act.wait_ge(kv_done, t + 1)
                nc.scalar.activation(kv[:, j % 2, D:KVR], bank[6 + j % 2][:, 0:D + E], ACT.Copy).then_inc(v_done, 1)
                nc.scalar.activation(kv[:, j % 2, 0:D], bank[j % 2][:, 0:D], ACT.Copy).then_inc(v_done, 1)
                if not first:
                    act.wait_ge(w_chain, t - G + 1)
                if not (first and j == 0):
                    act.wait_ge(sq_done, 2 * t)
                nc.scalar.activation(junk[:, 0, :], bank[j % 2][:, 0:D], ACT.Square, accum_out=nrm[:, j, 0:1]).then_inc(sq_done, 1)
                nc.scalar.activation(junk[:, 1, :], bank[6 + j % 2][:, 0:D], ACT.Square, accum_out=nrm[:, j, 1:2]).then_inc(sq_done, 1)

            def body(g, first=False, last=False):
                for j in range(G):
                    if j < 2:
                        hi(g, j + 2, first)
                    elif not last:
                        hi(g + 1, j - 2, False)
                    if first and j == 0:
                        ones_rows(0)
                    if first and j == 3:
                        ones_rows(1)
                    values(g, j, first)
                    if first and j == 3:
                        ones_rows(2)
                        ones_rows(3)
                    if (first and j < 2) or (last and j >= 2):
                        if j == 0:
                            act.wait_ge(sw_in, 64)
                        w_s, w, n, c = ((swg_s, swg, P, slice(0, 2)), (swu_s, swu, P, slice(0, 2)), (swd_s, swd, P, slice(0, 2)),
                                        (swd_s, swd, SC[2], slice(2, 3)))[j]
                        nc.scalar.activation(w_s[0:n, c, 0, :], w[0:n, c, :], ACT.Copy).then_inc(sw_hi, 1)

            hi(0, 0, True)
            hi(0, 1, True)
            act.wait_ge(wi_in, 48)
            for c in range(DC):
                nc.scalar.activation(wkv_s[:, c, 0, :], wi[:, c, D:3 * D], ACT.Copy, scale=gam[:, c:c + 1]).then_inc(act_prep, 1)
            nc.scalar.activation(gt_s[:, :, 0, :], gt[:, :, :], ACT.Copy).then_inc(act_prep, 1)
            act.wait_ge(pe_prep, 1)
            nc.scalar.activation(b3h[:, :], bank[3][0:3, :], ACT.Copy).then_inc(act_prep, 1)
            act.wait_ge(act_prep, 4)
            nc.scalar.activation(b3u[:, :], f(b3h[:, :]), ACT.Copy, scale=cst[0:3, C_ROW + 1:C_ROW + 2]).then_inc(act_prep, 1)
            body(0, first=True)
            with act.Fori(1, GROUPS - 1) as g:
                body(g)
            body(GROUPS - 1, last=True)

            def shared(g, c, pair):
                n, k, q = SC[c], c % 2, g * 3 + c
                if not (isinstance(g, int) and q < 2):
                    act.wait_ge(sm_done, q - 1 if c else q)
                act.wait_ge(sh_done, q + 1)
                nc.scalar.activation(sg[0:n, k, :], bank[pair][0:n, :], ACT.Silu).then_inc(sg_done, 1)
                act.wait_ge(sm_done, q + 1)
                if not (isinstance(g, int) and g == 0):
                    act.wait_ge(dn_done, 2 * g)
                nc.scalar.activation(smid_s[0:n, c, 0, :], smid[0:n, k, :], ACT.Copy).then_inc(hi_m, 1)

            act.wait_ge(red_done, 1)
            for b in range(BATCH):
                nc.scalar.activation(ab[:, b, :], bank[2 + b][0:1, 0:D + ROT], ACT.Copy).then_inc(ab_done, 1)
            act.wait_ge(lm_done, 1)
            nc.scalar.activation(ex[:, :, :], ex[:, :, :], ACT.Exp).then_inc(exp_done, 1)
            for c in range(3):
                shared(0, c, GAP_PAIR[c])
            for b in range(BATCH):
                for c in range(DC):
                    act.wait_ge(m_done, b * DC + c + 1)
                    nc.scalar.activation(m_s[:, b, c, 0, :], bank[2 + b * DC + c][:, 0:D], ACT.Copy, scale=gam[:, c:c + 1]).then_inc(m_hi, 1)

            def evac(e, k):
                if not (isinstance(e, int) and e < 2):
                    act.wait_ge(gu_done, e - 1)
                act.wait_ge(xt_e, e + 1)
                nc.scalar.activation(xgt[:, k, :, :], bank[4 + k][:, 0:D].rearrange("p (c n) -> p c n", c=DC),
                                     ACT.Copy).then_inc(xgt_done, 1)

            def silu(e, k):
                if not (isinstance(e, int) and e < 2):
                    act.wait_ge(mid_done, 2 * (e - 1))
                act.wait_ge(gu_done, e + 1)
                nc.scalar.activation(sil[:, k, 0, :], bank[k][:, 0:P], ACT.Silu).then_inc(silu_done, 1)
                nc.scalar.activation(sil[0:I2, k, 1, :], bank[k][0:I2, 2 * P:3 * P], ACT.Silu).then_inc(silu_done, 1)

            def moe_body(h, first=False, last=False):
                for j in range(G):
                    e = h * G + j
                    if not (last and j == G - 1):
                        evac(e + 1, (j + 1) % 2)
                    silu(e, j % 2)
                    if not first and not last and j < 3:
                        shared(h, j, 6)

            act.wait_ge(c_done, 1)
            nc.scalar.activation(c3h[:, :, :], bank[7][0:3, :].rearrange("p (b n) -> p b n", b=BATCH), ACT.Copy).then_inc(c3_chain, 1)
            act.wait_ge(c3_chain, 1)
            nc.scalar.activation(c3u[:, :, :], f(c3h[:, :, :]), ACT.Copy, scale=cst[0:3, C_ROW + 1:C_ROW + 2]).then_inc(c3_chain, 1)

            evac(0, 0)
            moe_body(0, first=True)
            with act.Fori(1, E // G - 1) as h:
                moe_body(h)
            moe_body(E // G - 1, last=True)
            for c in range(3):
                shared(GROUPS - 1, c, 6)

        @block.vector
        def _(dve):
            def stats(g):
                dve.wait_ge(x_in[g], 16)
                if g > 0:
                    dve.wait_ge(st_chain, g * 8)
                for j in range(G):
                    nc.vector.bn_stats(st6[:, j, :], x_all[:, g * G + j, :]).then_inc(st_chain, 1)
                dve.wait_ge(st_chain, g * 8 + G)
                for j in range(G):
                    nc.vector.bn_aggr(mv[:, g * G + j, :], st6[:, j, :]).then_inc(st_chain, 1)
                dve.wait_ge(st_chain, g * 8 + 8)
                nc.vector.tensor_scalar(lt[:, 0, g * G:(g + 1) * G], mv[:, g * G:(g + 1) * G, 1], EPS, None, ALU.add).then_inc(stats_done, 1)

            def second_var(k, a, b):
                dve.wait_ge(ln_ready, k)
                nc.vector.tensor_tensor(lt[:, 1, a:b], rstd[:, a:b], rstd[:, a:b], ALU.mult).then_inc(v2_chain, 1)
                dve.wait_ge(v2_chain, 2 * k - 1)
                nc.vector.tensor_tensor(lt[:, 2, a:b], lt[:, 1, a:b], mv[:, a:b, 1], ALU.mult).then_inc(v2_chain, 1)
                dve.wait_ge(v2_chain, 2 * k)
                nc.vector.tensor_scalar(lt[:, 3, a:b], lt[:, 2, a:b], EPS, None, ALU.add).then_inc(v2_ready, 1)

            def inverse(k, a, b):
                dve.wait_ge(s2_ready, k)
                nc.vector.tensor_tensor(lt[:, 0, a:b], lt[:, 3, a:b], s2[:, a:b], ALU.mult).then_inc(i3_chain, 1)
                dve.wait_ge(i3_chain, 2 * k - 1)
                nc.vector.tensor_copy(ihi[:, a:b], lt[:, 0, a:b]).then_inc(i3_chain, 1)
                dve.wait_ge(i3_chain, 2 * k)
                nc.vector.tensor_copy(i3[:, a:b, 0:2], f(ihi[:, a:b]).unsqueeze(2).to_broadcast([P, b - a, 2])).then_inc(i3_ready, 1)
                nc.vector.tensor_tensor(i3[:, a:b, 2], lt[:, 0, a:b], f(ihi[:, a:b]), ALU.subtract).then_inc(i3_ready, 1)

            def norm(g, j, first):
                t = g * G + j
                dve.wait_ge(ln_ready, 1 if first else 2 if isinstance(g, int) and g == 1 else 3)
                if not first:
                    dve.wait_ge(t_done, t - G + 1)
                    dve.wait_ge(xn_saved[j // 2], g * 16)
                nc.vector.tensor_scalar(xn[:, j, :], x_all[:, t, :], mv[:, bass.ds(t, 1), 0], rstd[:, bass.ds(t, 1)],
                                        ALU.subtract, ALU.mult).then_inc(norm_done, 1)

            def lo(g, j, first):
                t = g * G + j
                dve.wait_ge(hi_done, t + 1)
                nc.vector.tensor_tensor(hl[:, j, 1, :, :], bank[4 + j % 2][:, 0:D].rearrange("p (c n) -> p c n", c=DC),
                                        f(hl[:, j, 0, :, :]), ALU.subtract).then_inc(lo_done, 1)

            def products(g, j, first):
                t = g * G + j
                if not first:
                    dve.wait_ge(acc_done_t, t - G + 1)
                if j == 0 and not first:
                    dve.wait_ge(top_kept, 2 * g)
                dve.wait_ge(v_done, 2 * t + 2)
                k_, v_, r_ = kv[:, j % 2, 0:D], kv[:, j % 2, D:2 * D], kv[:, j % 2, 2 * D:KVR]
                nc.vector.tensor_scalar(lg[:, bass.ds(t, 1), :], r_.unsqueeze(1), 0.0, None, ALU.add).then_inc(lg_kept, 1)
                nc.vector.max(mx[:, j, :], r_).then_inc(mx_done, 1)
                v2 = v_[:, 0:ROT].rearrange("p (a n) -> p a n", a=2)[:, ::-1, :]
                nc.vector.tensor_tensor(ph[:, j, D:D + ROT].rearrange("p (a n) -> p a n", a=2),
                                        k_[:, 0:ROT].rearrange("p (a n) -> p a n", a=2), v2, ALU.mult).then_inc(prod_done, 1)
                dve.wait_ge(mx_done, t + 1)
                nc.vector.tensor_tensor(ph[:, j, 0:D], k_, v_, ALU.mult).then_inc(prod_done, 1)
                nc.vector.max_index(ix[:, j, :], mx[:, j, :], r_).then_inc(ix_done, 1)

            def accumulate(g, j, b, first):
                t = g * G + j
                dve.wait_ge(acc_done_t, t) if not (first and j == 0) else dve.wait_ge(acc_zero, 1)
                dve.wait_ge(tab_done, t + 1)
                dve.wait_ge(w_ready, t + 1)
                nc.vector.scalar_tensor_tensor(acc[:, b, :], ph[:, j, :], wtok[:, j:j + 1], acc[:, b, :], ALU.mult, ALU.add).then_inc(acc_done_t, 1)

            def keep_top(g):
                dve.wait_ge(mx_done, g * G + G)
                nc.vector.tensor_scalar(top1[:, bass.ds(g * G, G)], mx[:, :, 0], 0.0, None, ALU.add).then_inc(top_kept, 1)
                dve.wait_ge(ix_done, g * G + G)
                nc.vector.tensor_scalar(ixf[:, bass.ds(g * G, G), :], ix[:, :, 0:TOP], 0.0, None, ALU.add).then_inc(top_kept, 1)

            def body(g, first=False, second=False, last=False):
                batch = (lambda k: k // GROUPS_B) if isinstance(g, int) else (lambda k: bass.ds((k >> 1) & 1, 1))
                for j in range(G):
                    if j < 2:
                        lo(g, j + 2, first)
                    elif not last:
                        lo(g + 1, j - 2, False)
                    products(g, j, first)
                    if not last:
                        norm(g + 1, j, False)
                    if j < 2 and not first:
                        accumulate(g - 1, j + 2, batch(g - 1), second)
                    if j >= 2:
                        accumulate(g, j - 2, batch(g), first)
                    if j == 3:
                        keep_top(g)
                    if first and j == 0:
                        stats(3)
                    if first and j == 1:
                        second_var(3, 2 * G, TILES)
                    if first and j == 2:
                        inverse(3, 2 * G, TILES)

            stats(0)
            nc.vector.memset(ones3[:, :], 1.0).then_inc(ones_set, 1)
            nc.vector.memset(one16[:, :], 1.0).then_inc(ones_set, 1)
            nc.vector.memset(one_col[:, :], 1.0).then_inc(ones_set, 1)
            nc.vector.memset(acc[:, :, :], 0.0).then_inc(acc_zero, 1)
            for j in range(G):
                norm(0, j, True)
            second_var(1, 0, G)
            dve.wait_ge(wi_in, 48)
            nc.vector.tensor_copy(bet3[:, :, :], bet[:, :].unsqueeze(2).to_broadcast([P, DC, 3])).then_inc(ones_set, 1)
            lo(0, 0, True)
            lo(0, 1, True)
            for c in range(DC):
                dve.wait_ge(act_prep, c + 1)
                nc.vector.scalar_tensor_tensor(wkv_s[:, c, 1, :], wi[:, c, D:3 * D], gam[:, c:c + 1], f(wkv_s[:, c, 0, :]),
                                               ALU.mult, ALU.subtract).then_inc(prep_done, 1)
            inverse(1, 0, G)
            stats(1)
            dve.wait_ge(act_prep, 3)
            nc.vector.tensor_tensor(gt_s[:, :, 1, :], gt[:, :, :], f(gt_s[:, :, 0, :]), ALU.subtract).then_inc(prep_done, 1)
            dve.wait_ge(cst_in, 16)
            dve.wait_ge(act_prep, 5)
            nc.vector.scalar_tensor_tensor(b3[:, 0:2 * D], bank[3][0:3, :], cst[0:3, C_ROW:C_ROW + 1], b3u[:, :],
                                           ALU.mult, ALU.add).then_inc(prep_done, 1)
            nc.vector.tensor_scalar(b3[:, 2 * D:KVR], cst[0:3, C_I16:C_I16 + E], 0.0, None, ALU.mult).then_inc(prep_done, 1)
            second_var(2, G, 2 * G)
            stats(2)
            inverse(2, G, 2 * G)
            nc.vector.tensor_copy(iota_b[:, :, :], cst[:, C_I16:C_I16 + E].unsqueeze(2).to_broadcast([P, SLOT_B, E])).then_inc(const_done, 1)
            nc.vector.tensor_copy(iota_k[:, :, :], cst[:, C_I16:C_I16 + E].unsqueeze(2).to_broadcast([P, E, TOP])).then_inc(const_done, 1)
            nc.vector.tensor_copy(tri16[:, :], cst[:, C_TRI:C_TRI + P]).then_inc(const_done, 1)
            nc.vector.tensor_copy(exp16[:, :], cst[:, C_EXP:C_EXP + E]).then_inc(const_done, 1)
            nc.vector.tensor_copy(tok16[:, :], cst[:, C_TOK:C_TOK + TILES]).then_inc(const_done, 1)
            body(0, first=True)
            body(1, second=True)
            with dve.Fori(2, GROUPS - 1) as g:
                body(g)
            body(GROUPS - 1, last=True)
            for j in (2, 3):
                accumulate(GROUPS - 1, j, BATCH - 1, False)

            chain = [0]

            def link(ins):
                chain[0] += 1
                ins.then_inc(r_chain, 1)
                dve.wait_ge(r_chain, chain[0])

            def shared_mid(g, c, pair):
                n, k, q = SC[c], c % 2, g * 3 + c
                if not (isinstance(g, int) and q < 2):
                    dve.wait_ge(lo_m, q - 1 if c else q)
                dve.wait_ge(sg_done, q + 1)
                nc.vector.tensor_tensor(smid[0:n, k, :], sg[0:n, k, :], bank[pair + 1][0:n, :], ALU.mult).then_inc(sm_done, 1)

            def shared_lo(g, c):
                n, k, q = SC[c], c % 2, g * 3 + c
                dve.wait_ge(hi_m, q + 1)
                nc.vector.tensor_tensor(smid_s[0:n, c, 1, :], smid[0:n, k, :], f(smid_s[0:n, c, 0, :]), ALU.subtract).then_inc(lo_m, 1)

            def keep(g, pair):
                dve.wait_ge(xn_in, 16 * g + 16)
                for q in range(2):
                    dve.wait_ge(dn_done, 2 * g + q + 1)
                    nc.vector.tensor_tensor(sh[:, bass.ds(g * G + 2 * q, 2), :], xn[:, 2 * q:2 * q + 2, :],
                                            bank[pair + q][:, :].rearrange("p (j n) -> p j n", j=2), ALU.add).then_inc(kept, 1)

            dve.wait_ge(lg_kept, TILES)
            dve.wait_ge(top_kept, 2 * GROUPS)
            dve.wait_ge(const_done, 5)
            link(nc.vector.tensor_tensor(eq[:, :, :, :], ixf[:, :, :].unsqueeze(2).to_broadcast([P, TILES, E, TOP]),
                                         iota_k[:, :, :].unsqueeze(1).to_broadcast([P, TILES, E, TOP]), ALU.is_equal))
            with nc.allow_low_precision("a sum of four zeros and ones"):
                nc.vector.tensor_reduce(mask16[:, :, :], eq[:, :, :, :], axis=AX.X, op=ALU.add).then_inc(mask_done, 1)
            nc.vector.tensor_tensor(ex[:, :, :], lg[:, :, :], top1[:, :].unsqueeze(2).to_broadcast([P, TILES, E]), ALU.subtract).then_inc(lm_done, 1)

            dve.wait_ge(mask_done, 1)
            dve.wait_ge(rank_done, 1)
            link(nc.vector.scalar_tensor_tensor(rank[:, :, :], mask16[:, :, :], -1024.0, bank[7][:, 0:TILES * E].rearrange("p (t e) -> p t e", t=TILES),
                                                ALU.mult, ALU.add))
            link(nc.vector.tensor_scalar(rank_i[:, :, :], rank[:, :, :], 1024.0, None, ALU.add))
            link(nc.vector.tensor_scalar(ra_i[:, :, :], rank_i[:, :, :], 4, None, ALU.logical_shift_right))
            link(nc.vector.tensor_copy(ra[:, :, :], ra_i[:, :, :]))
            dve.wait_ge(x_saved, 16)
            nc.vector.tensor_tensor(oa[:, :, :, :], ra[:, :, :].unsqueeze(2).to_broadcast([P, TILES, SLOT_A, E]),
                                    iota_b[:, 0:SLOT_A, :].unsqueeze(1).to_broadcast([P, TILES, SLOT_A, E]),
                                    ALU.is_equal).then_inc(onehot_done, 1)
            link(nc.vector.tensor_scalar(rb_i[:, :, :], rank_i[:, :, :], SLOT_B - 1, None, ALU.bitwise_and))
            link(nc.vector.tensor_copy(rb[:, :, :], rb_i[:, :, :]))
            nc.vector.tensor_tensor(ob[:, :, :, :], rb[:, :, :].unsqueeze(2).to_broadcast([P, TILES, SLOT_B, E]),
                                    iota_b[:, :, :].unsqueeze(1).to_broadcast([P, TILES, SLOT_B, E]),
                                    ALU.is_equal).then_inc(onehot_done, 1)
            shared_mid(0, 0, GAP_PAIR[0])
            dve.wait_ge(exp_done, 1)
            link(nc.vector.tensor_reduce(zsum[:, :], ex[:, :, :], axis=AX.X, op=ALU.add))
            link(nc.vector.tensor_tensor(em[:, :, :], ex[:, :, :], mask16[:, :, :], ALU.mult))
            link(nc.vector.tensor_reduce(esum[:, :], em[:, :, :], axis=AX.X, op=ALU.add))
            link(nc.vector.scalar_tensor_tensor(esum[:, :], zsum[:, :], 1e-20, esum[:, :], ALU.mult, ALU.add))
            link(nc.vector.reciprocal(einv[:, :], esum[:, :]))
            nc.vector.tensor_tensor(wd[:, :, :], em[:, :, :], einv[:, :].unsqueeze(2).to_broadcast([P, TILES, E]), ALU.mult).then_inc(wd_done, 1)
            dve.wait_ge(table_done, 1)
            link(nc.vector.tensor_tensor(diag[:, :, :], bank[6][:, 0:E * SLOT_B].rearrange("p (b e) -> p b e", e=E),
                                         cst[:, C_EXP:C_EXP + E].unsqueeze(1).to_broadcast([P, SLOT_B, E]), ALU.mult))
            link(nc.vector.tensor_reduce(tb[:, :], diag[:, :, :], axis=AX.X, op=ALU.add))
            nc.vector.tensor_tensor(spread[:, :, :], tb[:, :].unsqueeze(1).to_broadcast([P, SLOT_A, SLOT_B]),
                                    cst[:, C_ASEL:C_ASEL + SLOT_A].unsqueeze(2).to_broadcast([P, SLOT_A, SLOT_B]), ALU.mult).then_inc(spread_done, 1)
            shared_lo(0, 0)
            dve.wait_ge(acol_done, 1)
            link(nc.vector.tensor_copy(acol[:, :], bank[2][:, 384:384 + BATCH * DC]))
            nc.vector.tensor_copy(bq3[:, :, :], bank[2][:, 392:392 + DC * 3].rearrange("p (c k) -> p c k", c=DC)).then_inc(aw_done, 1)
            dve.wait_ge(mix_in, 32)
            for b in range(BATCH):
                for c in range(DC):
                    nc.vector.tensor_scalar(aw[:, b, c, :], wo[:, c, :], acol[:, b * DC + c:b * DC + c + 1], None, ALU.mult).then_inc(aw_done, 1)
            dve.wait_ge(slot_done, 1)
            link(nc.vector.tensor_copy(slot_v[:, :], bank[6][:, 256:256 + E]))
            link(nc.vector.tensor_scalar(slot_e[:, :], slot_v[:, :], 0.0, cst[:, C_SPARE:C_SPARE + 1], ALU.is_equal, ALU.mult))
            link(nc.vector.tensor_tensor(slot_f[:, :], slot_v[:, :], slot_e[:, :], ALU.add))
            nc.vector.tensor_scalar(idx[:, :], slot_f[:, :], -1.0, None, ALU.add).then_inc(idx_done, 1)
            shared_mid(0, 1, GAP_PAIR[1])
            shared_lo(0, 1)
            shared_mid(0, 2, GAP_PAIR[2])
            shared_lo(0, 2)
            for b in range(BATCH):
                for c in range(DC):
                    dve.wait_ge(m_hi, b * DC + c + 1)
                    nc.vector.scalar_tensor_tensor(m_s[:, b, c, 1, :], bank[2 + b * DC + c][:, 0:D], gam[:, c:c + 1], f(m_s[:, b, c, 0, :]),
                                                   ALU.mult, ALU.subtract).then_inc(m_lo, 1)
            keep(0, 0)

            def gated(e, k):
                if not (isinstance(e, int) and e < 2):
                    dve.wait_ge(d_done, e - 1)
                dve.wait_ge(silu_done, 2 * e + 2)
                nc.vector.tensor_tensor(mid[:, k, 0, :], sil[:, k, 0, :], bank[k][:, P:2 * P], ALU.mult).then_inc(mid_done, 1)
                nc.vector.tensor_tensor(mid[0:I2, k, 1, :], sil[0:I2, k, 1, :], bank[k][UP2:UP2 + I2, 2 * P:3 * P], ALU.mult).then_inc(mid_done, 1)

            def weigh(eh, j, first):
                e = eh * G + j
                if not first:
                    dve.wait_ge(scat_done, 16 * (e - G + 1))
                dve.wait_ge(d_done, e + 1)
                nc.vector.tensor_scalar(eo[:, j, :], bank[2 + j % 2][:, 0:D], xg[:, j, bass.ds(D + e, 1)], None, ALU.mult).then_inc(eo_done, 1)

            def mix(t):
                dve.wait_ge(kept, 2 * (t // G) + 2)
                dve.wait_ge(att_done, t + 1)
                nc.vector.scalar_tensor_tensor(sh[:, t, :], bank[MIX_BANK[t]][:, 0:D], s2[:, t:t + 1], sh[:, t, :], ALU.mult, ALU.add).then_inc(half_done, 1)

            def moe_body(h, first=False, second=False, last=False):
                for j in range(G):
                    e = h * G + j
                    early = first or (second and j == 0)
                    gated(e, j % 2)
                    if not (first and j == 0):
                        weigh(h + (j - 1) // G, (j - 1) % G, early)
                    if first and j == 0:
                        dve.wait_ge(c3_chain, 2)
                        nc.vector.scalar_tensor_tensor(c3[:, :, :], bank[7][0:3, :].rearrange("p (b n) -> p b n", b=BATCH), cst[0:3, C_ROW:C_ROW + 1],
                                                       c3u[:, :, :], ALU.mult, ALU.add).then_inc(c3_done, 1)
                    for t in MIX_FIRST[j] if first else MIX_LAST[j] if last else ():
                        mix(t)
                    if not first and not last:
                        if j < 3:
                            shared_mid(h, j, 6)
                            shared_lo(h, j)
                        else:
                            keep(h, 6)

            moe_body(0, first=True)
            moe_body(1, second=True)
            with dve.Fori(2, E // G - 1) as h:
                moe_body(h)
            moe_body(E // G - 1, last=True)
            weigh(E // G - 1, G - 1, False)

            def add_y(g):
                dve.wait_ge(y_in[g], 16)
                for j in (1, 3):
                    t = g * G + j
                    dve.wait_ge(half_done, t + 1)
                    nc.vector.tensor_tensor(sh[:, t, :], sh[:, t, :], yin[g][:, j, :], ALU.add).then_inc(ot_dve, 1)

            last_g = GROUPS - 1
            for c in range(3):
                shared_mid(last_g, c, 6)
                shared_lo(last_g, c)
                for t in MIX_CHUNK[c]:
                    if t < last_g * G:
                        mix(t)
            for g in range(last_g):
                add_y(g)
            for j in range(G):
                t = last_g * G + j
                dve.wait_ge(yx_done, j // 2 + 1)
                dve.wait_ge(att_done, t + 1)
                nc.vector.scalar_tensor_tensor(sh[:, t, :], bank[MIX_BANK[t]][:, 0:D], s2[:, t:t + 1], xn[:, j, :], ALU.mult, ALU.add).then_inc(half_done, 1)
            for q in range(2):
                t = last_g * G + 2 * q
                dve.wait_ge(half_done, t + 2)
                dve.wait_ge(dn_done, 2 * last_g + q + 1)
                nc.vector.tensor_tensor(sh[:, t:t + 2, :], sh[:, t:t + 2, :], bank[6 + q][:, :].rearrange("p (j n) -> p j n", j=2), ALU.add).then_inc(kept, 1)

        @block.tensor
        def _(pe):
            ident = cst[:, C_ID:C_ID + P]
            pe.wait_ge(zero_set, 1)
            for _ in range(WARM_UP):
                nc.tensor.matmul(bank[6][:, 0:ROW], zero[:, 0:P], zero[:, :], start=True, stop=True)

            def turn(g, j, first):
                t = g * G + j
                pe.wait_ge(norm_done, t + 1)
                if not (first and j < 2):
                    pe.wait_ge(lo_done, t - 1)
                for c in range(DC):
                    last = nc.tensor.transpose(bank[4 + j % 2][:, c * P:(c + 1) * P], xn[:, j, c * P:(c + 1) * P], ident)
                last.then_inc(t_done, 1)

            def turn_rows(g):
                pe.wait_ge(i3_ready, min(2 * g + 2, 6))
                if g == 1:
                    pe.wait_ge(prep_done, 4)
                if g >= 2:
                    pe.wait_ge(ib_done, g - 1)
                for j in range(G):
                    last = nc.tensor.transpose(bank[2 + g % 2][0:3, j * P:(j + 1) * P], i3[:, g * G + j, :], ident)
                last.then_inc(ibt_done, 1)

            def keys(g, j, first):
                t = g * G + j
                if not (first and j < 2):
                    pe.wait_ge(sq_done, 2 * t - 2)
                pe.wait_ge(lo_done, t + 1)
                if first and j == 0:
                    pe.wait_ge(prep_done, 3)
                halves = ((bank[j % 2][:, 0:D], slice(0, D)), (bank[6 + j % 2][:, 0:D + E], slice(D, KVR)))
                for dst, n in halves:
                    for c in range(DC):
                        mm3(dst, hl[:, j, 0, c, :], hl[:, j, 1, c, :], wkvr_s[:, c, 0, n], wkvr_s[:, c, 1, n], c == 0, False)
                if first and j == 0:
                    pe.wait_ge(ib_set, 1)
                if not first and j % 2 == 0:
                    pe.wait_ge(ib_in[j // 2], 16 * g)
                if first and j == 0:
                    pe.wait_ge(prep_done, 5)
                for dst, n in halves:
                    last = nc.tensor.matmul(dst, ib[:, j, :], b3[:, n], start=False, stop=True)
                last.then_inc(kv_done, 1)

            def body(g, first=False, last=False):
                for j in range(G):
                    if j < 2:
                        turn(g, j + 2, first)
                    elif not last:
                        turn(g + 1, j - 2, False)
                    keys(g, j, first)
                    if first and j == 2:
                        turn_rows(1)
                    if first and j == 3:
                        turn_rows(2)
                        turn_rows(3)

            pe.wait_ge(cst_in, 16)
            turn(0, 0, True)
            turn(0, 1, True)
            pe.wait_ge(ones_set, 4)
            pe.wait_ge(wi_in, 48)
            for c in range(DC):
                nc.tensor.matmul(bank[3][0:3, :], bet3[:, c, :], wi[:, c, D:3 * D], start=c == 0, stop=False)
            nc.tensor.matmul(bank[3][0:3, :], ones3[:, 0:3], bin_row[:, D:3 * D], start=False, stop=True).then_inc(pe_prep, 1)
            turn_rows(0)
            body(0, first=True)
            with pe.Fori(1, GROUPS - 1) as g:
                body(g)
            body(GROUPS - 1, last=True)
            pe.wait_ge(ib_done, GROUPS)
            for c in range(DC):
                for k in range(DC):
                    nc.tensor.matmul(bank[2][:, 392 + c * 3:395 + c * 3], wi[:, k, c * P:(c + 1) * P], bet3[:, k, :], start=k == 0, stop=False)
                nc.tensor.matmul(bank[2][:, 392 + c * 3:395 + c * 3], bin_row[:, c * P:(c + 1) * P], ones3[:, 0:3], start=False, stop=True)
            def shared(g, c, pair):
                n, q = SC[c], g * 3 + c
                if not isinstance(g, int) or g > 0:
                    pe.wait_ge(sm_done, q)
                if not (isinstance(g, int) and g == 0) and c == 0:
                    pe.wait_ge(kept, 2 * g)
                for w_s, dst in ((swg_s, bank[pair]), (swu_s, bank[pair + 1])):
                    for d in range(DC):
                        xr = xt_all[:, bass.ds(g * G, G), :, d, :]
                        last = mm3(dst[0:n, :].rearrange("p (t n) -> p t n", n=P), w_s[:, d, 0, c * P:c * P + n], w_s[:, d, 1, c * P:c * P + n],
                                   xr[:, :, 0, :], xr[:, :, 1, :], d == 0, d == DC - 1)
                last.then_inc(sh_done, 1)

            def shared_down(g, pair):
                pe.wait_ge(sg_done, g * 3 + 3)
                for j in range(G):
                    for c in range(3):
                        n = SC[c]
                        if j == 0:
                            pe.wait_ge(lo_m, g * 3 + c + 1)
                        last = mm3(bank[pair + j // 2][:, j % 2 * D:(j % 2 + 1) * D], smid_s[0:n, c, 0, j * P:(j + 1) * P],
                                   smid_s[0:n, c, 1, j * P:(j + 1) * P], swd_s[0:n, c, 0, :], swd_s[0:n, c, 1, :], c == 0, c == 2)
                    if j % 2 == 1:
                        last.then_inc(dn_done, 1)

            for q in range(2):
                pe.wait_ge(xt_saved[q], 16)
            pe.wait_ge(sw_lo, 2)
            pe.wait_ge(sq_done, 2 * TILES)
            shared(0, 0, GAP_PAIR[0])
            pe.wait_ge(acc_done_t, TILES)
            for b in range(BATCH):
                last = nc.tensor.matmul(bank[2 + b][0:1, 0:D + ROT], one_col[:, :], acc[:, b, :], start=True, stop=True)
            last.then_inc(red_done, 1)

            pe.wait_ge(mask_done, 1)
            pe.wait_ge(const_done, 5)
            pe.wait_ge(sq_done, 2 * TILES)
            nc.tensor.matmul(bank[7][:, 0:TILES * E], tri16[:, :], mask16[:, :, :].rearrange("p t e -> p (t e)"), start=True, stop=False)
            for t in range(TILES - 1):
                n = TILES - 1 - t
                last = nc.tensor.matmul(bank[7][:, (t + 1) * E:TILES * E].rearrange("p (t e) -> p t e", e=E), one16[:, :],
                                        mask16[:, t:t + 1, :].to_broadcast([P, n, E]), start=False, stop=t == TILES - 2)
            last.then_inc(rank_done, 1)
            pe.wait_ge(arow_done, 3)
            for b in range(BATCH):
                for c in range(DC):
                    last = nc.tensor.matmul(bank[2][:, 384 + b * DC + c:385 + b * DC + c], arow[0:1, b, c * P:(c + 1) * P], ones3[0:1, 0:1],
                                            start=True, stop=True)
            last.then_inc(acol_done, 1)
            pe.wait_ge(lo_done, TILES)
            shared(0, 1, GAP_PAIR[1])
            pe.wait_ge(onehot_done, 2)
            pe.wait_ge(oa_done, 1)
            for t in range(TILES):
                last = nc.tensor.matmul(bank[6][:, 0:E * SLOT_B], oat[:, t, :, :].rearrange("p a e -> p (a e)"),
                                        ob[:, t, :, :].rearrange("p b e -> p (b e)"), start=t == 0, stop=t == TILES - 1)
            last.then_inc(table_done, 1)
            pe.wait_ge(sm_done, 1)
            shared(0, 2, GAP_PAIR[2])
            pe.wait_ge(spread_done, 1)
            nc.tensor.matmul(bank[6][:, 256:256 + E], spread[:, :, :].rearrange("p a b -> p (a b)"), exp16[:, :],
                             start=True, stop=True).then_inc(slot_done, 1)

            pe.wait_ge(aw_done, 1 + BATCH * DC)
            pe.wait_ge(mix_in, 32)
            for b in range(BATCH):
                for c in range(DC):
                    if b * DC + c == 2:
                        pe.wait_ge(sm_done, 2)
                    for k in range(DC):
                        last = nc.tensor.matmul(bank[2 + b * DC + c][:, 0:D], wqt[:, k, c * P:(c + 1) * P], aw[:, b, k, :], start=k == 0, stop=k == DC - 1)
                    last.then_inc(m_done, 1)
            pe.wait_ge(onehot_done, 1)
            for b in range(BATCH):
                for k in range(DC):
                    nc.tensor.matmul(bank[7][0:3, b * D:(b + 1) * D], bq3[:, k, :], aw[:, b, k, :], start=k == 0, stop=False)
                last = nc.tensor.matmul(bank[7][0:3, b * D:(b + 1) * D], ones3[:, 0:3], bout_row[:, :], start=False, stop=True)
            last.then_inc(c_done, 1)
            pe.wait_ge(sw_lo, 4)
            pe.wait_ge(sm_done, 3)
            shared_down(0, 0)

            def turn_rows_e(e, j, h):
                pe.wait_ge(gath[j], 16 * (h + 1))
                if not (isinstance(e, int) and e < 2):
                    pe.wait_ge(xgt_done, e - 1)
                for c in range(DC):
                    last = nc.tensor.transpose(bank[4 + j % 2][:, c * P:(c + 1) * P], xg[:, j, c * P:(c + 1) * P], ident)
                last.then_inc(xt_e, 1)

            def gate_up(e, j, h):
                k = j % 2
                pe.wait_ge(ew_in[j], 48 * (h + 1))
                if not (isinstance(e, int) and e < 2):
                    pe.wait_ge(mid_done, 2 * (e - 1))
                pe.wait_ge(xgt_done, e + 1)
                for q, (lo_, n) in enumerate(((0, P), (P, P), (2 * P, UP2 + I2))):
                    for c in range(DC):
                        last = nc.tensor.matmul(bank[k][0:n, q * P:(q + 1) * P], wgu[:, j, c, lo_:lo_ + n], xgt[:, k, c, :],
                                                start=c == 0, stop=c == DC - 1)
                last.then_inc(gu_done, 1)

            def down(e, j, first):
                k = j % 2
                pe.wait_ge(mid_done, 2 * e + 2)
                if not first:
                    pe.wait_ge(eo_done, e - 1)
                nc.tensor.matmul(bank[2 + k][:, 0:D], mid[:, k, 0, :], wdn[:, j, 0, :], start=True, stop=False)
                nc.tensor.matmul(bank[2 + k][:, 0:D], mid[0:I2, k, 1, :], wdn[0:I2, j, 1, :], start=False, stop=True).then_inc(d_done, 1)

            def moe_body(h, first=False, last=False):
                for j in range(G):
                    e = h * G + j
                    if not (last and j == G - 1):
                        turn_rows_e(e + 1, (j + 1) % G, h + (j + 1) // G)
                    gate_up(e, j, h)
                    if not (first and j == 0):
                        down(e - 1, (j - 1) % G, first and j <= 2)
                    if first and j == 1:
                        pe.wait_ge(idx_done, 1)
                        pe.wait_ge(c3_done, 1)
                    if last and j == 0:
                        pe.wait_ge(kept, 2 * GROUPS - 2)
                    for t in MIX_FIRST[j] if first else MIX_LAST[j] if last else ():
                        mixed(t)
                    if not first and not last:
                        if j < 3:
                            shared(h, j, 6)
                        else:
                            shared_down(h, 6)

            def mixed(t):
                b, dst = t // TILES_B, bank[MIX_BANK[t]][:, 0:D]
                if 2 <= t < 8:
                    pe.wait_ge(half_done, t - 1)
                if t >= 14:
                    pe.wait_ge(half_done, t - 5)
                for d in range(DC):
                    mm3(dst, xt_all[:, t, 0, d, :], xt_all[:, t, 1, d, :], m_s[:, b, d, 0, :], m_s[:, b, d, 1, :], d == 0, False)
                nc.tensor.matmul(dst, ib_all[:, t, :], c3[:, b, :], start=False, stop=True).then_inc(att_done, 1)

            for q in range(2):
                pe.wait_ge(xt_saved[q], 16 * TILES // 4)
            pe.wait_ge(m_lo, BATCH * DC)
            turn_rows_e(0, 0, 0)
            pe.wait_ge(kept, 2)
            moe_body(0, first=True)
            pe.wait_ge(half_done, G)
            with pe.Fori(1, E // G - 1) as h:
                moe_body(h)
            moe_body(E // G - 1, last=True)
            down(E - 1, G - 1, False)

            pe.wait_ge(half_done, 8)
            pe.wait_ge(mid_done, 2 * E)
            for c in range(3):
                shared(GROUPS - 1, c, 6)
                for t in MIX_CHUNK[c]:
                    if MIX_BANK[t] == 2:
                        pe.wait_ge(eo_done, E)
                    mixed(t)
            shared_down(GROUPS - 1, 6)


def kernel(L0_attn_X, L0_attn_W_in, L0_attn_b_in, L0_attn_W_out, L0_attn_b_out, L0_attn_gamma, L0_attn_beta,
           L0_ffn_gate_w, L0_ffn_w_gate, L0_ffn_w_up, L0_ffn_w_down, L0_ffn_sw_gate, L0_ffn_sw_up, L0_ffn_sw_down):
    import numpy as np
    import concourse.bacc as bacc
    from concourse.bass_utils import run_bass_kernel_spmd as run

    order = np.concatenate([np.arange(0, ROT, 2), np.arange(1, ROT, 2), np.arange(ROT, D)])
    w_in, b_in = np.asarray(L0_attn_W_in), np.asarray(L0_attn_b_in)
    cols = np.concatenate([order + k * D for k in range(3)])
    w_gate, w_up = np.asarray(L0_ffn_w_gate), np.asarray(L0_ffn_w_up)
    gap = np.zeros((E, D, UP2 - I2), np.float32)
    w_gu = np.concatenate([w_gate[:, :, :P], w_up[:, :, :P], w_gate[:, :, P:], gap, w_up[:, :, P:]], axis=2)

    seq = TOKENS // BATCH
    inv = (1.0 / np.float32(10000.0) ** (np.arange(0, ROT, 2, dtype=np.float32) / np.float32(ROT))).astype(np.float32)
    angle = (np.arange(seq, dtype=np.float32)[:, None] * inv[None, :]).astype(np.float64)
    cos, sin = np.cos(2 * angle) / 4, np.sin(2 * angle) / 4
    trig = np.concatenate([cos, -cos, -sin, -sin], axis=1).astype(np.float32)

    p = np.arange(P)
    consts = np.zeros((P, C_ALL), np.float32)
    consts[:, C_ID:C_ID + P] = np.eye(P)
    consts[:, C_TRI:C_TRI + P] = p[:, None] < p[None, :]
    consts[:, C_EXP:C_EXP + E] = (p[:, None] % E) == np.arange(E)[None, :]
    consts[:, C_ASEL:C_ASEL + SLOT_A] = (p[:, None] // E) == np.arange(SLOT_A)[None, :]
    consts[:, C_I16:C_I16 + E] = np.arange(E)[None, :]
    consts[:, C_TOK:C_TOK + TILES] = P * np.arange(TILES)[None, :] + p[:, None] + 1
    consts[:, C_SPARE] = TOKENS + 1 + p
    consts[0:3, C_ROW] = (0, 1, 0)
    consts[0:3, C_ROW + 1] = (1, -1, 1)

    ins = {
        "x": L0_attn_X, "w_in": np.concatenate([w_in[:, cols], np.asarray(L0_ffn_gate_w).T], axis=1),
        "bias": np.concatenate([b_in[cols], np.asarray(L0_attn_b_out)])[None, :], "wq_t": w_in[:, order].T,
        "w_out": np.asarray(L0_attn_W_out)[order, :],
        "gb": np.concatenate([np.asarray(a).reshape(DC, P).T for a in (L0_attn_gamma, L0_attn_beta)], axis=1),
        "w_gu": w_gu, "w_dn": L0_ffn_w_down,
        "sw_g": L0_ffn_sw_gate, "sw_u": L0_ffn_sw_up, "sw_d": L0_ffn_sw_down, "trig": trig, "consts": consts,
    }
    nc = bacc.Bacc("TRN2", target_bir_lowering=False, num_devices=1)
    arrays, args = {}, []
    for name, a in ins.items():
        a = np.ascontiguousarray(a)
        arrays[f"in_{name}"] = a
        args.append(nc.dram_tensor(f"in_{name}", a.shape, mybir.dt.from_np(a.dtype), kind="ExternalInput").ap())
    args.append(nc.dram_tensor("out", (BATCH, TOKENS // BATCH, D), F32, kind="ExternalOutput").ap())
    layer(nc, *args)
    r = run(nc, [arrays], core_ids=[0])
    return r.results[0]["out"]
```
